# Optimizing a Trainium2 kernel written in Bass

```python
import numpy as np
import jax
import jax.numpy as jnp

def _softmax(x, axis=-1):
    return jax.nn.softmax(x, axis=axis)

def _gelu(x):
    return jax.nn.gelu(x, approximate=True)

def _silu(x):
    return jax.nn.silu(x)

def _sigmoid(x):
    return jax.nn.sigmoid(x)

def _layernorm(x, axis=-1, eps=1e-05):
    m = jnp.mean(x, axis=axis, keepdims=True)
    v = jnp.var(x, axis=axis, keepdims=True)
    return (x - m) / jnp.sqrt(v + eps)

def _scatter_add(tgt, idx, src, axis=0):
    return tgt.at[idx].add(src)

def _segment_sum(src, seg, n):
    return jax.ops.segment_sum(src, seg, n)
kernel_name = 'mk_recurrent_d4_jaxref_r8_b3275f'

def setup_inputs(seed: int=0):
    np.random.seed(seed)
    _w = jnp.asarray

    def _L0_attn_setup():
        import jax, jax.numpy as jnp
        import numpy as np
        B, S, D_MODEL = (4, 256, 128)
        NUM_HEADS, HEAD_DIM = (16, 64)
        EPS = 1e-06
        key = jax.random.key(seed)
        ks = jax.random.split(key, 6)
        hd = NUM_HEADS * HEAD_DIM
        scale_in = 1.0 / np.sqrt(D_MODEL)
        scale_hd = 1.0 / np.sqrt(hd)
        return {'x': jax.random.normal(ks[0], (B, S, D_MODEL), dtype=jnp.float32), 'w_q': jax.random.normal(ks[1], (D_MODEL, hd), dtype=jnp.float32) * scale_in, 'w_k': jax.random.normal(ks[2], (D_MODEL, hd), dtype=jnp.float32) * scale_in, 'w_v': jax.random.normal(ks[3], (D_MODEL, hd), dtype=jnp.float32) * scale_in, 'w_proj': jax.random.normal(ks[4], (hd, D_MODEL), dtype=jnp.float32) * scale_hd, 'b_proj': jax.random.normal(ks[5], (D_MODEL,), dtype=jnp.float32) * 0.01, 'ln_gamma': jnp.ones((D_MODEL,), dtype=jnp.float32), 'ln_beta': jnp.zeros((D_MODEL,), dtype=jnp.float32)}
    _L0_attn_in = _L0_attn_setup()

    def _L0_ffn_setup():
        import jax, jax.numpy as jnp
        import numpy as np
        E = 32
        H = 128
        I = 64
        G = 8
        TKG = 4
        TOPK = 8
        NSH = 2
        SCALE = 2.5
        key = jax.random.key(seed)
        ks = jax.random.split(key, 10)
        s = 0.02
        return {'hidden_states': jax.random.normal(ks[0], (2, 128, H), jnp.float32), 'gate_w': jax.random.normal(ks[1], (E, H), jnp.float32) * s, 'gate_bias': jax.random.normal(ks[2], (E,), jnp.float32) * s, 'w_gate': jax.random.normal(ks[3], (E, I, H), jnp.float32) * s, 'w_up': jax.random.normal(ks[4], (E, I, H), jnp.float32) * s, 'w_down': jax.random.normal(ks[5], (E, H, I), jnp.float32) * s, 'sh_gate': jax.random.normal(ks[6], (I * NSH, H), jnp.float32) * s, 'sh_up': jax.random.normal(ks[7], (I * NSH, H), jnp.float32) * s, 'sh_down': jax.random.normal(ks[8], (H, I * NSH), jnp.float32) * s}
    _L0_ffn_in = _L0_ffn_setup()

    def _L1_attn_setup():
        import jax, jax.numpy as jnp
        import numpy as np
        from math import sqrt
        EMBED = 128
        HEADS = 16
        key = jax.random.key(seed)
        k1, k2, k3, k4, k5 = jax.random.split(key, 5)
        x = jax.random.normal(k1, (2, 256, EMBED), dtype=jnp.float32)
        s = 1.0 / sqrt(EMBED)
        W_qkv = jax.random.normal(k2, (EMBED, 3 * EMBED), dtype=jnp.float32) * s
        b_qkv = jax.random.normal(k3, (3 * EMBED,), dtype=jnp.float32) * 0.01
        W_out = jax.random.normal(k4, (EMBED, EMBED), dtype=jnp.float32) * s
        b_out = jax.random.normal(k5, (EMBED,), dtype=jnp.float32) * 0.01
        return {'x': x, 'W_qkv': W_qkv, 'b_qkv': b_qkv, 'W_out': W_out, 'b_out': b_out}
    _L1_attn_in = _L1_attn_setup()

    def _L1_ffn_setup():
        import jax, jax.numpy as jnp
        import numpy as np
        B, S, D = (2, 256, 128)
        E, K, DFF = (8, 2, 4 * 128)
        EPS_GATE = 1e-08
        EPS_LN = 1e-05
        key = jax.random.key(seed)
        ks = jax.random.split(key, 4)
        scaled = lambda k, shape, fan: jax.random.normal(k, shape, jnp.float32) / np.sqrt(fan).astype(np.float32)
        return {'x': jax.random.normal(ks[0], (B, S, D), jnp.float32), 'Wg': scaled(ks[1], (D, E), D), 'bg': jnp.zeros((E,), jnp.float32), 'W1': scaled(ks[2], (E, D, DFF), D), 'b1': jnp.zeros((E, DFF), jnp.float32), 'W2': scaled(ks[3], (E, DFF, D), DFF), 'b2': jnp.zeros((E, D), jnp.float32), 'gamma': jnp.ones((D,), jnp.float32), 'beta': jnp.zeros((D,), jnp.float32)}
    _L1_ffn_in = _L1_ffn_setup()

    def _L2_attn_setup():
        import jax, jax.numpy as jnp
        import numpy as np
        B, L, DM = (4, 512, 128)
        key = jax.random.key(seed)
        ks = jax.random.split(key, 8)
        return {'u': jax.random.normal(ks[0], (B, L, DM), dtype=jnp.float32), 'A_real': 0.05 * jax.random.normal(ks[1], (DM,), dtype=jnp.float32), 'A_imag': 0.05 * jax.random.normal(ks[2], (DM,), dtype=jnp.float32), 'B_real': 0.05 * jax.random.normal(ks[3], (DM,), dtype=jnp.float32), 'B_imag': 0.05 * jax.random.normal(ks[4], (DM,), dtype=jnp.float32), 'C_real': 0.05 * jax.random.normal(ks[5], (DM,), dtype=jnp.float32), 'C_imag': 0.05 * jax.random.normal(ks[6], (DM,), dtype=jnp.float32), 'D': jnp.zeros((DM,), dtype=jnp.float32)}
    _L2_attn_in = _L2_attn_setup()

    def _L2_ffn_setup():
        import jax, jax.numpy as jnp
        import numpy as np
        B, T, D, F_FF, E, TOP_K = (8, 256, 128, 512, 8, 2)
        CAP_FACTOR = 1.25
        key = jax.random.key(seed)
        ks = jax.random.split(key, 7)
        s = 0.02
        return {'x': jax.random.normal(ks[0], (B, T, D), dtype=jnp.float32), 'w_router': jax.random.normal(ks[1], (D, E), dtype=jnp.float32) * s, 'b_router': jnp.zeros((E,), dtype=jnp.float32), 'w1': jax.random.normal(ks[2], (E, D, F_FF), dtype=jnp.float32) * s, 'b1': jnp.zeros((E, F_FF), dtype=jnp.float32), 'w2': jax.random.normal(ks[3], (E, F_FF, D), dtype=jnp.float32) * s, 'b2': jnp.zeros((E, D), dtype=jnp.float32)}
    _L2_ffn_in = _L2_ffn_setup()

    def _L3_attn_setup():
        import jax, jax.numpy as jnp
        import numpy as np
        import math
        CHUNK = 128
        key = jax.random.key(seed)
        ks = jax.random.split(key, 12)
        B, S, H, D = (2, 512, 128, 256)
        std = 0.02
        inp = {'hidden_states': jax.random.normal(ks[0], (B, S, H), jnp.float32), 'Wq': jax.random.normal(ks[1], (H, D), jnp.float32) * std, 'bq': jnp.zeros((D,), jnp.float32), 'Wk': jax.random.normal(ks[2], (H, D), jnp.float32) * std, 'bk': jnp.zeros((D,), jnp.float32), 'Wv': jax.random.normal(ks[3], (H, D), jnp.float32) * std, 'bv': jnp.zeros((D,), jnp.float32), 'Wg': jax.random.normal(ks[4], (H, D), jnp.float32) * std, 'bg': jnp.zeros((D,), jnp.float32), 'Wo': jax.random.normal(ks[5], (D, H), jnp.float32) * std, 'bo': jnp.zeros((H,), jnp.float32)}
        return inp
    _L3_attn_in = _L3_attn_setup()

    def _L3_ffn_setup():
        import jax, jax.numpy as jnp
        import numpy as np
        EPS = 1e-05

        def _ln(x, g, b):
            mu = jnp.mean(x, axis=-1, keepdims=True)
            var = jnp.mean(jnp.square(x - mu), axis=-1, keepdims=True)
            return (x - mu) * jax.lax.rsqrt(var + EPS) * g + b

        def _forward(x, index_b, index_t, sw1, sb1, sw2, sb2, sw3, sb3, s_ln_g, s_ln_b, sg_w, sg_b, eg_w, eg_b, exp_bias, ew1, eb1, ew2, eb2, ew3, eb3, sel_ln_g, sel_ln_b):
            x1 = jnp.einsum('btd,hd->bth', x, sw1) + sb1
            x2 = jnp.einsum('btd,hd->bth', x, sw2) + sb2
            sh = _ln(jax.nn.silu(x1) * x2, s_ln_g, s_ln_b)
            shared_out = jnp.einsum('bth,dh->btd', sh, sw3) + sb3
            x_moe = x[index_b, index_t]
            shared_scores = jax.nn.sigmoid(x_moe @ sg_w.T + sg_b)
            expert_scores = jax.nn.sigmoid(x_moe @ eg_w.T + eg_b)
            top1_idx = jnp.argmax(expert_scores + exp_bias, axis=-1)
            top1_score = jnp.take_along_axis(expert_scores, top1_idx[:, None], axis=-1)
            weights = jax.nn.softmax(jnp.concatenate([shared_scores, top1_score], axis=-1), axis=-1)
            shared_w, expert_w = (weights[:, 0], weights[:, 1])
            shared_moe_out = shared_out[index_b, index_t] * shared_w[:, None]
            h1 = jnp.einsum('md,ehd->meh', x_moe, ew1) + eb1
            h2 = jnp.einsum('md,ehd->meh', x_moe, ew2) + eb2
            z = _ln(jax.nn.silu(h1) * h2, sel_ln_g, sel_ln_b)
            out_all = jnp.einsum('meh,edh->med', z, ew3) + eb3
            expert_out = jnp.take_along_axis(out_all, top1_idx[:, None, None], axis=1)[:, 0]
            expert_moe_out = expert_out * expert_w[:, None]
            final_out = shared_out.at[index_b, index_t].set(shared_moe_out + expert_moe_out)
            return final_out
        B, T, D, E, H, M = (2, 256, 128, 8, 64, 256)
        key = jax.random.key(seed)
        ks = jax.random.split(key, 24)
        s = 0.02
        inp = {}
        inp['x'] = jax.random.normal(ks[0], (B, T, D), jnp.float32)
        flat = jnp.arange(M, dtype=jnp.int32) * 2
        inp['index_b'] = flat // T
        inp['index_t'] = flat % T
        inp['sw1'] = jax.random.normal(ks[1], (H, D), jnp.float32) * s
        inp['sb1'] = jnp.zeros((H,), jnp.float32)
        inp['sw2'] = jax.random.normal(ks[2], (H, D), jnp.float32) * s
        inp['sb2'] = jnp.zeros((H,), jnp.float32)
        inp['sw3'] = jax.random.normal(ks[3], (D, H), jnp.float32) * s
        inp['sb3'] = jnp.zeros((D,), jnp.float32)
        inp['s_ln_g'] = jnp.ones((H,), jnp.float32)
        inp['s_ln_b'] = jnp.zeros((H,), jnp.float32)
        inp['sg_w'] = jax.random.normal(ks[4], (1, D), jnp.float32) * s
        inp['sg_b'] = jnp.zeros((1,), jnp.float32)
        inp['eg_w'] = jax.random.normal(ks[5], (E, D), jnp.float32) * s
        inp['eg_b'] = jnp.zeros((E,), jnp.float32)
        inp['exp_bias'] = jnp.zeros((E,), jnp.float32)
        inp['ew1'] = jax.random.normal(ks[6], (E, H, D), jnp.float32) * s
        inp['eb1'] = jnp.zeros((E, H), jnp.float32)
        inp['ew2'] = jax.random.normal(ks[7], (E, H, D), jnp.float32) * s
        inp['eb2'] = jnp.zeros((E, H), jnp.float32)
        inp['ew3'] = jax.random.normal(ks[8], (E, D, H), jnp.float32) * s
        inp['eb3'] = jnp.zeros((E, D), jnp.float32)
        inp['sel_ln_g'] = jnp.ones((H,), jnp.float32)
        inp['sel_ln_b'] = jnp.zeros((H,), jnp.float32)
        return inp
    _L3_ffn_in = _L3_ffn_setup()
    _d = {'L0_attn_x': _L0_attn_in['x'], 'L0_attn_w_q': _L0_attn_in['w_q'], 'L0_attn_w_k': _L0_attn_in['w_k'], 'L0_attn_w_v': _L0_attn_in['w_v'], 'L0_attn_w_proj': _L0_attn_in['w_proj'], 'L0_attn_b_proj': _L0_attn_in['b_proj'], 'L0_attn_ln_gamma': _L0_attn_in['ln_gamma'], 'L0_attn_ln_beta': _L0_attn_in['ln_beta'], 'L0_ffn_gate_w': _L0_ffn_in['gate_w'], 'L0_ffn_gate_bias': _L0_ffn_in['gate_bias'], 'L0_ffn_w_gate': _L0_ffn_in['w_gate'], 'L0_ffn_w_up': _L0_ffn_in['w_up'], 'L0_ffn_w_down': _L0_ffn_in['w_down'], 'L0_ffn_sh_gate': _L0_ffn_in['sh_gate'], 'L0_ffn_sh_up': _L0_ffn_in['sh_up'], 'L0_ffn_sh_down': _L0_ffn_in['sh_down'], 'L1_attn_W_qkv': _L1_attn_in['W_qkv'], 'L1_attn_b_qkv': _L1_attn_in['b_qkv'], 'L1_attn_W_out': _L1_attn_in['W_out'], 'L1_attn_b_out': _L1_attn_in['b_out'], 'L1_ffn_Wg': _L1_ffn_in['Wg'], 'L1_ffn_bg': _L1_ffn_in['bg'], 'L1_ffn_W1': _L1_ffn_in['W1'], 'L1_ffn_b1': _L1_ffn_in['b1'], 'L1_ffn_W2': _L1_ffn_in['W2'], 'L1_ffn_b2': _L1_ffn_in['b2'], 'L1_ffn_gamma': _L1_ffn_in['gamma'], 'L1_ffn_beta': _L1_ffn_in['beta'], 'L2_attn_A_real': _L2_attn_in['A_real'], 'L2_attn_A_imag': _L2_attn_in['A_imag'], 'L2_attn_B_real': _L2_attn_in['B_real'], 'L2_attn_B_imag': _L2_attn_in['B_imag'], 'L2_attn_C_real': _L2_attn_in['C_real'], 'L2_attn_C_imag': _L2_attn_in['C_imag'], 'L2_attn_D': _L2_attn_in['D'], 'L2_ffn_w_router': _L2_ffn_in['w_router'], 'L2_ffn_b_router': _L2_ffn_in['b_router'], 'L2_ffn_w1': _L2_ffn_in['w1'], 'L2_ffn_b1': _L2_ffn_in['b1'], 'L2_ffn_w2': _L2_ffn_in['w2'], 'L2_ffn_b2': _L2_ffn_in['b2'], 'L3_attn_Wq': _L3_attn_in['Wq'], 'L3_attn_bq': _L3_attn_in['bq'], 'L3_attn_Wk': _L3_attn_in['Wk'], 'L3_attn_bk': _L3_attn_in['bk'], 'L3_attn_Wv': _L3_attn_in['Wv'], 'L3_attn_bv': _L3_attn_in['bv'], 'L3_attn_Wg': _L3_attn_in['Wg'], 'L3_attn_bg': _L3_attn_in['bg'], 'L3_attn_Wo': _L3_attn_in['Wo'], 'L3_attn_bo': _L3_attn_in['bo'], 'L3_ffn_index_b': _L3_ffn_in['index_b'], 'L3_ffn_index_t': _L3_ffn_in['index_t'], 'L3_ffn_sw1': _L3_ffn_in['sw1'], 'L3_ffn_sb1': _L3_ffn_in['sb1'], 'L3_ffn_sw2': _L3_ffn_in['sw2'], 'L3_ffn_sb2': _L3_ffn_in['sb2'], 'L3_ffn_sw3': _L3_ffn_in['sw3'], 'L3_ffn_sb3': _L3_ffn_in['sb3'], 'L3_ffn_s_ln_g': _L3_ffn_in['s_ln_g'], 'L3_ffn_s_ln_b': _L3_ffn_in['s_ln_b'], 'L3_ffn_sg_w': _L3_ffn_in['sg_w'], 'L3_ffn_sg_b': _L3_ffn_in['sg_b'], 'L3_ffn_eg_w': _L3_ffn_in['eg_w'], 'L3_ffn_eg_b': _L3_ffn_in['eg_b'], 'L3_ffn_exp_bias': _L3_ffn_in['exp_bias'], 'L3_ffn_ew1': _L3_ffn_in['ew1'], 'L3_ffn_eb1': _L3_ffn_in['eb1'], 'L3_ffn_ew2': _L3_ffn_in['ew2'], 'L3_ffn_eb2': _L3_ffn_in['eb2'], 'L3_ffn_ew3': _L3_ffn_in['ew3'], 'L3_ffn_eb3': _L3_ffn_in['eb3'], 'L3_ffn_sel_ln_g': _L3_ffn_in['sel_ln_g'], 'L3_ffn_sel_ln_b': _L3_ffn_in['sel_ln_b']}
    _x0 = _d['L0_attn_x']
    _d['L0_attn_x'] = jax.random.normal(jax.random.fold_in(jax.random.key(seed), 1), (4, 1024, 128), dtype=_x0.dtype)
    del _x0
    return _d

def reference(L0_attn_x, L0_attn_w_q, L0_attn_w_k, L0_attn_w_v, L0_attn_w_proj, L0_attn_b_proj, L0_attn_ln_gamma, L0_attn_ln_beta, L0_ffn_gate_w, L0_ffn_gate_bias, L0_ffn_w_gate, L0_ffn_w_up, L0_ffn_w_down, L0_ffn_sh_gate, L0_ffn_sh_up, L0_ffn_sh_down, L1_attn_W_qkv, L1_attn_b_qkv, L1_attn_W_out, L1_attn_b_out, L1_ffn_Wg, L1_ffn_bg, L1_ffn_W1, L1_ffn_b1, L1_ffn_W2, L1_ffn_b2, L1_ffn_gamma, L1_ffn_beta, L2_attn_A_real, L2_attn_A_imag, L2_attn_B_real, L2_attn_B_imag, L2_attn_C_real, L2_attn_C_imag, L2_attn_D, L2_ffn_w_router, L2_ffn_b_router, L2_ffn_w1, L2_ffn_b1, L2_ffn_w2, L2_ffn_b2, L3_attn_Wq, L3_attn_bq, L3_attn_Wk, L3_attn_bk, L3_attn_Wv, L3_attn_bv, L3_attn_Wg, L3_attn_bg, L3_attn_Wo, L3_attn_bo, L3_ffn_index_b, L3_ffn_index_t, L3_ffn_sw1, L3_ffn_sb1, L3_ffn_sw2, L3_ffn_sb2, L3_ffn_sw3, L3_ffn_sb3, L3_ffn_s_ln_g, L3_ffn_s_ln_b, L3_ffn_sg_w, L3_ffn_sg_b, L3_ffn_eg_w, L3_ffn_eg_b, L3_ffn_exp_bias, L3_ffn_ew1, L3_ffn_eb1, L3_ffn_ew2, L3_ffn_eb2, L3_ffn_ew3, L3_ffn_eb3, L3_ffn_sel_ln_g, L3_ffn_sel_ln_b):

    def _L0_attn_ref(x, w_q, w_k, w_v, w_proj, b_proj, ln_gamma, ln_beta):
        import jax, jax.numpy as jnp
        import numpy as np
        B, S, D_MODEL = (4, 256, 128)
        NUM_HEADS, HEAD_DIM = (16, 64)
        EPS = 1e-06

        def split_heads(t):
            b, s, _ = t.shape
            return t.reshape(b, s, NUM_HEADS, HEAD_DIM).transpose(0, 2, 1, 3)
        q = split_heads(x @ w_q)
        k = split_heads(x @ w_k)
        v = split_heads(x @ w_v)
        scale = HEAD_DIM ** (-0.5)
        attn = jnp.einsum('bnqd,bnkd->bnqk', q, k) * scale
        attn = jax.nn.softmax(attn, axis=-1)
        o = jnp.einsum('bnqk,bnkd->bnqd', attn, v)
        o = o.transpose(0, 2, 1, 3).reshape(x.shape[0], x.shape[1], NUM_HEADS * HEAD_DIM)
        y = o @ w_proj + b_proj + x
        mean = jnp.mean(y, axis=-1, keepdims=True)
        var = jnp.var(y, axis=-1, keepdims=True)
        y = (y - mean) * jax.lax.rsqrt(var + EPS) * ln_gamma + ln_beta
        return y

    def _L0_ffn_ref(hidden_states, gate_w, gate_bias, w_gate, w_up, w_down, sh_gate, sh_up, sh_down):
        import jax, jax.numpy as jnp
        import numpy as np
        E = 32
        H = 128
        I = 64
        G = 8
        TKG = 4
        TOPK = 8
        NSH = 2
        SCALE = 2.5
        B, S, Hd = hidden_states.shape
        h = hidden_states.reshape(-1, Hd)
        logits = h.astype(jnp.float32) @ gate_w.T
        scores = jax.nn.sigmoid(logits)
        sc = scores + gate_bias
        grp = sc.reshape(-1, G, E // G)
        group_scores = jax.lax.top_k(grp, 2)[0].sum(-1)
        gidx = jax.lax.top_k(group_scores, TKG)[1]
        gmask = jnp.sum(jax.nn.one_hot(gidx, G, dtype=sc.dtype), axis=1)
        smask = jnp.repeat(gmask, E // G, axis=1)
        masked = jnp.where(smask > 0, sc, jnp.zeros_like(sc))
        tki = jax.lax.top_k(masked, TOPK)[1]
        tkw = jnp.take_along_axis(scores, tki, axis=1)
        tkw = tkw / (tkw.sum(-1, keepdims=True) + 1e-20)
        tkw = tkw * SCALE
        combine = (jax.nn.one_hot(tki, E, dtype=tkw.dtype) * tkw[..., None]).sum(1)
        g = jax.nn.silu(jnp.einsum('th,eih->tei', h, w_gate))
        u = jnp.einsum('th,eih->tei', h, w_up)
        routed = jnp.einsum('tei,ehi->th', g * u * combine[:, :, None], w_down)
        sg = jax.nn.silu(h @ sh_gate.T)
        shared = sg * (h @ sh_up.T) @ sh_down.T
        return (routed + shared).reshape(B, S, Hd)

    def _L1_attn_ref(x, W_qkv, b_qkv, W_out, b_out):
        import jax, jax.numpy as jnp
        import numpy as np
        from math import sqrt
        EMBED = 128
        HEADS = 16
        B, N, E = x.shape
        H = HEADS
        d = E // H
        qkv = x @ W_qkv + b_qkv
        q, k, v = jnp.split(qkv, 3, axis=2)
        q = q.reshape(B, N, H, d)
        k = k.reshape(B, N, H, d)
        v = v.reshape(B, N, H, d)
        energy = jnp.einsum('bqhe,bkhe->bqhk', q, k)
        attn = jax.nn.softmax(energy, axis=-1) / sqrt(E)
        out = jnp.einsum('bihv,bvhd->bihd', attn, v)
        out = out.reshape(B, N, E)
        return out @ W_out + b_out

    def _L1_ffn_ref(x, Wg, bg, W1, b1, W2, b2, gamma, beta):
        import jax, jax.numpy as jnp
        import numpy as np
        B, S, D = (2, 256, 128)
        E, K, DFF = (8, 2, 4 * 128)
        EPS_GATE = 1e-08
        EPS_LN = 1e-05
        b, s, d = x.shape
        xf = x.reshape(-1, d)
        T = xf.shape[0]
        num_experts = Wg.shape[1]
        logits = xf @ Wg + bg
        w = jax.nn.softmax(logits, axis=-1)
        top_w, top_idx = jax.lax.top_k(w, K)
        top_w = top_w / (top_w.sum(axis=-1, keepdims=True) + EPS_GATE)
        cw = jnp.zeros((T, num_experts), xf.dtype).at[jnp.arange(T)[:, None], top_idx].add(top_w)
        out = jnp.zeros_like(xf)
        for e in range(num_experts):
            h = jax.nn.gelu(xf @ W1[e] + b1[e], approximate=False)
            y = h @ W2[e] + b2[e]
            out = out + cw[:, e:e + 1] * y
        mu = out.mean(axis=-1, keepdims=True)
        var = out.var(axis=-1, keepdims=True)
        out = (out - mu) / jnp.sqrt(var + EPS_LN) * gamma + beta
        return out.reshape(b, s, d)

    def _L2_attn_ref(u, A_real, A_imag, B_real, B_imag, C_real, C_imag, D):
        import jax, jax.numpy as jnp
        import numpy as np
        B, L, DM = (4, 512, 128)
        seq_len = u.shape[1]
        fft_len = int(2 ** np.ceil(np.log2(2 * seq_len - 1)))
        t = jnp.arange(seq_len, dtype=jnp.float32).astype(jnp.complex64)
        A_c = jax.lax.complex(A_real, A_imag)
        B_c = jax.lax.complex(B_real, B_imag)
        C_c = jax.lax.complex(C_real, C_imag)
        A_t = jnp.power(A_c[None, :], t[:, None])
        kernel = (C_c[None, :] * A_t * B_c[None, :]).T
        kernel_fft = jnp.fft.fft(kernel, n=fft_len, axis=-1)
        u_t = jnp.transpose(u, (0, 2, 1)).astype(jnp.complex64)
        U_f = jnp.fft.fft(u_t, n=fft_len, axis=-1)
        y_full = jnp.fft.ifft(U_f * kernel_fft[None], axis=-1)[..., :seq_len]
        y = jnp.transpose(jnp.real(y_full), (0, 2, 1))
        return y + D[None, None, :] * u

    def _L2_ffn_ref(x, w_router, b_router, w1, b1, w2, b2):
        import jax, jax.numpy as jnp
        import numpy as np
        B, T, D, F_FF, E, TOP_K = (8, 256, 128, 512, 8, 2)
        CAP_FACTOR = 1.25
        b, t, d = x.shape
        n = b * t
        e = w_router.shape[1]
        xf = x.reshape(n, d)
        logits = xf.astype(jnp.float32) @ w_router + b_router
        gates = jax.nn.softmax(logits, axis=-1)
        topv, topi = jax.lax.top_k(gates, TOP_K)
        cap = max(1, int(CAP_FACTOR * n / e))
        e_flat = topi.reshape(-1)
        g_flat = topv.reshape(-1)
        tok = jnp.repeat(jnp.arange(n), TOP_K)
        onehot = jax.nn.one_hot(e_flat, e, dtype=jnp.int32)
        pos = jnp.cumsum(onehot, axis=0)[jnp.arange(n * TOP_K), e_flat] - 1
        keep = pos < cap
        posc = jnp.minimum(pos, cap - 1)
        buf = jnp.zeros((e, cap, d), x.dtype).at[e_flat, posc].add(jnp.where(keep[:, None], xf[tok], 0.0))
        h = jax.nn.gelu(jnp.einsum('ecd,edf->ecf', buf, w1) + b1[:, None, :], approximate=False)
        out = jnp.einsum('ecf,efd->ecd', h, w2) + b2[:, None, :]
        og = out[e_flat, posc]
        w = jnp.where(keep, g_flat, 0.0).astype(x.dtype)
        y = jnp.zeros((n, d), x.dtype).at[tok].add(w[:, None] * og)
        ws = jnp.zeros((n,), x.dtype).at[tok].add(w)
        y = jnp.where((ws > 0.0)[:, None], y / jnp.maximum(ws, 1e-06)[:, None], y)
        return y.reshape(b, t, d)

    def _L3_attn_ref(hidden_states, Wq, bq, Wk, bk, Wv, bv, Wg, bg, Wo, bo):
        import jax, jax.numpy as jnp
        import numpy as np
        import math
        CHUNK = 128
        B, S, H = hidden_states.shape
        D = Wq.shape[1]
        cs = CHUNK
        nC = S // cs
        q = hidden_states @ Wq + bq
        k = hidden_states @ Wk + bk
        v = hidden_states @ Wv + bv
        gate = jax.nn.sigmoid(hidden_states @ Wg + bg)
        qc = q.reshape(B, nC, cs, D)
        kc = k.reshape(B, nC, cs, D)
        vc = v.reshape(B, nC, cs, D)
        gc = gate.reshape(B, nC, cs, D)
        scale = 1.0 / math.sqrt(D)
        attn = jnp.einsum('bncd,bnkd->bnck', qc, kc) * scale
        causal = jnp.tril(jnp.ones((cs, cs), bool))
        attn = jnp.where(causal, attn, -jnp.inf)
        attn = jax.nn.softmax(attn, axis=-1)
        local = jnp.einsum('bnck,bnkd->bncd', attn, vc)

        def step(state, xs):
            qi, ki, vi = xs
            cross = jnp.einsum('bcd,bde->bce', qi, state)
            state = state + jnp.einsum('bcd,bce->bde', ki, vi)
            return (state, cross)
        state0 = jnp.zeros((B, D, D), hidden_states.dtype)
        _, cross = jax.lax.scan(step, state0, (qc.transpose(1, 0, 2, 3), kc.transpose(1, 0, 2, 3), vc.transpose(1, 0, 2, 3)))
        cross = cross.transpose(1, 0, 2, 3)
        out = (local + cross) * gc
        out = out.reshape(B, S, D)
        return out @ Wo + bo

    def _L3_ffn_ref(x, index_b, index_t, sw1, sb1, sw2, sb2, sw3, sb3, s_ln_g, s_ln_b, sg_w, sg_b, eg_w, eg_b, exp_bias, ew1, eb1, ew2, eb2, ew3, eb3, sel_ln_g, sel_ln_b):
        import jax, jax.numpy as jnp
        import numpy as np
        EPS = 1e-05

        def _ln(x, g, b):
            mu = jnp.mean(x, axis=-1, keepdims=True)
            var = jnp.mean(jnp.square(x - mu), axis=-1, keepdims=True)
            return (x - mu) * jax.lax.rsqrt(var + EPS) * g + b

        def _forward(x, index_b, index_t, sw1, sb1, sw2, sb2, sw3, sb3, s_ln_g, s_ln_b, sg_w, sg_b, eg_w, eg_b, exp_bias, ew1, eb1, ew2, eb2, ew3, eb3, sel_ln_g, sel_ln_b):
            x1 = jnp.einsum('btd,hd->bth', x, sw1) + sb1
            x2 = jnp.einsum('btd,hd->bth', x, sw2) + sb2
            sh = _ln(jax.nn.silu(x1) * x2, s_ln_g, s_ln_b)
            shared_out = jnp.einsum('bth,dh->btd', sh, sw3) + sb3
            x_moe = x[index_b, index_t]
            shared_scores = jax.nn.sigmoid(x_moe @ sg_w.T + sg_b)
            expert_scores = jax.nn.sigmoid(x_moe @ eg_w.T + eg_b)
            top1_idx = jnp.argmax(expert_scores + exp_bias, axis=-1)
            top1_score = jnp.take_along_axis(expert_scores, top1_idx[:, None], axis=-1)
            weights = jax.nn.softmax(jnp.concatenate([shared_scores, top1_score], axis=-1), axis=-1)
            shared_w, expert_w = (weights[:, 0], weights[:, 1])
            shared_moe_out = shared_out[index_b, index_t] * shared_w[:, None]
            h1 = jnp.einsum('md,ehd->meh', x_moe, ew1) + eb1
            h2 = jnp.einsum('md,ehd->meh', x_moe, ew2) + eb2
            z = _ln(jax.nn.silu(h1) * h2, sel_ln_g, sel_ln_b)
            out_all = jnp.einsum('meh,edh->med', z, ew3) + eb3
            expert_out = jnp.take_along_axis(out_all, top1_idx[:, None, None], axis=1)[:, 0]
            expert_moe_out = expert_out * expert_w[:, None]
            final_out = shared_out.at[index_b, index_t].set(shared_moe_out + expert_moe_out)
            return final_out
        return _forward(x, index_b, index_t, sw1, sb1, sw2, sb2, sw3, sb3, s_ln_g, s_ln_b, sg_w, sg_b, eg_w, eg_b, exp_bias, ew1, eb1, ew2, eb2, ew3, eb3, sel_ln_g, sel_ln_b)
    x = L0_attn_x
    xn = _layernorm(x, axis=-1)
    s = _L0_attn_ref(xn, L0_attn_w_q, L0_attn_w_k, L0_attn_w_v, L0_attn_w_proj, L0_attn_b_proj, L0_attn_ln_gamma, L0_attn_ln_beta)
    g = _silu(_L0_ffn_ref(xn, L0_ffn_gate_w, L0_ffn_gate_bias, L0_ffn_w_gate, L0_ffn_w_up, L0_ffn_w_down, L0_ffn_sh_gate, L0_ffn_sh_up, L0_ffn_sh_down))
    x = x + s * g
    xn = _layernorm(x, axis=-1)
    s = _L1_attn_ref(xn, L1_attn_W_qkv, L1_attn_b_qkv, L1_attn_W_out, L1_attn_b_out)
    g = _silu(_L1_ffn_ref(xn, L1_ffn_Wg, L1_ffn_bg, L1_ffn_W1, L1_ffn_b1, L1_ffn_W2, L1_ffn_b2, L1_ffn_gamma, L1_ffn_beta))
    x = x + s * g
    xn = _layernorm(x, axis=-1)
    s = _L2_attn_ref(xn, L2_attn_A_real, L2_attn_A_imag, L2_attn_B_real, L2_attn_B_imag, L2_attn_C_real, L2_attn_C_imag, L2_attn_D)
    g = _silu(_L2_ffn_ref(xn, L2_ffn_w_router, L2_ffn_b_router, L2_ffn_w1, L2_ffn_b1, L2_ffn_w2, L2_ffn_b2))
    x = x + s * g
    xn = _layernorm(x, axis=-1)
    s = _L3_attn_ref(xn, L3_attn_Wq, L3_attn_bq, L3_attn_Wk, L3_attn_bk, L3_attn_Wv, L3_attn_bv, L3_attn_Wg, L3_attn_bg, L3_attn_Wo, L3_attn_bo)
    g = _silu(_L3_ffn_ref(xn, L3_ffn_index_b, L3_ffn_index_t, L3_ffn_sw1, L3_ffn_sb1, L3_ffn_sw2, L3_ffn_sb2, L3_ffn_sw3, L3_ffn_sb3, L3_ffn_s_ln_g, L3_ffn_s_ln_b, L3_ffn_sg_w, L3_ffn_sg_b, L3_ffn_eg_w, L3_ffn_eg_b, L3_ffn_exp_bias, L3_ffn_ew1, L3_ffn_eb1, L3_ffn_ew2, L3_ffn_eb2, L3_ffn_ew3, L3_ffn_eb3, L3_ffn_sel_ln_g, L3_ffn_sel_ln_b))
    x = x + s * g
    return x

_drawn_inputs = setup_inputs


def setup_inputs(seed=0):
    import zlib

    import numpy as np

    out = dict(_drawn_inputs(seed))
    spreads = {'L0_attn_ln_gamma': (1.0, 0.2),
     'L0_attn_ln_beta': (0.0, 0.1),
     'L1_ffn_bg': (0.0, 0.1),
     'L1_ffn_b1': (0.0, 0.1),
     'L1_ffn_b2': (0.0, 0.1),
     'L1_ffn_gamma': (1.0, 0.2),
     'L1_ffn_beta': (0.0, 0.1),
     'L2_attn_D': (0.0, 0.1),
     'L2_ffn_b_router': (0.0, 0.1),
     'L2_ffn_b1': (0.0, 0.1),
     'L2_ffn_b2': (0.0, 0.1),
     'L3_attn_bq': (0.0, 0.1),
     'L3_attn_bk': (0.0, 0.1),
     'L3_attn_bv': (0.0, 0.1),
     'L3_attn_bg': (0.0, 0.1),
     'L3_attn_bo': (0.0, 0.1),
     'L3_ffn_sb1': (0.0, 0.1),
     'L3_ffn_sb2': (0.0, 0.1),
     'L3_ffn_sb3': (0.0, 0.1),
     'L3_ffn_s_ln_g': (1.0, 0.2),
     'L3_ffn_s_ln_b': (0.0, 0.1),
     'L3_ffn_eg_b': (0.0, 0.1),
     'L3_ffn_exp_bias': (0.0, 0.1),
     'L3_ffn_eb1': (0.0, 0.1),
     'L3_ffn_eb2': (0.0, 0.1),
     'L3_ffn_eb3': (0.0, 0.1),
     'L3_ffn_sel_ln_g': (1.0, 0.2),
     'L3_ffn_sel_ln_b': (0.0, 0.1)}
    factors = {}
    for name, (base, spread) in spreads.items():
        noise = np.random.default_rng([zlib.crc32(name.encode()), seed]).standard_normal(out[name].shape)
        drawn = base * np.exp(spread * noise) if base else spread * noise
        out[name] = jnp.asarray(drawn.astype(out[name].dtype))
    for name, factor in factors.items():
        out[name] = (out[name] * factor).astype(out[name].dtype)
    return out
```

```python
import concourse.bass as bass
from concourse import mybir
from contextlib import ExitStack

F32 = mybir.dt.float32
F16 = mybir.dt.float16
BF16 = mybir.dt.bfloat16
I32 = mybir.dt.int32
U32 = mybir.dt.uint32
ALU = mybir.AluOpType
ACT = mybir.ActivationFunctionType
AX = mybir.AxisListType

P = 128
D = 128
BATCH, SEQ = 4, 1024
TOK = BATCH * SEQ
NT = TOK // P
CH = 512
NCH = TOK // CH
TPC = CH // P
DMA = 16


class Stage:

    def __init__(self, nc, name):
        self.nc, self.name, self.stack, self.sems = nc, name, ExitStack(), []

    def __enter__(self):
        self.stack.__enter__()
        return self

    def __exit__(self, *e):
        self.stack.__exit__(*e)
        self.nc.clear_and_free_semaphores(self.sems)
        self.nc.all_engine_barrier()

    def sb(self, name, shape, dt=F32):
        return self.stack.enter_context(self.nc.sbuf_tensor(f"{self.name}_{name}", shape, dt))

    def ps(self, name, shape, dt=F32):
        return self.stack.enter_context(self.nc.psum_tensor(f"{self.name}_{name}", shape, dt))

    def sem(self, name):
        self.sems.append(self.nc.alloc_semaphore(f"{self.name}_{name}"))
        return self.sems[-1]

    def block(self):
        return self.stack.enter_context(self.nc.Block())


class Chain:

    def __init__(self, eng, sem):
        self.eng, self.sem, self.n = eng, sem, 0

    def __call__(self, ins, base=0):
        self.n += 1
        ins.then_inc(self.sem, 1)
        self.eng.wait_ge(self.sem, base + self.n)


def rows(dram):
    return dram.rearrange("(t p) d -> p t d", p=P)


def over(ap, shape):
    return ap.to_broadcast(shape)


def make_identity(nc, ident):
    with Stage(nc, "ident") as st:
        cleared, made = st.sem("cleared"), st.sem("made")
        block = st.block()

        @block.gpsimd
        def _(pool):
            nc.gpsimd.memset(ident[:], 0.0).then_inc(cleared, 1)
            pool.wait_ge(cleared, 1)
            nc.gpsimd.affine_select(out=ident[:], in_=ident[:], compare_op=ALU.not_equal, fill=1.0, base=0,
                                    pattern=[[-1, P]], channel_multiplier=1).then_inc(made, 1)
            pool.wait_ge(made, 1)


def layernorm_stage(nc, name, ident, x_d, xn_d, xnT_d):
    NG = 4
    GT = NT // NG
    with Stage(nc, name) as st:
        x, sq = st.sb("x", [P, NT, D]), st.sb("sq", [P, GT, D])
        total, nmean = st.sb("total", [P, NT]), st.sb("nmean", [P, NT])
        var, std, rstd = st.sb("var", [P, NT]), st.sb("std", [P, NT]), st.sb("rstd", [P, NT])
        xT = st.sb("xT", [P, 2, GT * P])
        tp = st.ps("tp", [P, 2, GT * P])
        loaded = [st.sem(f"loaded{g}") for g in range(NG)]
        dve_step, var_ready, std_ready, xn_ready = (st.sem(n) for n in ("dve_step", "var_ready", "std_ready", "xn_ready"))
        turned, evacuated, stored, storedT = (st.sem(n) for n in ("turned", "evacuated", "stored", "storedT"))
        block = st.block()

        @block.sync
        def _(sp):
            for g in range(NG):
                sp.dma_start(x[:, g * GT:(g + 1) * GT, :], rows(x_d)[:, g * GT:(g + 1) * GT, :]).then_inc(loaded[g], DMA)
            for g in range(NG):
                sp.wait_ge(xn_ready, g + 1)
                sp.dma_start(rows(xn_d)[:, g * GT:(g + 1) * GT, :], x[:, g * GT:(g + 1) * GT, :]).then_inc(stored, DMA)
                sp.wait_ge(evacuated, g + 1)
                sp.dma_start(xnT_d[:, g * GT * P:(g + 1) * GT * P], xT[:, g % 2, :]).then_inc(storedT, DMA)
                sp.wait_ge(storedT, DMA * (g + 1))
            sp.wait_ge(stored, DMA * NG)

        @block.vector
        def _(dve):
            link = Chain(dve, dve_step)
            for g in range(NG):
                c = slice(g * GT, (g + 1) * GT)
                wide = [P, GT, D]
                dve.wait_ge(loaded[g], DMA)
                link(nc.vector.reduce_sum(total[:, c], x[:, c, :], AX.X))
                link(nc.vector.tensor_scalar(nmean[:, c], total[:, c], -1.0 / D, None, ALU.mult))
                link(nc.vector.tensor_tensor(x[:, c, :], x[:, c, :], over(nmean[:, c].unsqueeze(2), wide), ALU.add))
                link(nc.vector.tensor_tensor(sq[:], x[:, c, :], x[:, c, :], ALU.mult))
                link(nc.vector.reduce_sum(var[:, c], sq[:], AX.X))
                nc.vector.tensor_scalar(var[:, c], var[:, c], 1.0 / D, 1e-5, ALU.mult, ALU.add).then_inc(var_ready, 1)
                dve.wait_ge(std_ready, g + 1)
                link(nc.vector.reciprocal(rstd[:, c], std[:, c]))
                nc.vector.tensor_tensor(x[:, c, :], x[:, c, :], over(rstd[:, c].unsqueeze(2), wide),
                                        ALU.mult).then_inc(xn_ready, 1)

        @block.tensor
        def _(pe):
            for g in range(NG):
                pe.wait_ge(xn_ready, g + 1)
                if g >= 2:
                    pe.wait_ge(evacuated, g - 1)
                for t in range(GT):
                    last = nc.tensor.transpose(tp[:, g % 2, t * P:(t + 1) * P], x[:, g * GT + t, :], ident[:])
                last.then_inc(turned, 1)

        @block.scalar
        def _(act):
            def root(g):
                c = slice(g * GT, (g + 1) * GT)
                act.wait_ge(var_ready, g + 1)
                nc.scalar.activation(std[:, c], var[:, c], ACT.Sqrt).then_inc(std_ready, 1)
            root(0)
            for g in range(NG):
                if g + 1 < NG:
                    root(g + 1)
                act.wait_ge(turned, g + 1)
                if g >= 2:
                    act.wait_ge(storedT, DMA * (g - 1))
                nc.scalar.activation(xT[:, g % 2, :], tp[:, g % 2, :], ACT.Copy).then_inc(evacuated, 1)


def project_l0(nc, xnT_d, w_q, w_k, w_v, q_d, kh_d, kl_d, v_d):
    HP = 8
    HD = 64
    with Stage(nc, "proj0") as st:
        xnT = st.sb("xnT", [P, TOK])
        w = st.sb("w", [P, 2, 3, P])
        hi, lo = st.sb("hi", [P, 2, TOK], F16), st.sb("lo", [P, 2, TOK], F16)
        v = st.sb("v", [P, NT, P])
        ps = st.ps("ps", [P, 8, CH])
        x_loaded, stacked, v_stored = st.sem("x_loaded"), st.sem("stacked"), st.sem("v_stored")
        w_loaded = [st.sem("w_loaded0"), st.sem("w_loaded1")]
        made, hi_ready, lo_ready, v_ready = (st.sem(n) for n in ("made", "hi_ready", "lo_ready", "v_ready"))
        block = st.block()
        PIECES = 2 * NCH + NCH
        NST = 6

        @block.sync
        def _(sp):
            def load_w(hp, slot):
                for j, src in enumerate((w_q, w_k, w_v)):
                    sp.dma_start(w[:, slot, j, :], src[:, bass.ds(hp * P, P)]).then_inc(w_loaded[slot], DMA)
            sp.dma_start(xnT[:], xnT_d[:, :]).then_inc(x_loaded, DMA)
            load_w(0, 0)
            load_w(1, 1)
            for hp in range(HP):
                if 2 <= hp + 1 < HP:
                    sp.wait_ge(made, PIECES * hp)
                    load_w(hp + 1, (hp + 1) % 2)
                sp.wait_ge(hi_ready, 2 * NCH * (hp + 1))
                sp.wait_ge(lo_ready, 2 * NCH * (hp + 1))
                for g in range(2):
                    own = slice(g * HD, (g + 1) * HD)
                    h = 2 * hp + g
                    for part, src in ((0, hi), (1, lo)):
                        sp.dma_start(q_d[h, part * HD:(part + 1) * HD, :], src[own, 0, :]).then_inc(stacked, DMA)
                        for r in range(2):
                            sp.dma_start((kh_d, kl_d)[part][h, r * HD:(r + 1) * HD, :], src[own, 1, :]).then_inc(stacked, DMA)
                sp.wait_ge(v_ready, NCH * (hp + 1))
                sp.dma_start(v_d[hp].rearrange("(t p) e -> p t e", p=P), v[:]).then_inc(v_stored, DMA)
            sp.wait_ge(stacked, 2 * NST * DMA * HP)
            sp.wait_ge(v_stored, DMA * HP)

        @block.tensor
        def _(pe):
            pe.wait_ge(x_loaded, DMA)
            n = 0
            for hp in range(HP):
                pe.wait_ge(w_loaded[hp % 2], 3 * DMA * (hp // 2 + 1))
                for piece in range(PIECES):
                    if n >= 8:
                        m, before = divmod(n - 8, PIECES)
                        if before < 2 * NCH:
                            pe.wait_ge(lo_ready, 2 * NCH * m + before + 1)
                        else:
                            pe.wait_ge(v_ready, NCH * m + before - 2 * NCH + 1)
                    j, c = divmod(piece, NCH)
                    if j < 2:
                        last = nc.tensor.matmul(ps[:, n % 8, :], w[:, hp % 2, j, :], xnT[:, c * CH:(c + 1) * CH],
                                                start=True, stop=True)
                    else:
                        for t in range(TPC):
                            tile = c * TPC + t
                            last = nc.tensor.matmul(ps[:, n % 8, t * P:(t + 1) * P], xnT[:, tile * P:(tile + 1) * P],
                                                    w[:, hp % 2, 2, :], start=True, stop=True)
                    last.then_inc(made, 1)
                    n += 1

        @block.scalar
        def _(act):
            for hp in range(HP):
                for piece in range(PIECES):
                    n = hp * PIECES + piece
                    j, c = divmod(piece, NCH)
                    act.wait_ge(made, n + 1)
                    if j < 2:
                        if piece == 0 and hp >= 1:
                            act.wait_ge(stacked, 2 * NST * DMA * hp)
                        nc.scalar.activation(hi[:, j, c * CH:(c + 1) * CH], ps[:, n % 8, :], ACT.Copy,
                                             scale=HD ** -0.5 if j == 0 else 1.0).then_inc(hi_ready, 1)
                    else:
                        if c == 0 and hp >= 1:
                            act.wait_ge(v_stored, DMA * hp)
                        nc.scalar.activation(v[:, c * TPC:(c + 1) * TPC, :],
                                             ps[:, n % 8, :].rearrange("p (t e) -> p t e", t=TPC),
                                             ACT.Copy).then_inc(v_ready, 1)

        @block.vector
        def _(dve):
            for hp in range(HP):
                for piece in range(2 * NCH):
                    n = hp * PIECES + piece
                    j, c = divmod(piece, NCH)
                    dve.wait_ge(hi_ready, hp * 2 * NCH + piece + 1)
                    if piece == 0 and hp >= 1:
                        dve.wait_ge(stacked, 2 * NST * DMA * hp)
                    nc.vector.scalar_tensor_tensor(out=lo[:, j, c * CH:(c + 1) * CH], in0=ps[:, n % 8, :],
                                                   scalar=HD ** -0.5 if j == 0 else 1.0,
                                                   in1=hi[:, j, c * CH:(c + 1) * CH], op0=ALU.mult,
                                                   op1=ALU.subtract).then_inc(lo_ready, 1)


def attention_stage(nc, name, ident, q_d, k_ds, v_d, o_ds, scale_d, groups, heads, stack_rows, head_rows, qchunk, out_scale):
    NK = len(k_ds)
    KT = SEQ // P
    QT = qchunk // P
    UPC = QT * heads
    NC = SEQ // qchunk
    U = UPC * NC
    NI = BATCH * groups
    col = P // heads
    NPROB = 4
    HALF = U // 2
    assert U % NPROB == 0 and NC % 2 == 0 and U % 2 == 0
    with Stage(nc, name) as st:
        q = st.sb("q", [P, 2, heads, SEQ], q_d.dtype)
        k = [st.sb(f"k{n}", [P, 2, heads, SEQ], q_d.dtype) for n in range(NK)]
        v = st.sb("v", [P, 2, KT, P])
        prob = st.sb("prob", [P, NPROB, SEQ])
        probT = st.sb("probT", [P, 2, heads, KT, qchunk])
        nmax, sums = st.sb("nmax", [P, 2, U]), st.sb("sums", [P, 2, U])
        inv, invT = st.sb("inv", [P, 2, UPC]), st.sb("invT", [UPC, 2, P])
        invB = st.sb("invB", [P, 2, qchunk])
        out = st.sb("out", [P, 2, qchunk])
        score = st.ps("score", [P, 2, SEQ])
        turn = st.ps("turn", [P, KT, P])
        acc = st.ps("acc", [P, CH])
        small = st.ps("small", [P, CH])
        loaded = [st.sem("loaded0"), st.sem("loaded1")]
        names = ("zeroed", "scored", "maxed", "exped", "turned", "copied_a", "copied_v", "weighed", "inverted", "inv_turned",
                 "inv_copied", "normed")
        (zeroed, scored, maxed, exped, turned, copied_a, copied_v, weighed, inverted, inv_turned, inv_copied,
         normed) = (st.sem(n) for n in names)
        inv_out, inv_back, out_stored = ([st.sem(f"{n}{s}") for s in range(2)] for n in ("inv_out", "inv_back", "out_stored"))
        block = st.block()
        LOADS = NK + 2

        def iterations(eng, body):
            body(0, 0, True, False)
            with eng.Fori(0, (NI - 2) // 2) as j:
                body(2 * j + 1, 1, False, False)
                body(2 * j + 2, 0, False, False)
            body(NI - 1, 1, False, True)

        @block.sync
        def _(sp):
            def load(i, slot):
                b, g = i // groups, i % groups
                tok = bass.ds(b * SEQ, SEQ)
                for src, dst in [(q_d, q)] + list(zip(k_ds, k)):
                    sp.dma_start(dst[0:stack_rows, slot, :, :],
                                 src[bass.ds(g * heads, heads), :, tok].rearrange("h r t -> r h t")).then_inc(loaded[slot], DMA)
                sp.dma_start(v[:, slot, :, 0:heads * head_rows],
                             v_d[bass.ds(g, 1), tok, :].rearrange("a (t p) e -> p (a t) e", p=P)).then_inc(loaded[slot], DMA)

            def body(i, slot, first, final):
                if not final:
                    if not first:
                        sp.wait_ge(weighed, NC * i)
                    load(i + 1, 1 - slot)
                for c in range(NC):
                    g = NC * i + c
                    s = c % 2
                    turn_no = NC // 2 * i + c // 2
                    sp.wait_ge(inv_copied, g + 1)
                    sp.dma_start(scale_d[s], invT[:, s, :]).then_inc(inv_out[s], DMA)
                    sp.wait_ge(inv_out[s], DMA * (turn_no + 1))
                    for h in range(heads):
                        sp.dma_start(invB[h * col:h * col + head_rows, s, :],
                                     scale_d[s].rearrange("(h t) q -> h (t q)", h=heads)[h].partition_broadcast(head_rows)
                                     ).then_inc(inv_back[s], DMA)
                    if not (first and c == 0):
                        store(g - 1, i if c else i - 1, (c - 1) % NC, 1 - s)

            def store(g, i, c, s):
                sp.wait_ge(normed, g + 1)
                b, grp = i // groups, i % groups
                for h in range(heads):
                    sp.dma_start(o_ds[h][bass.ds(grp, 1), :, bass.ds(b * SEQ + c * qchunk, qchunk)].rearrange("a r t -> (a r) t"),
                                 out[h * col:h * col + head_rows, s, :]).then_inc(out_stored[s], DMA)

            if stack_rows < P:
                sp.wait_ge(zeroed, NK + 1)
            load(0, 0)
            iterations(sp, body)
            store(NC * NI - 1, NI - 1, NC - 1, 1)
            for s in range(2):
                sp.wait_ge(out_stored[s], DMA * heads * NC * NI // 2)

        @block.gpsimd
        def _(pool):
            if stack_rows < P:
                for t in [q] + k:
                    nc.gpsimd.memset(t[:], 0.0).then_inc(zeroed, 1)

        @block.tensor
        def _(pe):
            def scores(i, slot, u, first):
                if u == 0:
                    pe.wait_ge(loaded[slot], (i // 2 + 1) * LOADS * DMA)
                if not (first and u < 2):
                    pe.wait_ge(exped, U * i + u - 1)
                c, r = divmod(u, UPC)
                t, h = divmod(r, heads)
                qt = c * QT + t
                for half in range(SEQ // CH):
                    for n in range(NK):
                        last = nc.tensor.matmul(score[:, u % 2, half * CH:(half + 1) * CH],
                                                q[:, slot, h, qt * P:(qt + 1) * P],
                                                k[n][:, slot, h, half * CH:(half + 1) * CH], start=(n == 0), stop=(n == NK - 1))
                last.then_inc(scored, 1)

            def body(i, slot, first, final):
                for u in range(U):
                    if u + 1 < U:
                        scores(i, slot, u + 1, first)
                    elif not final:
                        scores(i + 1, 1 - slot, 0, False)
                    pe.wait_ge(exped, U * i + u + 1)
                    if not (first and u == 0):
                        if u % 2:
                            pe.wait_ge(copied_a, HALF * i + (u + 1) // 2)
                        else:
                            pe.wait_ge(copied_v, HALF * i + u // 2)
                    for t in range(KT):
                        last = nc.tensor.transpose(turn[:, t, :], prob[:, u % NPROB, t * P:(t + 1) * P], ident[:])
                    last.then_inc(turned, 1)
                    if u % UPC == UPC - 1:
                        c = u // UPC
                        g = NC * i + c
                        s = c % 2
                        pe.wait_ge(inverted, g + 1)
                        if not (first and c == 0):
                            pe.wait_ge(inv_copied, g)
                        nc.tensor.transpose(small[0:UPC, 0:P], inv[:, s, :], ident[:]).then_inc(inv_turned, 1)
                        pe.wait_ge(copied_a, HALF * i + (u + 1) // 2)
                        pe.wait_ge(copied_v, HALF * i + (u + 1) // 2)
                        if not (first and c == 0):
                            pe.wait_ge(normed, g)
                        for t in range(KT):
                            for h in range(heads):
                                last = nc.tensor.matmul(acc[h * col:h * col + head_rows, 0:qchunk],
                                                        v[:, slot, t, h * head_rows:(h + 1) * head_rows], probT[:, s, h, t, :],
                                                        start=(t == 0), stop=(t == KT - 1))
                        last.then_inc(weighed, 1)

            scores(0, 0, 0, True)
            iterations(pe, body)

        @block.scalar
        def _(act):
            def body(i, slot, first, final):
                for u in range(U):
                    act.wait_ge(maxed, U * i + u + 1)
                    if not (first and u < NPROB):
                        act.wait_ge(turned, U * i + u - NPROB + 1)
                    nc.scalar.activation(prob[:, u % NPROB, :], score[:, u % 2, :], ACT.Exp,
                                         bias=nmax[:, slot, u:u + 1], accum_out=sums[:, slot, u:u + 1]).then_inc(exped, 1)
                    if u >= 1:
                        copy(i, slot, u - 1, first)

            def copy(i, slot, u, first):
                if u % 2 == 0:
                    c, r = divmod(u, UPC)
                    t, h = divmod(r, heads)
                    act.wait_ge(turned, U * i + u + 1)
                    if not (first and c < 2):
                        act.wait_ge(weighed, NC * i + c - 1)
                    nc.scalar.activation(probT[:, c % 2, h, :, t * P:(t + 1) * P], turn[:], ACT.Copy
                                         ).then_inc(copied_a, 1)

            iterations(act, body)

        @block.vector
        def _(dve):
            def copy(i, slot, u, first):
                if u % 2 == 1:
                    c, r = divmod(u, UPC)
                    t, h = divmod(r, heads)
                    dve.wait_ge(turned, U * i + u + 1)
                    if not (first and c < 2):
                        dve.wait_ge(weighed, NC * i + c - 1)
                    nc.vector.tensor_copy(probT[:, c % 2, h, :, t * P:(t + 1) * P], turn[:]).then_inc(copied_v, 1)

            def maximum(i, slot, u):
                dve.wait_ge(scored, U * i + u + 1)
                nc.vector.tensor_reduce(nmax[:, slot, u:u + 1], score[:, u % 2, :], AX.X, ALU.max, negate=True).then_inc(maxed, 1)

            def invert(i, slot, c):
                g = NC * i + c
                s = c % 2
                nc.vector.reciprocal(inv[:, s, :].rearrange("p (h t) -> p t h", h=heads),
                                     sums[:, slot, c * UPC:(c + 1) * UPC].rearrange("p (t h) -> p t h", h=heads)
                                     ).then_inc(inverted, 1)

            def inv_copy(i, slot, c):
                g = NC * i + c
                dve.wait_ge(inv_turned, g + 1)
                nc.vector.tensor_scalar(invT[:, c % 2, :], small[0:UPC, 0:P], out_scale, None,
                                        ALU.mult).then_inc(inv_copied, 1)

            def normalise(i, slot, c, first):
                g = NC * i + c
                s = c % 2
                dve.wait_ge(weighed, g + 1)
                dve.wait_ge(inv_back[s], DMA * heads * (NC // 2 * i + c // 2 + 1))
                if not (first and c < 2):
                    dve.wait_ge(out_stored[s], DMA * heads * (NC // 2 * i + c // 2))
                for h in range(heads):
                    own = slice(h * col, h * col + head_rows)
                    if heads * head_rows == P:
                        own = slice(0, P)
                    last = nc.vector.tensor_tensor(out[own, s, :], acc[own, 0:qchunk], invB[own, s, :], ALU.mult)
                    if heads * head_rows == P:
                        break
                last.then_inc(normed, 1)

            DELAY = 3

            def body(i, slot, first, final):
                if first:
                    maximum(i, slot, 0)
                for u in range(U):
                    if u + 1 < U:
                        maximum(i, slot, u + 1)
                    elif not final:
                        maximum(i + 1, 1 - slot, 0)
                    c, r = divmod(u, UPC)
                    if r == UPC - 1:
                        dve.wait_ge(exped, U * i + u + 1)
                        invert(i, slot, c)
                    copy(i, slot, u, first)
                    if r == UPC - 1:
                        inv_copy(i, slot, c)
                    if r == DELAY and not (first and c == 0):
                        normalise(i if c else i - 1, slot if c else 1 - slot, (c - 1) % NC, first)

            iterations(dve, body)
            normalise(NI - 1, 1, NC - 1, False)


def broadcast_rows(vec, n=P):
    return vec.partition_broadcast(n)


def output_projection(nc, name, o_d, w, bias, resid_d, s_d):
    KH = o_d.shape[0] // P
    with Stage(nc, name) as st:
        o = st.sb("o", [P, 2, KH, CH])
        wt = st.sb("wt", [P, KH, D])
        bias_b = st.sb("bias_b", [P, D])
        res = st.sb("res", [P, 2, TPC, D])
        y = st.sb("y", [P, 2, TPC, D])
        acc = st.ps("acc", [P, 2, TPC, D])
        consts = st.sem("consts")
        o_loaded, r_loaded, stored = ([st.sem(f"{n}{s}") for s in range(2)] for n in ("o_loaded", "r_loaded", "stored"))
        projected, summed, biased = st.sem("projected"), st.sem("summed"), st.sem("biased")
        block = st.block()

        def iterations(eng, body):
            body(0, 0, True)
            body(1, 1, True)
            with eng.Fori(1, NCH // 2) as j:
                body(2 * j, 0, False)
                body(2 * j + 1, 1, False)

        @block.sync
        def _(sp):
            sp.dma_start(wt[:], w.rearrange("(k p) d -> p k d", p=P)).then_inc(consts, DMA)
            sp.dma_start(bias_b[:], broadcast_rows(bias)).then_inc(consts, DMA)

            def load(i, slot, first):
                if not first:
                    sp.wait_ge(projected, i - 1)
                sp.dma_start(o[:, slot, :, :], o_d.rearrange("(k p) t -> p k t", p=P)[:, :, bass.ds(i * CH, CH)]
                             ).then_inc(o_loaded[slot], DMA)
                if resid_d is not None:
                    if not first:
                        sp.wait_ge(summed, i - 1)
                    sp.dma_start(res[:, slot, :, :], rows(resid_d)[:, bass.ds(i * TPC, TPC), :]).then_inc(r_loaded[slot], DMA)
            iterations(sp, load)
            for s in range(2):
                sp.wait_ge(stored[s], DMA * NCH // 2)

        @block.tensor
        def _(pe):
            pe.wait_ge(consts, 2 * DMA)

            def body(i, slot, first):
                pe.wait_ge(o_loaded[slot], DMA * ((i - slot) // 2 + 1))
                if not first:
                    pe.wait_ge(summed, i - 1)
                for t in range(TPC):
                    for h in range(KH):
                        last = nc.tensor.matmul(acc[:, slot, t, :], o[:, slot, h, t * P:(t + 1) * P], wt[:, h, :],
                                                start=(h == 0), stop=(h == KH - 1))
                last.then_inc(projected, 1)
            iterations(pe, body)

        @block.vector
        def _(dve):
            dve.wait_ge(consts, 2 * DMA)

            def body(i, slot, first):
                dve.wait_ge(projected, i + 1)
                if not first:
                    dve.wait_ge(stored[slot], DMA * ((i - slot) // 2))
                ins = nc.vector.tensor_tensor(y[:, slot, :, :], acc[:, slot, :, :],
                                              bias_b[:].unsqueeze(1).to_broadcast([P, TPC, D]), ALU.add)
                if resid_d is not None:
                    ins.then_inc(biased, 1)
                    dve.wait_ge(biased, i + 1)
                    dve.wait_ge(r_loaded[slot], DMA * ((i - slot) // 2 + 1))
                    ins = nc.vector.tensor_tensor(y[:, slot, :, :], y[:, slot, :, :], res[:, slot, :, :], ALU.add)
                ins.then_inc(summed, 1)
            iterations(dve, body)

        @block.scalar
        def _(act):
            def body(i, slot, first):
                act.wait_ge(summed, i + 1)
                act.dma_start(rows(s_d)[:, bass.ds(i * TPC, TPC), :], y[:, slot, :, :]).then_inc(stored[slot], DMA)
            iterations(act, body)


def combine_stage(nc, name, ident, x_d, s_d, s_norm, f_d, f_turned, f_norm, x_out, xn_d, xnT_d):
    NG = 4
    GT = NT // NG
    wide = [P, GT, D]
    with Stage(nc, name) as st:
        x, s, f = (st.sb(n, [P, NT, D]) for n in ("x", "s", "f"))
        fT = st.sb("fT", [P, TOK]) if f_turned else None
        sq = st.sb("sq", wide)
        gate = st.sb("gate", wide)
        total, nmean, var, std, rstd = (st.sb(n, [P, GT]) for n in ("total", "nmean", "var", "std", "rstd"))
        affine = {id(n): (st.sb(f"gamma{m}", [P, D]), st.sb(f"beta{m}", [P, D])) for m, n in enumerate((s_norm, f_norm)) if n}
        xT = st.sb("xT", [P, 2, GT * P])
        ftp = st.ps("ftp", wide)
        tp = st.ps("tp", [P, 2, GT * P])
        consts, dve_step, f_tp = st.sem("consts"), st.sem("dve_step"), st.sem("f_tp")
        loaded = [st.sem(f"loaded{g}") for g in range(NG)]
        var_ready, std_ready, f_ready, gated, xn_ready, x_ready = (
            st.sem(n) for n in ("var_ready", "std_ready", "f_ready", "gated", "xn_ready", "x_ready"))
        turned, evacuated, storedT, stored = (st.sem(n) for n in ("turned", "evacuated", "storedT", "stored"))
        block = st.block()
        last_stage = xn_d is None
        NORMS = bool(s_norm) + bool(f_norm) + (not last_stage)
        grp = lambda g: slice(g * GT, (g + 1) * GT)

        @block.sync
        def _(sp):
            for n in (s_norm, f_norm):
                if n:
                    for t, v in zip(affine[id(n)], n[:2]):
                        sp.dma_start(t[:], broadcast_rows(v)).then_inc(consts, DMA)
            for g in range(NG):
                sp.dma_start(x[:, grp(g), :], rows(x_d)[:, grp(g), :]).then_inc(loaded[g], DMA)
                sp.dma_start(s[:, grp(g), :], rows(s_d)[:, grp(g), :]).then_inc(loaded[g], DMA)
                if f_turned:
                    sp.dma_start(fT[:, g * GT * P:(g + 1) * GT * P], f_d[:, g * GT * P:(g + 1) * GT * P]).then_inc(loaded[g], DMA)
                else:
                    sp.dma_start(f[:, grp(g), :], rows(f_d)[:, grp(g), :]).then_inc(loaded[g], DMA)
            for g in range(NG):
                sp.wait_ge(x_ready, g + 1)
                sp.dma_start(rows(x_out)[:, grp(g), :], x[:, grp(g), :]).then_inc(stored, DMA)
                if not last_stage:
                    sp.wait_ge(xn_ready, g + 1)
                    sp.dma_start(rows(xn_d)[:, grp(g), :], s[:, grp(g), :]).then_inc(stored, DMA)
                    sp.wait_ge(evacuated, g + 1)
                    sp.dma_start(xnT_d[:, g * GT * P:(g + 1) * GT * P], xT[:, g % 2, :]).then_inc(storedT, DMA)
                    sp.wait_ge(storedT, DMA * (g + 1))
            sp.wait_ge(stored, DMA * NG * (1 if last_stage else 2))

        @block.vector
        def _(dve):
            link = Chain(dve, dve_step)
            roots = [0]

            def normalise(out, src, norm, eps):
                link(nc.vector.reduce_sum(total[:], src, AX.X))
                link(nc.vector.tensor_scalar(nmean[:], total[:], -1.0 / D, None, ALU.mult))
                link(nc.vector.tensor_tensor(out, src, over(nmean[:].unsqueeze(2), wide), ALU.add))
                link(nc.vector.tensor_tensor(sq[:], out, out, ALU.mult))
                link(nc.vector.reduce_sum(var[:], sq[:], AX.X))
                nc.vector.tensor_scalar(var[:], var[:], 1.0 / D, eps, ALU.mult, ALU.add).then_inc(var_ready, 1)
                roots[0] += 1
                dve.wait_ge(std_ready, roots[0])
                link(nc.vector.reciprocal(rstd[:], std[:]))
                ins = nc.vector.tensor_tensor(out, out, over(rstd[:].unsqueeze(2), wide), ALU.mult)
                if norm:
                    gamma, beta = affine[id(norm)]
                    link(ins)
                    link(nc.vector.tensor_tensor(out, out, gamma[:].unsqueeze(1).to_broadcast(wide), ALU.mult))
                    ins = nc.vector.tensor_tensor(out, out, beta[:].unsqueeze(1).to_broadcast(wide), ALU.add)
                return ins

            if affine:
                dve.wait_ge(consts, 2 * DMA * len(affine))
            for g in range(NG):
                dve.wait_ge(loaded[g], 3 * DMA)
                if s_norm:
                    link(normalise(s[:, grp(g), :], s[:, grp(g), :], s_norm, s_norm[2]))
                if f_turned:
                    dve.wait_ge(f_tp, g + 1)
                    src = ftp[:]
                else:
                    src = f[:, grp(g), :]
                if f_norm:
                    normalise(f[:, grp(g), :], src, f_norm, f_norm[2]).then_inc(f_ready, 1)
                elif f_turned:
                    nc.vector.tensor_copy(f[:, grp(g), :], src).then_inc(f_ready, 1)
                dve.wait_ge(gated, g + 1)
                link(nc.vector.tensor_tensor(s[:, grp(g), :], s[:, grp(g), :], gate[:], ALU.mult))
                last = nc.vector.tensor_tensor(x[:, grp(g), :], x[:, grp(g), :], s[:, grp(g), :], ALU.add)
                last.then_inc(x_ready, 1)
                dve.wait_ge(x_ready, g + 1)
                if not last_stage:
                    normalise(s[:, grp(g), :], x[:, grp(g), :], None, 1e-5).then_inc(xn_ready, 1)

        @block.tensor
        def _(pe):
            def turn_f(g):
                pe.wait_ge(loaded[g], 3 * DMA)
                if g:
                    pe.wait_ge(f_ready, g)
                for t in range(GT):
                    last = nc.tensor.transpose(ftp[:, t, :], fT[:, (g * GT + t) * P:(g * GT + t + 1) * P], ident[:])
                last.then_inc(f_tp, 1)
            for g in range(NG):
                if f_turned:
                    turn_f(g)
                if not last_stage:
                    pe.wait_ge(xn_ready, g + 1)
                    if g >= 2:
                        pe.wait_ge(evacuated, g - 1)
                    for t in range(GT):
                        last = nc.tensor.transpose(tp[:, g % 2, t * P:(t + 1) * P], s[:, g * GT + t, :], ident[:])
                    last.then_inc(turned, 1)

        @block.scalar
        def _(act):
            n = [0]

            def root():
                n[0] += 1
                act.wait_ge(var_ready, n[0])
                nc.scalar.activation(std[:], var[:], ACT.Sqrt).then_inc(std_ready, 1)
            for g in range(NG):
                if s_norm:
                    root()
                if f_norm:
                    root()
                if f_norm or f_turned:
                    act.wait_ge(f_ready, g + 1)
                else:
                    act.wait_ge(loaded[g], 3 * DMA)
                if g:
                    act.wait_ge(x_ready, g)
                nc.scalar.activation(gate[:], f[:, grp(g), :], ACT.Silu).then_inc(gated, 1)
                if not last_stage:
                    root()
                    act.wait_ge(turned, g + 1)
                    if g >= 2:
                        act.wait_ge(storedT, DMA * (g - 1))
                    nc.scalar.activation(xT[:, g % 2, :], tp[:, g % 2, :], ACT.Copy).then_inc(evacuated, 1)


def routing_stage(nc, name, ident, kind, xnT_d, w, bias, c_d, cT_d):
    grouped = kind == "grouped"
    E = 32 if grouped else 8
    EP = 32
    PARTS = 3
    CAP = int(1.25 * TOK / 8)
    with Stage(nc, name) as st:
        xnT = st.sb("xnT", [P, TOK])
        wr, wT = st.sb("wr", [EP, D]), st.sb("wT", [P, E])
        bias_b = st.sb("bias_b", [P, E])
        score, pick, tmp = (st.sb(n, [P, NT, E]) for n in ("score", "pick", "tmp"))
        comb = st.sb("comb", [P, NT, EP])
        rest = st.sb("rest", [P, NT, EP])
        parts = st.sb("parts", [P, NT, PARTS, EP], BF16)
        ident16 = st.sb("ident16", [P, P], BF16)
        best = st.sb("best", [P, NT, 8])
        gs = [st.sb(f"gs{n}", [P, NT * 8]) for n in range(5)]
        pair, pair2 = st.sb("pair", [P, NT, 8, 8]), st.sb("pair2", [P, NT, 8, 8])
        before = st.sb("before", [P, 8, 8])
        rank, rank2 = st.sb("rank", [P, NT, 8]), st.sb("rank2", [P, NT, 8])
        red = st.sb("red", [P, NT])
        earlier, ones = st.sb("earlier", [P, P]), st.sb("ones", [P, P])
        cT = st.sb("cT", [PARTS * EP, TOK], BF16)
        cF = st.sb("cF", [EP, TOK])
        lg = st.ps("lg", [P, NT, EP])
        tr = st.ps("tr", [P, 2, CH])
        trb = st.ps("trb", [PARTS * EP, 2, 8, P], BF16)
        posp = st.ps("posp", [P, 2, CH])
        x_loaded, consts, made, stored = (st.sem(n) for n in ("x_loaded", "consts", "made", "stored"))
        w_turned, w_ready, logits, dve_step, act_in, act_out = (
            st.sem(n) for n in ("w_turned", "w_ready", "logits", "dve_step", "act_in", "act_out"))
        mask_ready, counted, parts_ready, f_turned, b_turned, f_copied, b_copied = (
            st.sem(n) for n in ("mask_ready", "counted", "parts_ready", "f_turned", "b_turned", "f_copied", "b_copied"))
        block = st.block()
        NCONST = 1 + (bias is not None)

        @block.sync
        def _(sp):
            sp.dma_start(wr[0:32, :] if grouped else wT[:], w).then_inc(consts, DMA)
            if bias is not None:
                sp.dma_start(bias_b[:], broadcast_rows(bias)).then_inc(consts, DMA)
            sp.dma_start(xnT[:], xnT_d[:, :]).then_inc(x_loaded, DMA)
            sp.wait_ge(f_copied, NT // 4)
            sp.dma_start(c_d[:, :], cF[:]).then_inc(stored, DMA)
            sp.wait_ge(b_copied, NT // 8)
            sp.dma_start(cT_d[:, :], cT[:]).then_inc(stored, DMA)
            sp.wait_ge(stored, 2 * DMA)

        @block.gpsimd
        def _(pool):
            nc.gpsimd.memset(before[:], 1.0).then_inc(made, 1)
            nc.gpsimd.memset(earlier[:], 1.0).then_inc(made, 1)
            nc.gpsimd.memset(ones[:], 1.0).then_inc(made, 1)
            nc.gpsimd.memset(comb[:], 0.0).then_inc(made, 1)
            nc.gpsimd.tensor_copy(ident16[:], ident[:]).then_inc(made, 1)
            pool.wait_ge(made, 5)
            nc.gpsimd.affine_select(out=before[:], in_=before[:], compare_op=ALU.is_ge, fill=0.0, base=-1,
                                    pattern=[[1, 8], [-1, 8]], channel_multiplier=0).then_inc(made, 1)
            nc.gpsimd.affine_select(out=earlier[:], in_=earlier[:], compare_op=ALU.is_ge, fill=0.0, base=-1,
                                    pattern=[[1, P]], channel_multiplier=-1).then_inc(made, 1)

        @block.tensor
        def _(pe):
            if grouped:
                pe.wait_ge(consts, NCONST * DMA)
                nc.tensor.transpose(tr[:, 0, 0:32], wr[0:32, :], ident[0:32, 0:32]).then_inc(w_turned, 1)
                pe.wait_ge(w_ready, 1)
            else:
                pe.wait_ge(consts, NCONST * DMA)
            pe.wait_ge(x_loaded, DMA)
            for t in range(NT):
                last = nc.tensor.matmul(lg[:, t, 0:E], xnT[:, t * P:(t + 1) * P], wT[:], start=True, stop=True)
            last.then_inc(logits, 1)
            if kind == "capacity":
                pe.wait_ge(mask_ready, 1)
                m = pick[:].rearrange("p t e -> p (t e)")
                nc.tensor.matmul(posp[:, 0, 0:NT * E], earlier[:], m, start=True, stop=True)
                nc.tensor.matmul(posp[:, 1, 0:NT * E], ones[:], m, start=True, stop=True).then_inc(counted, 1)
            pe.wait_ge(parts_ready, 1)
            for t in range(NT):
                if t % 4 == 0 and t >= 8:
                    pe.wait_ge(f_copied, t // 4 - 1)
                last = nc.tensor.transpose(tr[0:EP, t // 4 % 2, t % 4 * P:(t % 4 + 1) * P], comb[:, t, :], ident[:])
                if t % 4 == 3:
                    last.then_inc(f_turned, 1)
            for t in range(NT):
                if t % 8 == 0 and t >= 16:
                    pe.wait_ge(b_copied, t // 8 - 1)
                last = nc.tensor.transpose(trb[:, t // 8 % 2, t % 8, :], parts[:, t, :, :].rearrange("p a e -> p (a e)"), ident16[:])
                if t % 8 == 7:
                    last.then_inc(b_turned, 1)

        @block.scalar
        def _(act):
            if grouped:
                act.wait_ge(logits, 1)
                nc.scalar.activation(score[:], lg[:, :, 0:E], ACT.Sigmoid).then_inc(act_out, 1)
            else:
                act.wait_ge(act_in, 1)
                nc.scalar.activation(score[:], tmp[:], ACT.Exp).then_inc(act_out, 1)
            for n in range(NT // 4):
                act.wait_ge(f_turned, n + 1)
                nc.scalar.activation(cF[:, n * CH:(n + 1) * CH], tr[0:EP, n % 2, :], ACT.Copy).then_inc(f_copied, 1)

        @block.vector
        def _(dve):
            link = Chain(dve, dve_step)
            V = nc.vector
            full = [P, NT, E]
            per_tok = lambda a: over(a[:].unsqueeze(2), full)

            def ranks(src):
                four = [P, NT, 8, 8]
                vi, vj = over(src.unsqueeze(3), four), src.unsqueeze(2).to_broadcast(four)
                link(V.tensor_tensor(pair[:], vj, vi, ALU.is_gt))
                link(V.tensor_tensor(pair2[:], vj, vi, ALU.is_equal))
                flat = lambda a: a[:].rearrange("p t i j -> p t (i j)")
                link(V.tensor_tensor(flat(pair2), flat(pair2),
                                     before[:].rearrange("p i j -> p (i j)").unsqueeze(1).to_broadcast([P, NT, 64]), ALU.mult))
                link(V.tensor_tensor(flat(pair), flat(pair), flat(pair2), ALU.add))
                link(V.reduce_sum(rank[:], pair[:], AX.X))

            if grouped:
                dve.wait_ge(w_turned, 1)
                V.tensor_copy(wT[:], tr[:, 0, 0:32]).then_inc(w_ready, 1)
            dve.wait_ge(consts, NCONST * DMA)
            dve.wait_ge(made, 7)
            bias_f = bias_b[:].unsqueeze(1).to_broadcast(full)
            if grouped:
                dve.wait_ge(act_out, 1)
                link(V.tensor_tensor(tmp[:], score[:], bias_f, ALU.add))
                member = lambda j: tmp[:].rearrange("p t (g m) -> p (t g) m", m=4)[:, :, j]
                link(V.tensor_tensor(gs[0][:], member(0), member(1), ALU.max))
                link(V.tensor_tensor(gs[1][:], member(0), member(1), ALU.min))
                link(V.tensor_tensor(gs[2][:], member(2), member(3), ALU.max))
                link(V.tensor_tensor(gs[3][:], member(2), member(3), ALU.min))
                link(V.tensor_tensor(gs[1][:], gs[1][:], gs[3][:], ALU.max))
                link(V.tensor_tensor(gs[3][:], gs[0][:], gs[2][:], ALU.min))
                link(V.tensor_tensor(gs[4][:], gs[0][:], gs[2][:], ALU.max))
                link(V.tensor_tensor(gs[3][:], gs[3][:], gs[1][:], ALU.max))
                link(V.tensor_tensor(gs[0][:], gs[4][:], gs[3][:], ALU.add))
                ranks(gs[0][:].rearrange("p (t g) -> p t g", g=8))
                link(V.tensor_scalar(rank[:], rank[:], 4.0, None, ALU.is_lt))
                link(V.tensor_tensor(tmp[:].rearrange("p t (g m) -> p (t g) m", m=4), tmp[:].rearrange("p t (g m) -> p (t g) m", m=4),
                                     over(rank[:].rearrange("p t g -> p (t g)").unsqueeze(2), [P, NT * 8, 4]), ALU.mult))
                for t in range(NT):
                    last = V.max(best[:, t, :], tmp[:, t, :])
                link(last)
                TAKEN = -1e30
                for t in range(NT):
                    last = V.match_replace(pick[:, t, :], best[:, t, :], tmp[:, t, :], TAKEN)
                link(last)
                link(V.tensor_scalar(pick[:], pick[:], TAKEN / 2, None, ALU.is_lt))
                link(V.tensor_tensor(pick[:], pick[:], score[:], ALU.mult))
                link(V.reduce_sum(red[:], pick[:], AX.X))
                link(V.tensor_scalar(red[:], red[:], 1e-20, None, ALU.add))
                link(V.reciprocal(red[:], red[:]))
                link(V.tensor_scalar(red[:], red[:], 2.5, None, ALU.mult))
                link(V.tensor_tensor(comb[:], pick[:], per_tok(red), ALU.mult))
            else:
                dve.wait_ge(logits, 1)
                link(V.tensor_tensor(score[:], lg[:, :, 0:E], bias_f, ALU.add))
                link(V.reduce_max(red[:], score[:], AX.X))
                V.tensor_tensor(tmp[:], score[:], per_tok(red), ALU.subtract).then_inc(act_in, 1)
                dve.wait_ge(act_out, 1)
                link(V.reduce_sum(red[:], score[:], AX.X))
                link(V.reciprocal(red[:], red[:]))
                link(V.tensor_tensor(score[:], score[:], per_tok(red), ALU.mult))
                ranks(score[:])
                ins = V.tensor_scalar(pick[:], rank[:], 2.0, None, ALU.is_lt)
                if kind == "capacity":
                    ins.then_inc(mask_ready, 1)
                    dve.wait_ge(mask_ready, 1)
                    dve.wait_ge(counted, 1)
                    flat = lambda a: a[:].rearrange("p t e -> p (t e)")
                    a, b = rank, rank2
                    link(V.memset(a[:, 0, :], 0.0))
                    link(V.tensor_copy(a[:, 1:NT, :], posp[:, 1, 0:NT * E].rearrange("p (t e) -> p t e", e=E)[:, 0:NT - 1, :]))
                    step = 1
                    while step < NT:
                        link(V.tensor_copy(b[:, 0:step, :], a[:, 0:step, :]))
                        link(V.tensor_tensor(b[:, step:NT, :], a[:, step:NT, :], a[:, 0:NT - step, :], ALU.add))
                        a, b = b, a
                        step *= 2
                    link(V.tensor_tensor(flat(a), posp[:, 0, 0:NT * E], flat(a), ALU.add))
                    link(V.tensor_scalar(a[:], a[:], float(CAP), None, ALU.is_lt))
                    ins = V.tensor_tensor(pick[:], pick[:], a[:], ALU.mult)
                link(ins)
                link(V.tensor_tensor(pick[:], pick[:], score[:], ALU.mult))
                link(V.reduce_sum(red[:], pick[:], AX.X))
                if kind == "capacity":
                    link(V.tensor_scalar(red[:], red[:], 1e-6, None, ALU.max))
                else:
                    link(V.tensor_scalar(red[:], red[:], 1e-8, None, ALU.add))
                link(V.reciprocal(red[:], red[:]))
                link(V.tensor_tensor(comb[:, :, 0:E], pick[:], per_tok(red), ALU.mult))
            link(V.tensor_copy(parts[:, :, 0, :], comb[:]))
            link(V.tensor_tensor(rest[:], comb[:], parts[:, :, 0, :], ALU.subtract))
            link(V.tensor_copy(parts[:, :, 1, :], rest[:]))
            link(V.tensor_tensor(rest[:], rest[:], parts[:, :, 1, :], ALU.subtract))
            V.tensor_copy(parts[:, :, 2, :], rest[:]).then_inc(parts_ready, 1)
            for n in range(NT // 8):
                dve.wait_ge(b_turned, n + 1)
                V.tensor_copy(cT[:, n * 8 * P:(n + 1) * 8 * P].rearrange("r (t p) -> r t p", p=P), trb[:, n % 2, :, :]).then_inc(b_copied, 1)


def experts_stage(nc, name, ident, kind, xnT_d, c_d, cT_d, weights, fT_d):
    silu = kind == "silu"
    E = 32 if silu else 8
    HT = 17 if silu else 32
    NSEL = 16 if silu else 8
    with Stage(nc, name) as st:
        xnT = st.sb("xnT", [P, TOK])
        cT = st.sb("cT", [96, TOK], BF16)
        cF = st.sb("cF", [32, TOK])
        sel = st.sb("sel", [96, NSEL * P], BF16)
        up_w = [st.sb(f"up_w{n}", [P, HT * P]) for n in range(2 if silu else 1)]
        down_w = st.sb("down_w", [P, HT, D])
        raw = st.sb("raw", [P, HT, P]) if silu else None
        b1r, b1 = st.sb("b1r", [32, P]), st.sb("b1", [P, 32])
        b2 = st.sb("b2", [8, D])
        a = st.sb("a", [P, 2, CH])
        g = st.sb("g", [P, 2, CH])
        h = st.sb("h", [P, 2, CH])
        out = st.sb("out", [P, 2, CH])
        up = [st.ps(f"up{n}", [P, 2, CH]) for n in range(2 if silu else 1)]
        rep = st.ps("rep", [P, 2, CH])
        acc = st.ps("acc", [P, CH])
        x_loaded, made, acted, tmp_ready, mixed, summed, copied = (
            st.sem(n) for n in ("x_loaded", "made", "acted", "tmp_ready", "mixed", "summed", "copied"))
        first_up, second_up, repeated, w_turned, w_copied, sel_made = (
            st.sem(n) for n in ("first_up", "second_up", "repeated", "w_turned", "w_copied", "sel_made"))
        consts = [st.sem(f"consts{n}") for n in range(3)]
        stored = [st.sem(f"stored{n}") for n in range(2)]
        block = st.block()
        XLOADS = 2 if silu else 3

        def iterations(eng, body):
            body(0, 0, True)
            body(1, 1, False)
            with eng.Fori(1, NCH // 2) as j:
                body(2 * j, 0, False)
                body(2 * j + 1, 1, False)

        @block.sync
        def _(sp):
            if silu:
                w_gate, w_up, w_down, sh_gate, sh_up, sh_down = weights
                for n, (src, sh) in enumerate(((w_gate, sh_gate), (w_up, sh_up), (w_down, sh_down))):
                    if n:
                        sp.wait_ge(w_copied, 5 * n)
                    if n < 2:
                        sp.dma_start(raw[:, 0:HT - 1, :], src.rearrange("(k e) i h -> (e i) k h", e=2)).then_inc(consts[n], DMA)
                    else:
                        sp.dma_start(raw[:, 0:HT - 1, :].rearrange("h k (e i) -> h (k e) i", e=2),
                                     src.rearrange("e h i -> h e i")).then_inc(consts[n], DMA)
                    sp.dma_start(raw[:, HT - 1, :], sh).then_inc(consts[n], DMA)
            else:
                w1, b1_d, w2, b2_d = weights
                sp.dma_start(b1r[:], b1_d.rearrange("e (k p) -> (e k) p", p=P)).then_inc(consts[0], DMA)
                sp.dma_start(up_w[0][:].rearrange("d (e f) -> d e f", e=E), w1.rearrange("e d f -> d e f")).then_inc(consts[1], DMA)
                sp.dma_start(b2[:], b2_d).then_inc(consts[1], DMA)
                sp.dma_start(down_w[:], w2.rearrange("e (k p) d -> p (e k) d", p=P)).then_inc(consts[2], DMA)
            sp.dma_start(xnT[:], xnT_d[:, :]).then_inc(x_loaded, DMA)
            sp.dma_start(cT[:], cT_d[:, :]).then_inc(x_loaded, DMA)
            if not silu:
                sp.dma_start(cF[:], c_d[:, :]).then_inc(x_loaded, DMA)

            def body(i, slot, first):
                sp.wait_ge(copied, i + 1)
                sp.dma_start(fT_d[:, bass.ds(i * CH, CH)], out[:, slot, :]).then_inc(stored[slot], DMA)
            iterations(sp, body)
            for s in range(2):
                sp.wait_ge(stored[s], DMA * NCH // 2)

        @block.gpsimd
        def _(pool):
            width = P // 2 if silu else P
            nc.gpsimd.memset(sel[:], 1.0).then_inc(made, 1)
            n = 1
            for part in range(3):
                own = sel[32 * part:32 * part + 32, :]
                for sign, base in ((1, 0), (-1, width - 1)):
                    pool.wait_ge(made, n)
                    nc.gpsimd.affine_select(out=own, in_=own, compare_op=ALU.is_ge, fill=0.0, base=base,
                                            pattern=[[sign, NSEL * P]], channel_multiplier=-sign * width).then_inc(made, 1)
                    n += 1

        @block.tensor
        def _(pe):
            if silu:
                n = 0
                for m in range(3):
                    pe.wait_ge(consts[m], 2 * DMA)
                    for t in range(HT):
                        if t % 4 == 0 and n >= 2:
                            pe.wait_ge(w_copied, n - 1)
                        last = nc.tensor.transpose(up[0][:, n % 2, t % 4 * P:(t % 4 + 1) * P], raw[:, t, :], ident[:])
                        if t % 4 == 3 or t == HT - 1:
                            last.then_inc(w_turned, 1)
                            n += 1
                pe.wait_ge(w_copied, n)
            else:
                pe.wait_ge(consts[0], DMA)
                nc.tensor.transpose(up[0][:, 0, 0:32], b1r[:], ident[0:32, 0:32]).then_inc(w_turned, 1)
                pe.wait_ge(w_copied, 1)
                pe.wait_ge(consts[1], 2 * DMA)
                pe.wait_ge(consts[2], DMA)
            pe.wait_ge(made, 7)
            pe.wait_ge(x_loaded, XLOADS * DMA)

            def down(i, slot, k):
                pe.wait_ge(mixed, i * HT + k + 1)
                if k == 0 and not (isinstance(i, int) and i == 0):
                    pe.wait_ge(copied, i)
                ins = nc.tensor.matmul(acc[:], down_w[:, k, :], h[:, (slot * HT + k) % 2, :],
                                       start=(k == 0), stop=(silu and k == HT - 1))
                return ins

            def body(i, slot, first):
                tok = bass.ds(i * CH, CH)
                for k in range(HT):
                    s = (slot * HT + k) % 2
                    n = i * HT + k
                    if not (first and k < 2):
                        pe.wait_ge(acted, n - 1)
                    nc.tensor.matmul(up[0][:, s, :], up_w[0][:, k * P:(k + 1) * P], xnT[:, tok],
                                     start=True, stop=True).then_inc(first_up, 1)
                    if silu:
                        if not (first and k < 2):
                            pe.wait_ge(mixed, n - 1)
                        ins = nc.tensor.matmul(up[1][:, s, :], up_w[1][:, k * P:(k + 1) * P], xnT[:, tok], start=True, stop=True)
                        if k < NSEL:
                            ins = nc.tensor.matmul(rep[:, s, :], sel[:, k * P:(k + 1) * P], cT[:, tok], start=True, stop=True)
                        ins.then_inc(second_up, 1)
                    elif k % 4 == 0:
                        e = k // 4
                        if not (first and e < 2):
                            pe.wait_ge(mixed, n - 4)
                        nc.tensor.matmul(rep[:, e % 2, :], sel[:, e * P:(e + 1) * P], cT[:, tok],
                                         start=True, stop=True).then_inc(second_up, 1)
                    if k:
                        down(i, slot, k - 1)
                ins = down(i, slot, HT - 1)
                if not silu:
                    ins = nc.tensor.matmul(acc[:], b2[:], cF[0:8, tok], start=False, stop=True)
                ins.then_inc(summed, 1)

            iterations(pe, body)

        @block.scalar
        def _(act):
            if silu:
                n = 0
                for m, dst in enumerate((up_w[0][:], up_w[1][:], down_w[:].rearrange("p k d -> p (k d)"))):
                    for t in range(0, HT, 4):
                        width = min(4, HT - t) * P
                        act.wait_ge(w_turned, n + 1)
                        nc.scalar.activation(dst[:, t * P:t * P + width], up[0][:, n % 2, 0:width], ACT.Copy).then_inc(w_copied, 1)
                        n += 1
            else:
                act.wait_ge(w_turned, 1)
                nc.scalar.activation(b1[:], up[0][:, 0, 0:32], ACT.Copy).then_inc(w_copied, 1)
                act.wait_ge(w_copied, 1)

            def body(i, slot, first):
                for k in range(HT):
                    s = (slot * HT + k) % 2
                    n = i * HT + k
                    act.wait_ge(first_up, n + 1)
                    if not (first and k < 2):
                        act.wait_ge(mixed, n - 1)
                    if silu:
                        ins = nc.scalar.activation(a[:, s, :], up[0][:, s, :], ACT.Silu)
                    else:
                        ins = nc.scalar.activation(a[:, s, :], up[0][:, s, :], ACT.Gelu, bias=b1[:, k:k + 1])
                    ins.then_inc(acted, 1)
                act.wait_ge(summed, i + 1)
                if not first and not (isinstance(i, int) and i < 2):
                    act.wait_ge(stored[slot], DMA * ((i - slot) // 2))
                nc.scalar.activation(out[:, slot, :], acc[:], ACT.Copy).then_inc(copied, 1)
            iterations(act, body)

        @block.vector
        def _(dve):
            def body(i, slot, first):
                for k in range(HT):
                    s = (slot * HT + k) % 2
                    n = i * HT + k
                    dve.wait_ge(acted, n + 1)
                    if silu:
                        dve.wait_ge(second_up, n + 1)
                        if k < NSEL:
                            nc.vector.tensor_tensor(g[:, s, :], up[1][:, s, :], a[:, s, :], ALU.mult).then_inc(tmp_ready, 1)
                            dve.wait_ge(tmp_ready, i * NSEL + k + 1)
                            ins = nc.vector.tensor_tensor(h[:, s, :], rep[:, s, :], g[:, s, :], ALU.mult)
                        else:
                            ins = nc.vector.tensor_tensor(h[:, s, :], up[1][:, s, :], a[:, s, :], ALU.mult)
                    else:
                        dve.wait_ge(second_up, i * NSEL + k // 4 + 1)
                        ins = nc.vector.tensor_tensor(h[:, s, :], rep[:, k // 4 % 2, :], a[:, s, :], ALU.mult)
                    ins.then_inc(mixed, 1)
            iterations(dve, body)


def column(vec):
    return vec.rearrange("(p a) -> p a", a=1)


def project_l1(nc, xnT_d, w_qkv, b_qkv, q_d, k_d, v_d):
    HEADS, HD, GROUP = 16, 8, 4
    Q_PARTS, K_PARTS = (0, 0, 1, 1, 0, 2), (0, 1, 0, 1, 2, 0)
    with Stage(nc, "proj1") as st:
        xnT = st.sb("xnT", [P, TOK])
        w, b_col, bv_b = st.sb("w", [P, 3 * D]), st.sb("b_col", [P, 2]), st.sb("bv_b", [P, D])
        full, rest = st.sb("full", [P, 2, CH]), st.sb("rest", [P, 2, CH])
        part = [st.sb(f"part{n}", [P, 2, TOK], BF16) for n in range(3)]
        v = st.sb("v", [P, NT, D])
        ps = st.ps("ps", [P, 4, CH])
        x_loaded, consts, made, full_ready, step, parts_ready, v_ready, stored = (
            st.sem(n) for n in ("x_loaded", "consts", "made", "full_ready", "step", "parts_ready", "v_ready", "stored"))
        block = st.block()

        @block.sync
        def _(sp):
            sp.dma_start(w[:], w_qkv).then_inc(consts, DMA)
            for j in range(2):
                sp.dma_start(b_col[:, j:j + 1], column(b_qkv[j * D:(j + 1) * D])).then_inc(consts, DMA)
            sp.dma_start(bv_b[:], broadcast_rows(b_qkv[2 * D:3 * D])).then_inc(consts, DMA)
            sp.dma_start(xnT[:], xnT_d[:, :]).then_inc(x_loaded, DMA)
            n = 0
            for j, (dst, order) in enumerate(((q_d, Q_PARTS), (k_d, K_PARTS))):
                sp.wait_ge(parts_ready, NCH * (j + 1))
                for blk, which in enumerate(order):
                    for h in range(HEADS):
                        sp.dma_start(dst[h, blk * HD:(blk + 1) * HD, :],
                                     part[which][h * HD:(h + 1) * HD, j, :]).then_inc(stored, DMA)
                        n += 1
            sp.wait_ge(v_ready, NCH)
            for g in range(HEADS // GROUP):
                sp.dma_start(v_d[g].rearrange("(t p) e -> p t e", p=P), v[:, :, g * GROUP * HD:(g + 1) * GROUP * HD]).then_inc(stored, DMA)
                n += 1
            sp.wait_ge(stored, DMA * n)

        @block.tensor
        def _(pe):
            pe.wait_ge(consts, 4 * DMA)
            pe.wait_ge(x_loaded, DMA)
            for n in range(3 * NCH):
                j, c = divmod(n, NCH)
                if n >= 4:
                    if (n - 4) // NCH < 2:
                        pe.wait_ge(full_ready, n - 3)
                    else:
                        pe.wait_ge(v_ready, n - 4 - 2 * NCH + 1)
                if j < 2:
                    last = nc.tensor.matmul(ps[:, n % 4, :], w[:, j * D:(j + 1) * D], xnT[:, c * CH:(c + 1) * CH],
                                            start=True, stop=True)
                else:
                    for t in range(TPC):
                        last = nc.tensor.matmul(ps[:, n % 4, t * P:(t + 1) * P], xnT[:, (c * TPC + t) * P:(c * TPC + t + 1) * P],
                                                w[:, 2 * D:3 * D], start=True, stop=True)
                last.then_inc(made, 1)

        @block.scalar
        def _(act):
            act.wait_ge(consts, 4 * DMA)
            for n in range(2 * NCH):
                act.wait_ge(made, n + 1)
                if n >= 2:
                    act.wait_ge(parts_ready, n - 1)
                nc.scalar.activation(full[:, n % 2, :], ps[:, n % 4, :], ACT.Identity,
                                     bias=b_col[:, n // NCH:n // NCH + 1]).then_inc(full_ready, 1)

        @block.vector
        def _(dve):
            link = Chain(dve, step)
            V = nc.vector
            dve.wait_ge(consts, 4 * DMA)
            for n in range(2 * NCH):
                j, c = divmod(n, NCH)
                cols = slice(c * CH, (c + 1) * CH)
                x, r = full[:, n % 2, :], rest[:, n % 2, :]
                dve.wait_ge(full_ready, n + 1)
                link(V.tensor_copy(part[0][:, j, cols], x))
                link(V.tensor_tensor(r, x, part[0][:, j, cols], ALU.subtract))
                link(V.tensor_copy(part[1][:, j, cols], r))
                V.tensor_tensor(part[2][:, j, cols], r, part[1][:, j, cols], ALU.subtract).then_inc(parts_ready, 1)
            for c in range(NCH):
                n = 2 * NCH + c
                dve.wait_ge(made, n + 1)
                V.tensor_tensor(v[:, c * TPC:(c + 1) * TPC, :], ps[:, n % 4, :].rearrange("p (t e) -> p t e", t=TPC),
                                bv_b[:].unsqueeze(1).to_broadcast([P, TPC, D]), ALU.add).then_inc(v_ready, 1)


def ssm_stage(nc, ident, xnT_d, A_r, A_i, B_r, B_i, C_r, C_i, skip, s_d):
    LOG = SEQ.bit_length() - 1
    with Stage(nc, "ssm") as st:
        u = st.sb("u", [P, BATCH, SEQ])
        par = st.sb("par", [P, 7])
        Er, Ei, Wr, Wi, decay, tmp, tmp2 = (st.sb(n, [P, SEQ]) for n in ("Er", "Ei", "Wr", "Wi", "decay", "tmp", "tmp2"))
        vr, vi, gr, gi = (st.sb(n, [P, SEQ]) for n in ("vr", "vi", "gr", "gi"))
        y = st.sb("y", [P, 2, SEQ])
        cols = st.sb("cols", [P, 16])
        s = st.sb("s", [P, 2, SEQ // P, D])
        tp = st.ps("tp", [P, 2, SEQ // P, D])
        loaded, consts, step, squared, rooted, y_ready, turned, copied = (
            st.sem(n) for n in ("loaded", "consts", "step", "squared", "rooted", "y_ready", "turned", "copied"))
        stored = [st.sem(f"stored{n}") for n in range(2)]
        block = st.block()

        @block.sync
        def _(sp):
            for n, vec in enumerate((A_r, A_i, B_r, B_i, C_r, C_i, skip)):
                sp.dma_start(par[:, n:n + 1], column(vec)).then_inc(consts, DMA)
            sp.dma_start(u[:], xnT_d.rearrange("d (b t) -> d b t", b=BATCH)).then_inc(loaded, DMA)
            for b in range(BATCH):
                sp.wait_ge(copied, b + 1)
                sp.dma_start(rows(s_d)[:, b * SEQ // P:(b + 1) * SEQ // P, :], s[:, b % 2, :, :]).then_inc(stored[b % 2], DMA)
            for n in range(2):
                sp.wait_ge(stored[n], DMA * BATCH // 2)

        @block.vector
        def _(dve):
            link = Chain(dve, step)
            V = nc.vector
            col = lambda n: cols[:, n:n + 1]
            ar, ai, br, bi, cr, ci, dd = (par[:, n:n + 1] for n in range(7))
            r2, none, inv, c, sn, t, t2, r, wr, wi, nsn, nwi, t3 = (col(n) for n in range(13))
            mul = lambda o, a, b: link(V.tensor_tensor(o, a, b, ALU.mult))
            add = lambda o, a, b: link(V.tensor_tensor(o, a, b, ALU.add))
            sub = lambda o, a, b: link(V.tensor_tensor(o, a, b, ALU.subtract))
            affine = lambda o, a, m, k: link(V.tensor_scalar(o, a, m, k, ALU.mult, ALU.add))

            def to_unit():
                mul(t, c, c)
                mul(t2, sn, sn)
                add(t, t, t2)
                affine(t, t, -0.5, 1.5)
                mul(c, c, t)
                mul(sn, sn, t)

            dve.wait_ge(consts, 7 * DMA)
            mul(t, ar, ar)
            mul(t2, ai, ai)
            add(r2, t, t2)
            link(V.tensor_scalar(none, r2, 1e-34, None, ALU.is_lt))
            V.tensor_scalar(r2, r2, 1e-34, None, ALU.max).then_inc(squared, 1)
            dve.wait_ge(rooted, 1)
            link(V.reciprocal(inv, t3))
            mul(c, ar, inv)
            mul(sn, ai, inv)
            affine(t, none, -1.0, 1.0)
            mul(c, c, t)
            mul(sn, sn, t)
            add(c, c, none)
            to_unit()
            to_unit()
            mul(t, ar, c)
            mul(t2, ai, sn)
            add(r, t, t2)
            mul(t, cr, br)
            mul(t2, ci, bi)
            sub(wr, t, t2)
            mul(t, cr, bi)
            mul(t2, ci, br)
            add(wi, t, t2)
            affine(nwi, wi, -1.0, 0.0)
            link(V.memset(decay[:], 1.0))
            link(V.tensor_scalar(decay[:], decay[:], r, None, ALU.mult))
            link(V.memset(Er[:, 0:1], 1.0))
            link(V.memset(Ei[:, 0:1], 0.0))
            for k in range(LOG):
                n = 1 << k
                affine(nsn, sn, -1.0, 0.0)
                link(V.tensor_scalar(tmp[:, 0:n], Er[:, 0:n], c, None, ALU.mult))
                link(V.tensor_scalar(tmp2[:, 0:n], Ei[:, 0:n], c, None, ALU.mult))
                link(V.scalar_tensor_tensor(out=Er[:, n:2 * n], in0=Ei[:, 0:n], scalar=nsn, in1=tmp[:, 0:n],
                                            op0=ALU.mult, op1=ALU.add))
                link(V.scalar_tensor_tensor(out=Ei[:, n:2 * n], in0=Er[:, 0:n], scalar=sn, in1=tmp2[:, 0:n],
                                            op0=ALU.mult, op1=ALU.add))
                mul(t, c, c)
                mul(t2, sn, sn)
                mul(t3, c, sn)
                sub(c, t, t2)
                affine(sn, t3, 2.0, 0.0)
                to_unit()
            link(V.tensor_scalar(tmp[:], Er[:], wr, None, ALU.mult))
            link(V.scalar_tensor_tensor(out=Wr[:], in0=Ei[:], scalar=nwi, in1=tmp[:], op0=ALU.mult, op1=ALU.add))
            link(V.tensor_scalar(tmp[:], Ei[:], wr, None, ALU.mult))
            link(V.scalar_tensor_tensor(out=Wi[:], in0=Er[:], scalar=wi, in1=tmp[:], op0=ALU.mult, op1=ALU.add))
            dve.wait_ge(loaded, DMA)
            for b in range(BATCH):
                link(V.tensor_tensor(vr[:], Er[:], u[:, b, :], ALU.mult))
                link(V.tensor_tensor(vi[:], Ei[:], u[:, b, :], ALU.mult))
                link(V.tensor_tensor_scan(gr[:], decay[:], vr[:], 0.0, ALU.mult, ALU.add))
                link(V.tensor_tensor_scan(gi[:], decay[:], vi[:], 0.0, ALU.mult, ALU.add))
                link(V.tensor_tensor(gr[:], gr[:], Wr[:], ALU.mult))
                link(V.tensor_tensor(gi[:], gi[:], Wi[:], ALU.mult))
                link(V.tensor_tensor(gr[:], gr[:], gi[:], ALU.add))
                if b >= 2:
                    dve.wait_ge(turned, b - 1)
                V.scalar_tensor_tensor(out=y[:, b % 2, :], in0=u[:, b, :], scalar=dd, in1=gr[:], op0=ALU.mult,
                                       op1=ALU.add).then_inc(y_ready, 1)

        @block.scalar
        def _(act):
            act.wait_ge(squared, 1)
            nc.scalar.activation(cols[:, 12:13], cols[:, 0:1], ACT.Sqrt).then_inc(rooted, 1)
            for b in range(BATCH):
                act.wait_ge(turned, b + 1)
                if b >= 2:
                    act.wait_ge(stored[b % 2], DMA)
                nc.scalar.activation(s[:, b % 2, :, :], tp[:, b % 2, :, :], ACT.Copy).then_inc(copied, 1)

        @block.tensor
        def _(pe):
            for b in range(BATCH):
                pe.wait_ge(y_ready, b + 1)
                if b >= 2:
                    pe.wait_ge(copied, b - 1)
                for t in range(SEQ // P):
                    last = nc.tensor.transpose(tp[:, b % 2, t, :], y[:, b % 2, t * P:(t + 1) * P], ident[:])
                last.then_inc(turned, 1)


def linear_attention_stage(nc, ident, xnT_d, Wq, bq, Wk, bk, Wv, bv, Wg, bg, Wo, bo, s_d):
    DH = 256
    HALF = DH // P
    NCHUNK = SEQ // P
    PIECES = 10
    with Stage(nc, "linattn") as st:
        xc = st.sb("xc", [P, BATCH, P])
        wq, wk, wg, wo = st.sb("wq", [P, DH]), st.sb("wk", [P, DH]), st.sb("wg", [P, DH]), st.sb("wo", [P, HALF, D])
        wkv = st.sb("wkv", [P, 2 * DH])
        b_col = st.sb("b_col", [P, 2, HALF])
        bkv, bgr, bor = st.sb("bkv", [1, 2 * DH]), st.sb("bgr", [1, DH]), st.sb("bor", [1, D])
        ones = st.sb("ones", [1, P])
        mask = st.sb("mask", [P, BATCH, P])
        qkT = st.sb("qkT", [P, 2, HALF, BATCH * P])
        kv = st.sb("kv", [P, BATCH, 2 * DH])
        gate = st.sb("gate", [P, BATCH, DH])
        sc, prob, probT = (st.sb(n, [P, BATCH, P]) for n in ("sc", "prob", "probT"))
        nmax, total = st.sb("nmax", [P, BATCH]), st.sb("total", [P, BATCH])
        state = st.sb("state", [P, BATCH, HALF, DH])
        mixed = st.sb("mixed", [P, BATCH, DH])
        mixedT = st.sb("mixedT", [P, HALF, BATCH * P])
        y = st.sb("y", [P, BATCH, D])
        piece = st.ps("piece", [P, 2, CH])
        pscore = st.ps("pscore", [P, BATCH, P])
        pturn = st.ps("pturn", [P, BATCH, P])
        pout = st.ps("pout", [P, BATCH, DH])
        pmix = st.ps("pmix", [P, HALF, BATCH * P])
        names = ("consts", "made", "x_loaded", "projected", "pieced", "scored", "shifted", "exped", "step", "p_ready", "p_turned",
                 "p_copied", "crossed", "gated", "summed", "added", "m_turned", "m_copied", "out_ready", "out_copied", "stored")
        (consts, made, x_loaded, projected, pieced, scored, shifted, exped, step, p_ready, p_turned, p_copied, crossed, gated, summed,
         added, m_turned, m_copied, out_ready, out_copied, stored) = (st.sem(n) for n in names)
        sig_done = st.sem("sig_done")
        block = st.block()
        NCONST = 14

        @block.sync
        def _(sp):
            for dst, src in ((wq[:], Wq), (wkv[:, 0:DH], Wk), (wkv[:, DH:2 * DH], Wv), (wg[:], Wg), (wk[:], Wk),
                             (wo[:], Wo.rearrange("(h p) d -> p h d", p=P)),
                             *((b_col[:, j, h:h + 1], column(v[h * P:(h + 1) * P])) for j, v in enumerate((bq, bk)) for h in range(HALF)),
                             (bkv[:, 0:DH], bk.rearrange("(a n) -> a n", a=1)), (bkv[:, DH:2 * DH], bv.rearrange("(a n) -> a n", a=1)),
                             (bgr[:], bg.rearrange("(a n) -> a n", a=1)), (bor[:], bo.rearrange("(a n) -> a n", a=1))):
                sp.dma_start(dst, src).then_inc(consts, DMA)

            def load(n):
                sp.dma_start(xc[:], xnT_d.rearrange("d (b t) -> d b t", b=BATCH)[:, :, bass.ds(n * P, P)]).then_inc(x_loaded, DMA)

            def store(n):
                sp.wait_ge(out_copied, n + 1)
                sp.dma_start(s_d.rearrange("(b t) d -> t b d", b=BATCH)[bass.ds(n * P, P), :, :], y[:]).then_inc(stored, DMA)

            load(0)
            with sp.Fori(0, NCHUNK - 1) as n:
                sp.wait_ge(projected, PIECES * n + PIECES)
                load(n + 1)
                store(n)
            store(NCHUNK - 1)
            sp.wait_ge(stored, DMA * NCHUNK)

        @block.gpsimd
        def _(pool):
            nc.gpsimd.memset(ones[:], 1.0).then_inc(made, 1)
            nc.gpsimd.memset(state[:], 0.0).then_inc(made, 1)
            nc.gpsimd.memset(mask[:], 0.0).then_inc(made, 1)
            pool.wait_ge(made, 3)
            nc.gpsimd.affine_select(out=mask[:], in_=mask[:], compare_op=ALU.is_ge, fill=-1e30, base=0,
                                    pattern=[[0, BATCH], [-1, P]], channel_multiplier=1).then_inc(made, 1)

        @block.tensor
        def _(pe):
            mm = nc.tensor.matmul
            pe.wait_ge(consts, NCONST * DMA)
            pe.wait_ge(made, 4)
            with pe.Fori(0, NCHUNK) as n:
                pe.wait_ge(x_loaded, DMA * n + DMA)
                xall = xc[:].rearrange("d b t -> d (b t)")
                for p in range(PIECES):
                    if p >= 2:
                        pe.wait_ge(pieced, PIECES * n + p - 1)
                    elif p == 0:
                        pe.wait_ge(added, BATCH * n)
                        pe.wait_ge(pieced, PIECES * n)
                    bank = piece[:, p % 2, :]
                    if p < 4:
                        w = (wq, wk)[p // 2]
                        last = mm(bank, w[:, p % 2 * P:(p % 2 + 1) * P], xall, start=True, stop=True)
                    elif p < 8:
                        mm(bank, xc[:, p - 4, :], wkv[:], start=True, stop=False)
                        last = mm(bank, ones[:], bkv[:], start=False, stop=True)
                    else:
                        for j in range(2):
                            part = bank[:, j * DH:(j + 1) * DH]
                            mm(part, xc[:, 2 * (p - 8) + j, :], wg[:], start=True, stop=False)
                            last = mm(part, ones[:], bgr[:], start=False, stop=True)
                    last.then_inc(projected, 1)
                for b in range(BATCH):
                    own = slice(b * P, (b + 1) * P)
                    for h in range(HALF):
                        last = mm(pscore[:, b, :], qkT[:, 0, h, own], qkT[:, 1, h, own], start=(h == 0), stop=(h == HALF - 1))
                last.then_inc(scored, 1)
                pe.wait_ge(p_ready, n + 1)
                pe.wait_ge(out_copied, n)
                for b in range(BATCH):
                    last = nc.tensor.transpose(pturn[:, b, :], prob[:, b, :], ident[:])
                last.then_inc(p_turned, 1)
                pe.wait_ge(p_copied, n + 1)
                pe.wait_ge(added, BATCH * n)
                for b in range(BATCH):
                    own = slice(b * P, (b + 1) * P)
                    mm(pout[:, b, :], probT[:, b, :], kv[:, b, DH:2 * DH], start=True, stop=False)
                    for h in range(HALF):
                        last = mm(pout[:, b, :], qkT[:, 0, h, own], state[:, b, h, :], start=False, stop=(h == HALF - 1))
                last.then_inc(crossed, 1)
                for b in range(BATCH):
                    if b >= 2:
                        pe.wait_ge(added, BATCH * n + b - 1)
                    else:
                        pe.wait_ge(pieced, PIECES * n + PIECES)
                    for h in range(HALF):
                        last = mm(piece[:, b % 2, h * DH:(h + 1) * DH], kv[:, b, h * P:(h + 1) * P], kv[:, b, DH:2 * DH],
                                  start=True, stop=True)
                    last.then_inc(summed, 1)
                pe.wait_ge(gated, n + 1)
                for h in range(HALF):
                    for b in range(BATCH):
                        last = nc.tensor.transpose(pmix[:, h, b * P:(b + 1) * P], mixed[:, b, h * P:(h + 1) * P], ident[:])
                last.then_inc(m_turned, 1)
                pe.wait_ge(m_copied, n + 1)
                for b in range(BATCH):
                    for h in range(HALF):
                        mm(pturn[:, b, :], mixedT[:, h, b * P:(b + 1) * P], wo[:, h, :], start=(h == 0), stop=False)
                    last = mm(pturn[:, b, :], ones[:], bor[:], start=False, stop=True)
                last.then_inc(out_ready, 1)

        @block.scalar
        def _(act):
            act.wait_ge(consts, NCONST * DMA)
            with act.Fori(0, NCHUNK) as n:
                for p in range(4):
                    act.wait_ge(projected, PIECES * n + p + 1)
                    if p == 0:
                        act.wait_ge(crossed, n)
                    nc.scalar.activation(qkT[:, p // 2, p % 2, :], piece[:, p % 2, :], ACT.Identity,
                                         bias=b_col[:, p // 2, p % 2:p % 2 + 1]).then_inc(pieced, 1)
                for p in range(8, PIECES):
                    act.wait_ge(projected, PIECES * n + p + 1)
                    act.wait_ge(pieced, PIECES * n + p)
                    if p == 8:
                        act.wait_ge(gated, n)
                    nc.scalar.activation(gate[:, 2 * (p - 8):2 * (p - 8) + 2, :], piece[:, p % 2, :].rearrange("t (b e) -> t b e", b=2),
                                         ACT.Sigmoid).then_inc(pieced, 1)
                act.wait_ge(shifted, n + 1)
                nc.scalar.activation(prob[:], sc[:], ACT.Exp).then_inc(exped, 1)
                act.wait_ge(m_turned, n + 1)
                nc.scalar.activation(mixedT[:], pmix[:], ACT.Copy).then_inc(m_copied, 1)
                act.wait_ge(out_ready, n + 1)
                act.wait_ge(stored, DMA * n)
                nc.scalar.activation(y[:], pturn[:], ACT.Copy).then_inc(out_copied, 1)

        @block.vector
        def _(dve):
            V = nc.vector
            wide = [P, BATCH, P]
            dve.wait_ge(made, 4)
            with dve.Fori(0, NCHUNK) as n:
                link = Chain(dve, step)
                STEPS = 4
                for b in range(BATCH):
                    dve.wait_ge(projected, PIECES * n + 4 + b + 1)
                    dve.wait_ge(pieced, PIECES * n + 4 + b)
                    if b == 0:
                        dve.wait_ge(summed, BATCH * n)
                    V.tensor_copy(kv[:, b, :], piece[:, b % 2, :]).then_inc(pieced, 1)
                dve.wait_ge(scored, n + 1)
                link(V.scalar_tensor_tensor(out=sc[:], in0=pscore[:], scalar=DH ** -0.5, in1=mask[:], op0=ALU.mult, op1=ALU.add),
                     STEPS * n)
                link(V.tensor_reduce(nmax[:], sc[:], AX.X, ALU.max, negate=True), STEPS * n)
                V.tensor_tensor(sc[:], sc[:], over(nmax[:].unsqueeze(2), wide), ALU.add).then_inc(shifted, 1)
                dve.wait_ge(exped, n + 1)
                link(V.reduce_sum(total[:], prob[:], AX.X), STEPS * n)
                link(V.reciprocal(total[:], total[:]), STEPS * n)
                V.tensor_tensor(prob[:], prob[:], over(total[:].unsqueeze(2), wide), ALU.mult).then_inc(p_ready, 1)
                dve.wait_ge(p_turned, n + 1)
                V.tensor_copy(probT[:], pturn[:]).then_inc(p_copied, 1)
                dve.wait_ge(crossed, n + 1)
                dve.wait_ge(pieced, PIECES * n + PIECES)
                V.tensor_tensor(mixed[:], pout[:], gate[:], ALU.mult).then_inc(gated, 1)
                for b in range(BATCH):
                    dve.wait_ge(summed, BATCH * n + b + 1)
                    V.tensor_tensor(state[:, b, :, :], piece[:, b % 2, :].rearrange("p (h e) -> p h e", h=HALF), state[:, b, :, :],
                                    ALU.add).then_inc(added, 1)


def shared_ffn_stage(nc, ident, xnT_d, sw1, sb1, sw2, sb2, sw3, sb3, ln_g, ln_b, f_d):
    H = 64
    wide = [P, TPC, H]
    with Stage(nc, "shared") as st:
        xc = st.sb("xc", [P, 2, CH])
        raw12, raw3 = st.sb("raw12", [P, D]), st.sb("raw3", [P, H])
        w12, w3 = st.sb("w12", [P, 2 * H]), st.sb("w3", [H + 1, D])
        b12, ones = st.sb("b12", [1, 2 * H]), st.sb("ones", [1, P])
        gamma, beta = st.sb("gamma", [P, H]), st.sb("beta", [P, H])
        a, z, sq = (st.sb(n, wide) for n in ("a", "z", "sq"))
        total, var, std = (st.sb(n, [P, TPC]) for n in ("total", "var", "std"))
        zT = st.sb("zT", [H + 1, CH])
        y = st.sb("y", [P, 2, TPC, D])
        wt = st.ps("wt", [P, 2, P])
        hid = st.ps("hid", [P, 2, TPC, 2 * H])
        zt = st.ps("zt", [P, CH])
        out = st.ps("out", [P, 2, TPC, D])
        names = ("consts", "made", "w_turned", "w_copied", "projected", "silu_done", "step", "var_ready", "std_ready", "z_ready",
                 "z_turned", "z_copied", "out_ready", "out_copied")
        (consts, made, w_turned, w_copied, projected, silu_done, step, var_ready, std_ready, z_ready, z_turned, z_copied, out_ready,
         out_copied) = (st.sem(n) for n in names)
        x_loaded, stored = ([st.sem(f"{n}{s}") for s in range(2)] for n in ("x_loaded", "stored"))
        block = st.block()
        NCONST = 8

        def iterations(eng, body):
            body(0, 0, True)
            body(1, 1, True)
            with eng.Fori(1, NCH // 2) as j:
                body(2 * j, 0, False)
                body(2 * j + 1, 1, False)

        @block.sync
        def _(sp):
            sp.wait_ge(made, 2)
            for dst, src in ((raw12[0:H, :], sw1), (raw12[H:2 * H, :], sw2), (raw3[:], sw3), (w3[H:H + 1, :], sb3.rearrange("(a n) -> a n", a=1)),
                             (b12[:, 0:H], sb1.rearrange("(a n) -> a n", a=1)), (b12[:, H:2 * H], sb2.rearrange("(a n) -> a n", a=1)),
                             (gamma[:], broadcast_rows(ln_g)), (beta[:], broadcast_rows(ln_b))):
                sp.dma_start(dst, src).then_inc(consts, DMA)

            def body(i, slot, first):
                if not first:
                    sp.wait_ge(projected, i - 1)
                sp.dma_start(xc[:, slot, :], xnT_d[:, bass.ds(i * CH, CH)]).then_inc(x_loaded[slot], DMA)
            iterations(sp, body)
            for s in range(2):
                sp.wait_ge(stored[s], DMA * NCH // 2)

        @block.gpsimd
        def _(pool):
            nc.gpsimd.memset(ones[:], 1.0).then_inc(made, 1)
            nc.gpsimd.memset(zT[H:H + 1, :], 1.0).then_inc(made, 1)

            def body(i, slot, first):
                pool.wait_ge(out_copied, i + 1)
                pool.dma_start(rows(f_d)[:, bass.ds(i * TPC, TPC), :], y[:, slot, :, :]).then_inc(stored[slot], DMA)
            iterations(pool, body)

        @block.tensor
        def _(pe):
            mm = nc.tensor.matmul
            pe.wait_ge(consts, NCONST * DMA)
            nc.tensor.transpose(wt[:, 0, :], raw12[:], ident[:]).then_inc(w_turned, 1)
            nc.tensor.transpose(wt[0:H, 1, :], raw3[:], ident[:]).then_inc(w_turned, 1)
            pe.wait_ge(w_copied, 2)

            def up(i, slot, first):
                pe.wait_ge(x_loaded[slot], DMA * ((i - slot) // 2 + 1))
                if not first:
                    pe.wait_ge(z_ready, i - 1)
                for t in range(TPC):
                    mm(hid[:, slot, t, :], xc[:, slot, t * P:(t + 1) * P], w12[:], start=True, stop=False)
                    last = mm(hid[:, slot, t, :], ones[:], b12[:], start=False, stop=True)
                last.then_inc(projected, 1)

            def body(i, slot, first):
                up(i, slot, first)
                pe.wait_ge(z_ready, i + 1)
                nc.tensor.transpose(zt[:, 0:P], z[:, 0:2, :].rearrange("p t h -> p (t h)"), ident[:])
                for t in range(1, TPC):
                    last = nc.tensor.transpose(zt[0:H, t * P:(t + 1) * P], z[:, t, :], ident[:])
                last.then_inc(z_turned, 1)
                pe.wait_ge(z_copied, i + 1)
                if not first:
                    pe.wait_ge(out_copied, i - 1)
                for t in range(TPC):
                    last = mm(out[:, slot, t, :], zT[:, t * P:(t + 1) * P], w3[:], start=True, stop=True)
                last.then_inc(out_ready, 1)
            iterations(pe, body)

        @block.scalar
        def _(act):
            act.wait_ge(w_turned, 2)
            nc.scalar.activation(w12[:], wt[:, 0, :], ACT.Copy).then_inc(w_copied, 1)
            nc.scalar.activation(w3[0:H, :], wt[0:H, 1, :], ACT.Copy).then_inc(w_copied, 1)

            def body(i, slot, first):
                act.wait_ge(projected, i + 1)
                if not (first and slot == 0):
                    act.wait_ge(z_ready, i)
                nc.scalar.activation(a[:], hid[:, slot, :, 0:H], ACT.Silu).then_inc(silu_done, 1)
                act.wait_ge(var_ready, i + 1)
                nc.scalar.activation(std[:], var[:], ACT.Sqrt).then_inc(std_ready, 1)
                act.wait_ge(z_turned, i + 1)
                nc.scalar.activation(zT[0:H, :], zt[0:H, :], ACT.Copy).then_inc(z_copied, 1)
                act.wait_ge(out_ready, i + 1)
                if not first:
                    act.wait_ge(stored[slot], DMA * ((i - slot) // 2))
                nc.scalar.activation(y[:, slot, :, :], out[:, slot, :, :], ACT.Copy).then_inc(out_copied, 1)
            iterations(act, body)

        @block.vector
        def _(dve):
            V = nc.vector
            dve.wait_ge(consts, NCONST * DMA)

            def body(i, slot, first):
                STEPS = 9
                link = Chain(dve, step)
                run = lambda ins: link(ins, STEPS * i)
                dve.wait_ge(silu_done, i + 1)
                if not (first and slot == 0):
                    dve.wait_ge(z_turned, i)
                run(V.tensor_tensor(z[:], hid[:, slot, :, H:2 * H], a[:], ALU.mult))
                run(V.reduce_sum(total[:], z[:], AX.X))
                run(V.tensor_scalar(total[:], total[:], -1.0 / H, None, ALU.mult))
                run(V.tensor_tensor(z[:], z[:], over(total[:].unsqueeze(2), wide), ALU.add))
                run(V.tensor_tensor(sq[:], z[:], z[:], ALU.mult))
                run(V.reduce_sum(var[:], sq[:], AX.X))
                V.tensor_scalar(var[:], var[:], 1.0 / H, 1e-5, ALU.mult, ALU.add).then_inc(var_ready, 1)
                dve.wait_ge(std_ready, i + 1)
                run(V.reciprocal(total[:], std[:]))
                run(V.tensor_tensor(z[:], z[:], over(total[:].unsqueeze(2), wide), ALU.mult))
                run(V.tensor_tensor(z[:], z[:], gamma[:].unsqueeze(1).to_broadcast(wide), ALU.mult))
                V.tensor_tensor(z[:], z[:], beta[:].unsqueeze(1).to_broadcast(wide), ALU.add).then_inc(z_ready, 1)
            iterations(dve, body)


def routed_ffn_stage(nc, ident, xn_d, f_d, index_b, index_t, sg_w, sg_b, eg_w, eg_b, exp_bias, ew1, eb1, ew2, eb2, ew3, eb3,
                     ln_g, ln_b):
    M = index_b.shape[0] // P
    E, H = 8, 64
    F = E * H
    FT = F // P
    with Stage(nc, "routed") as st:
        ib, it = st.sb("ib", [P, M], I32), st.sb("it", [P, M], I32)
        fb, ft, neg = (st.sb(n, [P, M]) for n in ("fb", "ft", "neg"))
        row = st.sb("row", [P, M], I32)
        x, old, new = (st.sb(n, [P, M, D]) for n in ("x", "old", "new"))
        xT = st.sb("xT", [P, M, P])
        raw = st.sb("raw", [P, 3, FT, P])
        w = st.sb("w", [P, 2, F])
        w3 = st.sb("w3", [P, FT, D])
        gr, gw, gbias = st.sb("gr", [E + 1, D]), st.sb("gw", [P, E + 1]), st.sb("gbias", [1, E + 1])
        xbias = st.sb("xbias", [P, E])
        b12, b3, ones = st.sb("b12", [1, 2, F]), st.sb("b3", [E, D]), st.sb("ones", [1, P])
        before = st.sb("before", [P, E, E])
        gamma, beta = st.sb("gamma", [P, H]), st.sb("beta", [P, H])
        sc = st.sb("sc", [P, M, E + 1])
        pick, hot, tmp = (st.sb(n, [P, M, E]) for n in ("pick", "hot", "tmp"))
        pair, pair2 = st.sb("pair", [P, M, E, E]), st.sb("pair2", [P, M, E, E])
        two = st.sb("two", [P, M, 2])
        red = st.sb("red", [P, M])
        a, z, sq = (st.sb(n, [P, M, E, H]) for n in ("a", "z", "sq"))
        total, var, std = (st.sb(n, [P, M, E]) for n in ("total", "var", "std"))
        zT, hotT = st.sb("zT", [P, M, FT, P]), st.sb("hotT", [E, M, P])
        turn = st.ps("turn", [P, 2, CH])
        score = st.ps("score", [P, M, E + 1])
        hid = st.ps("hid", [P, M, 2, F])
        out = st.ps("out", [P, M, D])
        names = ("consts", "made", "idx_loaded", "row_ready", "gathered", "turned", "copied", "scored", "sig_done", "step", "two_ready",
                 "two_done", "projected", "silu_done", "var_ready", "std_ready", "z_ready", "out_ready", "old_loaded", "new_ready", "stored")
        (consts, made, idx_loaded, row_ready, gathered, turned, copied, scored, sig_done, step, two_ready, two_done, projected,
         silu_done, var_ready, std_ready, z_ready, out_ready, old_loaded, new_ready, stored) = (st.sem(n) for n in names)
        block = st.block()
        NCONST = 13
        WTURNS = 3 + 1
        one = lambda v: v.rearrange("(a n) -> a n", a=1)

        @block.sync
        def _(sp):
            for m in range(M):
                for dst, src in ((ib, index_b), (it, index_t)):
                    sp.dma_start(dst[:, m:m + 1], column(src[m * P:(m + 1) * P])).then_inc(idx_loaded, DMA)
            for dst, src in ((raw[:, 0, :, :], ew1.rearrange("(k e) h d -> (e h) k d", e=2)),
                             (raw[:, 1, :, :], ew2.rearrange("(k e) h d -> (e h) k d", e=2)),
                             (raw[:, 2, :, :].rearrange("d k (e h) -> d (k e) h", e=2), ew3.rearrange("e d h -> d e h")),
                             (gr[0:E, :], eg_w), (gr[E:E + 1, :], sg_w), (gbias[:, 0:E], one(eg_b)), (gbias[:, E:E + 1], one(sg_b)),
                             (xbias[:], broadcast_rows(exp_bias)), (b12[:, 0, :], one(eb1.rearrange("e h -> (e h)"))),
                             (b12[:, 1, :], one(eb2.rearrange("e h -> (e h)"))), (b3[:], eb3),
                             (gamma[:], broadcast_rows(ln_g)), (beta[:], broadcast_rows(ln_b))):
                sp.dma_start(dst, src).then_inc(consts, DMA)

        @block.gpsimd
        def _(pool):
            nc.gpsimd.memset(ones[:], 1.0).then_inc(made, 1)
            nc.gpsimd.memset(before[:], 1.0).then_inc(made, 1)
            pool.wait_ge(made, 2)
            nc.gpsimd.affine_select(out=before[:], in_=before[:], compare_op=ALU.is_ge, fill=0.0, base=-1,
                                    pattern=[[1, E], [-1, E]], channel_multiplier=0).then_inc(made, 1)
            pool.wait_ge(row_ready, 1)
            at = lambda m: bass.IndirectOffsetOnAxis(ap=row[:, m:m + 1].bitcast(U32), axis=0)
            for m in range(M):
                pool.indirect_dma_start(out=x[:, m, :], out_offset=None, in_=xn_d[:, :], in_offset=at(m)).then_inc(gathered, DMA)
                pool.indirect_dma_start(out=old[:, m, :], out_offset=None, in_=f_d[:, :], in_offset=at(m)).then_inc(old_loaded, DMA)
            pool.wait_ge(new_ready, 1)
            for m in range(M):
                pool.indirect_dma_start(out=f_d[:, :], out_offset=at(m), in_=new[:, m, :], in_offset=None).then_inc(stored, DMA)
            pool.wait_ge(stored, DMA * M)

        @block.tensor
        def _(pe):
            mm = nc.tensor.matmul
            T = nc.tensor.transpose
            pe.wait_ge(consts, NCONST * DMA)
            for j in range(3):
                if j == 2:
                    pe.wait_ge(copied, 1)
                for k in range(FT):
                    last = T(turn[:, j % 2, k * P:(k + 1) * P], raw[:, j, k, :], ident[:])
                last.then_inc(turned, 1)
            pe.wait_ge(copied, 2)
            T(turn[:, 1, 0:E + 1], gr[:], ident[0:E + 1, 0:E + 1]).then_inc(turned, 1)
            pe.wait_ge(gathered, DMA * M)
            pe.wait_ge(copied, 3)
            for m in range(M):
                last = T(turn[:, 0, m * P:(m + 1) * P], x[:, m, :], ident[:])
            last.then_inc(turned, 1)
            pe.wait_ge(copied, 5)
            pe.wait_ge(made, 3)
            for m in range(M):
                mm(score[:, m, :], xT[:, m, :], gw[:], start=True, stop=False)
                last = mm(score[:, m, :], ones[:], gbias[:], start=False, stop=True)
            last.then_inc(scored, 1)
            for m in range(M):
                for j in range(2):
                    mm(hid[:, m, j, :], xT[:, m, :], w[:, j, :], start=True, stop=False)
                    last = mm(hid[:, m, j, :], ones[:], b12[:, j, :], start=False, stop=True)
            last.then_inc(projected, 1)
            pe.wait_ge(z_ready, 1)
            for m in range(M):
                for k in range(FT):
                    last = T(turn[:, m, k * P:(k + 1) * P], z[:, m, :, :].rearrange("p e h -> p (e h)")[:, k * P:(k + 1) * P], ident[:])
            last.then_inc(turned, 1)
            pe.wait_ge(copied, 6)
            for m in range(M):
                last = T(turn[0:E, 0, m * P:(m + 1) * P], hot[:, m, :], ident[:])
            last.then_inc(turned, 1)
            pe.wait_ge(copied, 7)
            for m in range(M):
                for k in range(FT):
                    mm(out[:, m, :], zT[:, m, k, :], w3[:, k, :], start=(k == 0), stop=False)
                last = mm(out[:, m, :], hotT[:, m, :], b3[:], start=False, stop=True)
            last.then_inc(out_ready, 1)

        @block.scalar
        def _(act):
            copy = lambda o, i: nc.scalar.activation(o, i, ACT.Copy).then_inc(copied, 1)
            for n, (dst, src) in enumerate(((w[:, 0, :], turn[:, 0, :]), (w[:, 1, :], turn[:, 1, :]),
                                            (w3[:].rearrange("p k d -> p (k d)"), turn[:, 0, :]), (gw[:], turn[:, 1, 0:E + 1]),
                                            (xT[:].rearrange("p m t -> p (m t)"), turn[:, 0, 0:M * P]))):
                act.wait_ge(turned, n + 1)
                copy(dst, src)
            act.wait_ge(scored, 1)
            nc.scalar.activation(sc[:], score[:], ACT.Sigmoid).then_inc(sig_done, 1)
            act.wait_ge(projected, 1)
            nc.scalar.activation(a[:].rearrange("p m e h -> p m (e h)"), hid[:, :, 0, :], ACT.Silu).then_inc(silu_done, 1)
            act.wait_ge(two_ready, 1)
            nc.scalar.activation(two[:], two[:], ACT.Exp).then_inc(two_done, 1)
            act.wait_ge(var_ready, 1)
            nc.scalar.activation(std[:], var[:], ACT.Sqrt).then_inc(std_ready, 1)
            act.wait_ge(turned, 6)
            copy(zT[:].rearrange("p m k t -> p m (k t)"), turn[:])
            act.wait_ge(turned, 7)
            copy(hotT[:].rearrange("e m t -> e (m t)"), turn[0:E, 0, 0:M * P])

        @block.vector
        def _(dve):
            V = nc.vector
            link = Chain(dve, step)
            TT = lambda o, p, q, op: link(V.tensor_tensor(o, p, q, op))
            dve.wait_ge(idx_loaded, 2 * M * DMA)
            for f, i, size in ((fb, ib, BATCH), (ft, it, SEQ)):
                link(V.tensor_copy(f[:], i[:]))
                link(V.tensor_scalar(neg[:], f[:], 0.0, float(size), ALU.is_lt, ALU.mult))
                TT(f[:], f[:], neg[:], ALU.add)
            link(V.scalar_tensor_tensor(out=fb[:], in0=fb[:], scalar=float(SEQ), in1=ft[:], op0=ALU.mult, op1=ALU.add))
            V.tensor_copy(row[:], fb[:]).then_inc(row_ready, 1)
            dve.wait_ge(consts, NCONST * DMA)
            dve.wait_ge(made, 3)
            dve.wait_ge(sig_done, 1)
            s8 = sc[:, :, 0:E]
            TT(pick[:], s8, xbias[:].unsqueeze(1).to_broadcast([P, M, E]), ALU.add)
            four = [P, M, E, E]
            vi, vj = over(pick[:].unsqueeze(3), four), pick[:].unsqueeze(2).to_broadcast(four)
            flat = lambda t: t[:].rearrange("p m i j -> p m (i j)")
            TT(pair[:], vj, vi, ALU.is_gt)
            TT(pair2[:], vj, vi, ALU.is_equal)
            TT(flat(pair2), flat(pair2), before[:].rearrange("p i j -> p (i j)").unsqueeze(1).to_broadcast([P, M, E * E]), ALU.mult)
            TT(flat(pair), flat(pair), flat(pair2), ALU.add)
            link(V.reduce_sum(hot[:], pair[:], AX.X))
            link(V.tensor_scalar(hot[:], hot[:], 0.5, None, ALU.is_lt))
            TT(tmp[:], s8, hot[:], ALU.mult)
            link(V.reduce_sum(red[:], tmp[:], AX.X))
            link(V.tensor_copy(two[:, :, 0], sc[:, :, E]))
            link(V.tensor_copy(two[:, :, 1], red[:]))
            link(V.reduce_max(red[:], two[:], AX.X))
            V.tensor_tensor(two[:], two[:], over(red[:].unsqueeze(2), [P, M, 2]), ALU.subtract).then_inc(two_ready, 1)
            dve.wait_ge(two_done, 1)
            link(V.reduce_sum(red[:], two[:], AX.X))
            link(V.reciprocal(red[:], red[:]))
            TT(two[:], two[:], over(red[:].unsqueeze(2), [P, M, 2]), ALU.mult)
            dve.wait_ge(silu_done, 1)
            wide, me = [P, M * E, H], lambda t: t[:].rearrange("p m e h -> p (m e) h")
            st8 = lambda t: over(t[:].rearrange("p m e -> p (m e)").unsqueeze(2), wide)
            TT(z[:].rearrange("p m e h -> p m (e h)"), hid[:, :, 1, :], a[:].rearrange("p m e h -> p m (e h)"), ALU.mult)
            link(V.reduce_sum(total[:], z[:], AX.X))
            link(V.tensor_scalar(total[:], total[:], -1.0 / H, None, ALU.mult))
            TT(me(z), me(z), st8(total), ALU.add)
            TT(sq[:], z[:], z[:], ALU.mult)
            link(V.reduce_sum(var[:], sq[:], AX.X))
            V.tensor_scalar(var[:], var[:], 1.0 / H, 1e-5, ALU.mult, ALU.add).then_inc(var_ready, 1)
            dve.wait_ge(std_ready, 1)
            link(V.reciprocal(total[:], std[:]))
            TT(me(z), me(z), st8(total), ALU.mult)
            TT(me(z), me(z), gamma[:].unsqueeze(1).to_broadcast(wide), ALU.mult)
            TT(me(z), me(z), beta[:].unsqueeze(1).to_broadcast(wide), ALU.add)
            V.tensor_tensor(me(z), me(z), st8(hot), ALU.mult).then_inc(z_ready, 1)
            dve.wait_ge(out_ready, 1)
            dve.wait_ge(old_loaded, DMA * M)
            rowwise = [P, M, D]
            TT(old[:], old[:], over(two[:, :, 0:1], rowwise), ALU.mult)
            TT(new[:], out[:], over(two[:, :, 1:2], rowwise), ALU.mult)
            V.tensor_tensor(new[:], new[:], old[:], ALU.add).then_inc(new_ready, 1)


def recurrent_block_kernel(nc, a, out):
    def scratch(name, shape, dt=F32):
        return nc.dram_tensor(name, shape, dt).ap()

    def inputs(prefix, names):
        return [a[prefix + n] for n in names.split()]

    x = [a["L0_attn_x"].rearrange("b t d -> (b t) d")] + [scratch(f"x{n}", [TOK, D]) for n in (1, 2, 3)]
    xn, xnT = scratch("xn", [TOK, D]), scratch("xnT", [D, TOK])
    s, fT, f = scratch("s", [TOK, D]), scratch("fT", [D, TOK]), scratch("f", [TOK, D])
    c, cT = scratch("c", [32, TOK]), scratch("cT", [96, TOK], BF16)
    with ExitStack() as ctx:
        ident = ctx.enter_context(nc.sbuf_tensor("identity", [P, P], F32))
        make_identity(nc, ident)
        layernorm_stage(nc, "norm0", ident, x[0], xn, xnT)

        q0, kh0, kl0 = (scratch(n, [16, P, TOK], F16) for n in ("q0", "kh0", "kl0"))
        v0, o0 = scratch("v0", [8, TOK, P]), scratch("o0", [8, P, TOK])
        project_l0(nc, xnT, *inputs("L0_attn_", "w_q w_k w_v"), q0, kh0, kl0, v0)
        o0h = o0.rearrange("g (h r) t -> h g r t", h=2)
        attention_stage(nc, "attn0", ident, q0, [kh0, kl0], v0, [o0h[0], o0h[1]], scratch("inv0", [2, 8, P]), 8, 2, P, 64, 512, 1.0)
        output_projection(nc, "out0", o0.rearrange("g r t -> (g r) t"), a["L0_attn_w_proj"], a["L0_attn_b_proj"], xn, s)
        routing_stage(nc, "route0", ident, "grouped", xnT, a["L0_ffn_gate_w"], a["L0_ffn_gate_bias"], c, cT)
        experts_stage(nc, "experts0", ident, "silu", xnT, c, cT, inputs("L0_ffn_", "w_gate w_up w_down sh_gate sh_up sh_down"), fT)
        combine_stage(nc, "mix0", ident, x[0], s, (a["L0_attn_ln_gamma"], a["L0_attn_ln_beta"], 1e-6), fT, True, None, x[1], xn, xnT)

        q1, k1, v1, o1 = (scratch(n, sh, dt) for n, sh, dt in (("q1", [16, 48, TOK], BF16), ("k1", [16, 48, TOK], BF16),
                                                               ("v1", [4, TOK, 32], F32), ("o1", [P, TOK], F32)))
        project_l1(nc, xnT, a["L1_attn_W_qkv"], a["L1_attn_b_qkv"], q1, k1, v1)
        o1h = o1.rearrange("(g h r) t -> h g r t", h=4, r=8)
        attention_stage(nc, "attn1", ident, q1, [k1], v1, [o1h[h] for h in range(4)], scratch("inv1", [2, 8, P]), 4, 4, 48, 8, 256,
                        D ** -0.5)
        output_projection(nc, "out1", o1, a["L1_attn_W_out"], a["L1_attn_b_out"], None, s)
        routing_stage(nc, "route1", ident, "top2", xnT, a["L1_ffn_Wg"], a["L1_ffn_bg"], c, cT)
        experts_stage(nc, "experts1", ident, "gelu", xnT, c, cT, inputs("L1_ffn_", "W1 b1 W2 b2"), fT)
        combine_stage(nc, "mix1", ident, x[1], s, None, fT, True, (a["L1_ffn_gamma"], a["L1_ffn_beta"], 1e-5), x[2], xn, xnT)

        ssm_stage(nc, ident, xnT, *inputs("L2_attn_", "A_real A_imag B_real B_imag C_real C_imag D"), s)
        routing_stage(nc, "route2", ident, "capacity", xnT, a["L2_ffn_w_router"], a["L2_ffn_b_router"], c, cT)
        experts_stage(nc, "experts2", ident, "gelu", xnT, c, cT, inputs("L2_ffn_", "w1 b1 w2 b2"), fT)
        combine_stage(nc, "mix2", ident, x[2], s, None, fT, True, None, x[3], xn, xnT)

        linear_attention_stage(nc, ident, xnT, *inputs("L3_attn_", "Wq bq Wk bk Wv bv Wg bg Wo bo"), s)
        shared_ffn_stage(nc, ident, xnT, *inputs("L3_ffn_", "sw1 sb1 sw2 sb2 sw3 sb3 s_ln_g s_ln_b"), f)
        routed_ffn_stage(nc, ident, xn, f, *inputs(
            "L3_ffn_", "index_b index_t sg_w sg_b eg_w eg_b exp_bias ew1 eb1 ew2 eb2 ew3 eb3 sel_ln_g sel_ln_b"))
        combine_stage(nc, "mix3", ident, x[3], s, None, f, False, None, out.rearrange("b t d -> (b t) d"), None, None)


def kernel(**inputs):
    import numpy as _np
    import concourse.bacc as _bacc
    from concourse import mybir as _mybir
    from concourse.bass_utils import run_bass_kernel_spmd as _run

    nc = _bacc.Bacc("TRN2", target_bir_lowering=False, num_devices=1)
    arrays, args = {}, {}
    for name, value in inputs.items():
        value = _np.ascontiguousarray(value)
        arrays[f"in_{name}"] = value
        args[name] = nc.dram_tensor(f"in_{name}", value.shape, _mybir.dt.from_np(value.dtype), kind="ExternalInput").ap()
    out = nc.dram_tensor("out", (BATCH, SEQ, D), F32, kind="ExternalOutput").ap()
    recurrent_block_kernel(nc, args, out)
    return _run(nc, [arrays], core_ids=[0]).results[0]["out"]
```

```python
import concourse.bass as bass
from concourse import mybir
from contextlib import ExitStack

F32 = mybir.dt.float32
F16 = mybir.dt.float16
BF16 = mybir.dt.bfloat16
I32 = mybir.dt.int32
U32 = mybir.dt.uint32
ALU = mybir.AluOpType
ACT = mybir.ActivationFunctionType
AX = mybir.AxisListType

P = 128
D = 128
BATCH, SEQ = 4, 1024
TOK = BATCH * SEQ
NT = TOK // P
CH = 512
NCH = TOK // CH
TPC = CH // P
DMA = 16


class Stage:

    def __init__(self, nc, name):
        self.nc, self.name, self.stack, self.sems = nc, name, ExitStack(), []

    def __enter__(self):
        self.stack.__enter__()
        return self

    def __exit__(self, *e):
        self.stack.__exit__(*e)
        self.nc.clear_and_free_semaphores(self.sems)
        self.nc.all_engine_barrier()

    def sb(self, name, shape, dt=F32):
        return self.stack.enter_context(self.nc.sbuf_tensor(f"{self.name}_{name}", shape, dt))

    def ps(self, name, shape, dt=F32):
        return self.stack.enter_context(self.nc.psum_tensor(f"{self.name}_{name}", shape, dt))

    def sem(self, name):
        self.sems.append(self.nc.alloc_semaphore(f"{self.name}_{name}"))
        return self.sems[-1]

    def block(self):
        return self.stack.enter_context(self.nc.Block())


class Chain:

    def __init__(self, eng, sem):
        self.eng, self.sem, self.n = eng, sem, 0

    def __call__(self, ins, base=0):
        self.n += 1
        ins.then_inc(self.sem, 1)
        self.eng.wait_ge(self.sem, base + self.n)


def rows(dram):
    return dram.rearrange("(t p) d -> p t d", p=P)


def over(ap, shape):
    return ap.to_broadcast(shape)


def make_identity(nc, ident):
    with Stage(nc, "ident") as st:
        cleared, made = st.sem("cleared"), st.sem("made")
        block = st.block()

        @block.gpsimd
        def _(pool):
            nc.gpsimd.memset(ident[:], 0.0).then_inc(cleared, 1)
            pool.wait_ge(cleared, 1)
            nc.gpsimd.affine_select(out=ident[:], in_=ident[:], compare_op=ALU.not_equal, fill=1.0, base=0,
                                    pattern=[[-1, P]], channel_multiplier=1).then_inc(made, 1)
            pool.wait_ge(made, 1)


def layernorm_stage(nc, name, ident, x_d, xn_d, xnT_d):
    NG = 4
    GT = NT // NG
    with Stage(nc, name) as st:
        x, sq = st.sb("x", [P, NT, D]), st.sb("sq", [P, GT, D])
        total, nmean = st.sb("total", [P, NT]), st.sb("nmean", [P, NT])
        var, std, rstd = st.sb("var", [P, NT]), st.sb("std", [P, NT]), st.sb("rstd", [P, NT])
        xT = st.sb("xT", [P, 2, GT * P])
        tp = st.ps("tp", [P, 2, GT * P])
        loaded = [st.sem(f"loaded{g}") for g in range(NG)]
        dve_step, var_ready, std_ready, xn_ready = (st.sem(n) for n in ("dve_step", "var_ready", "std_ready", "xn_ready"))
        turned, evacuated, stored, storedT = (st.sem(n) for n in ("turned", "evacuated", "stored", "storedT"))
        block = st.block()

        @block.sync
        def _(sp):
            for g in range(NG):
                sp.dma_start(x[:, g * GT:(g + 1) * GT, :], rows(x_d)[:, g * GT:(g + 1) * GT, :]).then_inc(loaded[g], DMA)
            for g in range(NG):
                sp.wait_ge(xn_ready, g + 1)
                sp.dma_start(rows(xn_d)[:, g * GT:(g + 1) * GT, :], x[:, g * GT:(g + 1) * GT, :]).then_inc(stored, DMA)
                sp.wait_ge(evacuated, g + 1)
                sp.dma_start(xnT_d[:, g * GT * P:(g + 1) * GT * P], xT[:, g % 2, :]).then_inc(storedT, DMA)
                sp.wait_ge(storedT, DMA * (g + 1))
            sp.wait_ge(stored, DMA * NG)

        @block.vector
        def _(dve):
            link = Chain(dve, dve_step)
            for g in range(NG):
                c = slice(g * GT, (g + 1) * GT)
                wide = [P, GT, D]
                dve.wait_ge(loaded[g], DMA)
                link(nc.vector.reduce_sum(total[:, c], x[:, c, :], AX.X))
                link(nc.vector.tensor_scalar(nmean[:, c], total[:, c], -1.0 / D, None, ALU.mult))
                link(nc.vector.tensor_tensor(x[:, c, :], x[:, c, :], over(nmean[:, c].unsqueeze(2), wide), ALU.add))
                link(nc.vector.tensor_tensor(sq[:], x[:, c, :], x[:, c, :], ALU.mult))
                link(nc.vector.reduce_sum(var[:, c], sq[:], AX.X))
                nc.vector.tensor_scalar(var[:, c], var[:, c], 1.0 / D, 1e-5, ALU.mult, ALU.add).then_inc(var_ready, 1)
                dve.wait_ge(std_ready, g + 1)
                link(nc.vector.reciprocal(rstd[:, c], std[:, c]))
                nc.vector.tensor_tensor(x[:, c, :], x[:, c, :], over(rstd[:, c].unsqueeze(2), wide),
                                        ALU.mult).then_inc(xn_ready, 1)

        @block.tensor
        def _(pe):
            for g in range(NG):
                pe.wait_ge(xn_ready, g + 1)
                if g >= 2:
                    pe.wait_ge(evacuated, g - 1)
                for t in range(GT):
                    last = nc.tensor.transpose(tp[:, g % 2, t * P:(t + 1) * P], x[:, g * GT + t, :], ident[:])
                last.then_inc(turned, 1)

        @block.scalar
        def _(act):
            def root(g):
                c = slice(g * GT, (g + 1) * GT)
                act.wait_ge(var_ready, g + 1)
                nc.scalar.activation(std[:, c], var[:, c], ACT.Sqrt).then_inc(std_ready, 1)
            root(0)
            for g in range(NG):
                if g + 1 < NG:
                    root(g + 1)
                act.wait_ge(turned, g + 1)
                if g >= 2:
                    act.wait_ge(storedT, DMA * (g - 1))
                nc.scalar.activation(xT[:, g % 2, :], tp[:, g % 2, :], ACT.Copy).then_inc(evacuated, 1)


def project_l0(nc, xnT_d, w_q, w_k, w_v, q_d, kh_d, kl_d, v_d):
    HP = 8
    HD = 64
    with Stage(nc, "proj0") as st:
        xnT = st.sb("xnT", [P, TOK])
        w = st.sb("w", [P, 2, 3, P])
        hi, lo = st.sb("hi", [P, 2, TOK], F16), st.sb("lo", [P, 2, TOK], F16)
        v = st.sb("v", [P, NT, P])
        ps = st.ps("ps", [P, 8, CH])
        x_loaded, stacked, v_stored = st.sem("x_loaded"), st.sem("stacked"), st.sem("v_stored")
        w_loaded = [st.sem("w_loaded0"), st.sem("w_loaded1")]
        made, hi_ready, lo_ready, v_ready = (st.sem(n) for n in ("made", "hi_ready", "lo_ready", "v_ready"))
        block = st.block()
        PIECES = 2 * NCH + NCH
        NST = 6

        @block.sync
        def _(sp):
            def load_w(hp, slot):
                for j, src in enumerate((w_q, w_k, w_v)):
                    sp.dma_start(w[:, slot, j, :], src[:, bass.ds(hp * P, P)]).then_inc(w_loaded[slot], DMA)
            sp.dma_start(xnT[:], xnT_d[:, :]).then_inc(x_loaded, DMA)
            load_w(0, 0)
            load_w(1, 1)
            for hp in range(HP):
                if 2 <= hp + 1 < HP:
                    sp.wait_ge(made, PIECES * hp)
                    load_w(hp + 1, (hp + 1) % 2)
                sp.wait_ge(hi_ready, 2 * NCH * (hp + 1))
                sp.wait_ge(lo_ready, 2 * NCH * (hp + 1))
                for g in range(2):
                    own = slice(g * HD, (g + 1) * HD)
                    h = 2 * hp + g
                    for part, src in ((0, hi), (1, lo)):
                        sp.dma_start(q_d[h, part * HD:(part + 1) * HD, :], src[own, 0, :]).then_inc(stacked, DMA)
                        for r in range(2):
                            sp.dma_start((kh_d, kl_d)[part][h, r * HD:(r + 1) * HD, :], src[own, 1, :]).then_inc(stacked, DMA)
                sp.wait_ge(v_ready, NCH * (hp + 1))
                sp.dma_start(v_d[hp].rearrange("(t p) e -> p t e", p=P), v[:]).then_inc(v_stored, DMA)
            sp.wait_ge(stacked, 2 * NST * DMA * HP)
            sp.wait_ge(v_stored, DMA * HP)

        @block.tensor
        def _(pe):
            pe.wait_ge(x_loaded, DMA)
            n = 0
            for hp in range(HP):
                pe.wait_ge(w_loaded[hp % 2], 3 * DMA * (hp // 2 + 1))
                for piece in range(PIECES):
                    if n >= 8:
                        m, before = divmod(n - 8, PIECES)
                        if before < 2 * NCH:
                            pe.wait_ge(lo_ready, 2 * NCH * m + before + 1)
                        else:
                            pe.wait_ge(v_ready, NCH * m + before - 2 * NCH + 1)
                    j, c = divmod(piece, NCH)
                    if j < 2:
                        last = nc.tensor.matmul(ps[:, n % 8, :], w[:, hp % 2, j, :], xnT[:, c * CH:(c + 1) * CH],
                                                start=True, stop=True)
                    else:
                        for t in range(TPC):
                            tile = c * TPC + t
                            last = nc.tensor.matmul(ps[:, n % 8, t * P:(t + 1) * P], xnT[:, tile * P:(tile + 1) * P],
                                                    w[:, hp % 2, 2, :], start=True, stop=True)
                    last.then_inc(made, 1)
                    n += 1

        @block.scalar
        def _(act):
            for hp in range(HP):
                for piece in range(PIECES):
                    n = hp * PIECES + piece
                    j, c = divmod(piece, NCH)
                    act.wait_ge(made, n + 1)
                    if j < 2:
                        if piece == 0 and hp >= 1:
                            act.wait_ge(stacked, 2 * NST * DMA * hp)
                        nc.scalar.activation(hi[:, j, c * CH:(c + 1) * CH], ps[:, n % 8, :], ACT.Copy,
                                             scale=HD ** -0.5 if j == 0 else 1.0).then_inc(hi_ready, 1)
                    else:
                        if c == 0 and hp >= 1:
                            act.wait_ge(v_stored, DMA * hp)
                        nc.scalar.activation(v[:, c * TPC:(c + 1) * TPC, :],
                                             ps[:, n % 8, :].rearrange("p (t e) -> p t e", t=TPC),
                                             ACT.Copy).then_inc(v_ready, 1)

        @block.vector
        def _(dve):
            for hp in range(HP):
                for piece in range(2 * NCH):
                    n = hp * PIECES + piece
                    j, c = divmod(piece, NCH)
                    dve.wait_ge(hi_ready, hp * 2 * NCH + piece + 1)
                    if piece == 0 and hp >= 1:
                        dve.wait_ge(stacked, 2 * NST * DMA * hp)
                    nc.vector.scalar_tensor_tensor(out=lo[:, j, c * CH:(c + 1) * CH], in0=ps[:, n % 8, :],
                                                   scalar=HD ** -0.5 if j == 0 else 1.0,
                                                   in1=hi[:, j, c * CH:(c + 1) * CH], op0=ALU.mult,
                                                   op1=ALU.subtract).then_inc(lo_ready, 1)


def attention_stage(nc, name, ident, q_d, k_ds, v_d, o_ds, scale_d, groups, heads, stack_rows, head_rows, qchunk, out_scale):
    NK = len(k_ds)
    KT = SEQ // P
    QT = qchunk // P
    UPC = QT * heads
    NC = SEQ // qchunk
    U = UPC * NC
    NI = BATCH * groups
    col = P // heads
    NPROB = 4
    G = NC * NI
    KH = KT // 2
    SHARES = [[r - 1] if r < UPC - 1 else list(range(r - 1, KT)) for r in range(1, UPC)]
    assert U % NPROB == 0 and NC % 2 == 0 and U % 2 == 0 and UPC == KT
    with Stage(nc, name) as st:
        q = st.sb("q", [P, 2, heads, SEQ], q_d.dtype)
        k = [st.sb(f"k{n}", [P, 2, heads, SEQ], q_d.dtype) for n in range(NK)]
        v = st.sb("v", [P, 2, KT, P])
        prob = st.sb("prob", [P, NPROB, SEQ])
        probT = st.sb("probT", [P, 2, heads, KT, qchunk])
        nmax, sums = st.sb("nmax", [P, 2, U]), st.sb("sums", [P, 2, U])
        inv, invT = st.sb("inv", [P, 2, UPC]), st.sb("invT", [UPC, 2, P])
        invB = st.sb("invB", [P, 2, qchunk])
        out = st.sb("out", [P, 2, qchunk])
        score = st.ps("score", [P, 2, SEQ])
        turn = [st.ps(f"turn{n}", [P, KH, P]) for n in range(2)]
        acc = st.ps("acc", [P, CH])
        small = st.ps("small", [P, CH])
        loaded = [st.sem("loaded0"), st.sem("loaded1")]
        names = ("zeroed", "scored", "maxed", "exped", "turned", "copied_a", "copied_v", "weighed", "inverted", "inv_turned",
                 "inv_copied", "normed")
        (zeroed, scored, maxed, exped, turned, copied_a, copied_v, weighed, inverted, inv_turned, inv_copied,
         normed) = (st.sem(n) for n in names)
        inv_out, inv_back, out_stored = ([st.sem(f"{n}{s}") for s in range(2)] for n in ("inv_out", "inv_back", "out_stored"))
        block = st.block()
        LOADS = NK + 2

        def iterations(eng, body):
            body(0, 0, True, False)
            with eng.Fori(0, (NI - 2) // 2) as j:
                body(2 * j + 1, 1, False, False)
                body(2 * j + 2, 0, False, False)
            body(NI - 1, 1, False, True)

        @block.sync
        def _(sp):
            def load(i, slot):
                b, g = i // groups, i % groups
                tok = bass.ds(b * SEQ, SEQ)
                for src, dst in [(q_d, q)] + list(zip(k_ds, k)):
                    sp.dma_start(dst[0:stack_rows, slot, :, :],
                                 src[bass.ds(g * heads, heads), :, tok].rearrange("h r t -> r h t")).then_inc(loaded[slot], DMA)
                sp.dma_start(v[:, slot, :, 0:heads * head_rows],
                             v_d[bass.ds(g, 1), tok, :].rearrange("a (t p) e -> p (a t) e", p=P)).then_inc(loaded[slot], DMA)

            def store(i, c):
                s = c % 2
                sp.wait_ge(normed, NC * i + c + 1)
                b, grp = i // groups, i % groups
                for h in range(heads):
                    sp.dma_start(o_ds[h][bass.ds(grp, 1), :, bass.ds(b * SEQ + c * qchunk, qchunk)].rearrange("a r t -> (a r) t"),
                                 out[h * col:h * col + head_rows, s, :]).then_inc(out_stored[s], DMA)

            def bounce(i, c):
                s = c % 2
                sp.wait_ge(inv_copied, NC * i + c + 1)
                sp.dma_start(scale_d[s], invT[:, s, :]).then_inc(inv_out[s], DMA)
                sp.wait_ge(inv_out[s], DMA * (NC // 2 * i + c // 2 + 1))
                for h in range(heads):
                    sp.dma_start(invB[h * col:h * col + head_rows, s, :],
                                 scale_d[s].rearrange("(h t) q -> h (t q)", h=heads)[h].partition_broadcast(head_rows)
                                 ).then_inc(inv_back[s], DMA)

            def body(i, slot, first, final):
                if first:
                    load(1, 1)
                for c in range(NC):
                    if not (first and c < 2):
                        store(*((i, c - 2) if c >= 2 else (i - 1, c - 2 + NC)))
                    if not (first and c == 0):
                        bounce(*((i, c - 1) if c else (i - 1, NC - 1)))
                    if c == 0 and not (first or final):
                        sp.wait_ge(weighed, NC * i)
                        load(i + 1, 1 - slot)

            if stack_rows < P:
                sp.wait_ge(zeroed, NK + 1)
            load(0, 0)
            iterations(sp, body)
            store(NI - 1, NC - 2)
            bounce(NI - 1, NC - 1)
            store(NI - 1, NC - 1)
            for s in range(2):
                sp.wait_ge(out_stored[s], DMA * heads * NC * NI // 2)

        @block.gpsimd
        def _(pool):
            if stack_rows < P:
                for t in [q] + k:
                    nc.gpsimd.memset(t[:], 0.0).then_inc(zeroed, 1)

        @block.tensor
        def _(pe):
            def scores(i, slot, u, first):
                if u == 0:
                    pe.wait_ge(loaded[slot], (i // 2 + 1) * LOADS * DMA)
                if not (first and u < 2):
                    pe.wait_ge(exped, U * i + u - 1)
                c, r = divmod(u, UPC)
                t, h = divmod(r, heads)
                qt = c * QT + t
                for half in range(SEQ // CH):
                    for n in range(NK):
                        last = nc.tensor.matmul(score[:, u % 2, half * CH:(half + 1) * CH],
                                                q[:, slot, h, qt * P:(qt + 1) * P],
                                                k[n][:, slot, h, half * CH:(half + 1) * CH], start=(n == 0), stop=(n == NK - 1))
                last.then_inc(scored, 1)

            def turn_unit(n, u, any_before):
                pe.wait_ge(exped, n + 1)
                if any_before:
                    pe.wait_ge(copied_a, n)
                    pe.wait_ge(copied_v, n)
                for t in range(KT):
                    last = nc.tensor.transpose(turn[t // KH][:, t % KH, :], prob[:, u % NPROB, t * P:(t + 1) * P], ident[:])
                last.then_inc(turned, 1)

            def turn_factors(g, c, any_before):
                pe.wait_ge(inverted, g + 1)
                if any_before:
                    pe.wait_ge(inv_copied, g)
                nc.tensor.transpose(small[0:UPC, 0:P], inv[:, c % 2, :], ident[:]).then_inc(inv_turned, 1)

            def weigh(g, slot, c, tiles, any_before):
                if tiles[0] == 0:
                    pe.wait_ge(copied_a, UPC * (g + 1))
                    pe.wait_ge(copied_v, UPC * (g + 1))
                    if any_before:
                        pe.wait_ge(normed, g)
                for t in tiles:
                    for h in range(heads):
                        last = nc.tensor.matmul(acc[h * col:h * col + head_rows, 0:qchunk],
                                                v[:, slot, t, h * head_rows:(h + 1) * head_rows], probT[:, c % 2, h, t, :],
                                                start=(t == 0), stop=(t == KT - 1))
                if tiles[-1] == KT - 1:
                    last.then_inc(weighed, 1)

            def body(i, slot, first, final):
                for u in range(U):
                    if u + 1 < U:
                        scores(i, slot, u + 1, first)
                    elif not final:
                        scores(i + 1, 1 - slot, 0, False)
                    if not (first and u == 0):
                        turn_unit(U * i + u - 1, (u - 1) % U, not (first and u == 1))
                    c, r = divmod(u, UPC)
                    if not (first and c == 0):
                        g, before = NC * i + c - 1, not (first and c == 1)
                        if r == 1:
                            turn_factors(g, (c - 1) % NC, before)
                        if r >= 1:
                            weigh(g, slot if c else 1 - slot, (c - 1) % NC, SHARES[r - 1], before)

            scores(0, 0, 0, True)
            iterations(pe, body)
            turn_unit(U * NI - 1, U - 1, True)
            turn_factors(G - 1, NC - 1, True)
            weigh(G - 1, 1, NC - 1, list(range(KT)), True)

        @block.scalar
        def _(act):
            def copy(g, c, n, u, any_used):
                t, h = divmod(u % UPC, heads)
                act.wait_ge(turned, n + 1)
                if any_used:
                    act.wait_ge(weighed, g - 1)
                nc.scalar.activation(probT[:, c % 2, h, 0:KH, t * P:(t + 1) * P], turn[0][:], ACT.Copy).then_inc(copied_a, 1)

            def body(i, slot, first, final):
                for u in range(U):
                    act.wait_ge(maxed, U * i + u + 1)
                    if not (first and u < NPROB):
                        act.wait_ge(turned, U * i + u - NPROB + 1)
                    nc.scalar.activation(prob[:, u % NPROB, :], score[:, u % 2, :], ACT.Exp,
                                         bias=nmax[:, slot, u:u + 1], accum_out=sums[:, slot, u:u + 1]).then_inc(exped, 1)
                    if not (first and u == 0):
                        c = (u - 1) // UPC
                        copy(NC * i + c, c % NC, U * i + u - 1, (u - 1) % U, not (first and c < 2))

            iterations(act, body)
            copy(G - 1, NC - 1, U * NI - 1, U - 1, True)

        @block.vector
        def _(dve):
            def copy(g, c, n, u, any_used):
                t, h = divmod(u % UPC, heads)
                dve.wait_ge(turned, n + 1)
                if any_used:
                    dve.wait_ge(weighed, g - 1)
                nc.vector.tensor_copy(probT[:, c % 2, h, KH:KT, t * P:(t + 1) * P], turn[1][:]).then_inc(copied_v, 1)

            def maximum(i, slot, u):
                dve.wait_ge(scored, U * i + u + 1)
                nc.vector.tensor_reduce(nmax[:, slot, u:u + 1], score[:, u % 2, :], AX.X, ALU.max, negate=True).then_inc(maxed, 1)

            def invert(g, slot, c):
                dve.wait_ge(exped, UPC * (g + 1))
                nc.vector.reciprocal(inv[:, c % 2, :].rearrange("p (h t) -> p t h", h=heads),
                                     sums[:, slot, c * UPC:(c + 1) * UPC].rearrange("p (t h) -> p t h", h=heads)
                                     ).then_inc(inverted, 1)

            def inv_copy(g, c):
                dve.wait_ge(inv_turned, g + 1)
                nc.vector.tensor_scalar(invT[:, c % 2, :], small[0:UPC, 0:P], out_scale, None,
                                        ALU.mult).then_inc(inv_copied, 1)

            def normalise(i, c, any_before):
                g, s = NC * i + c, c % 2
                nth = NC // 2 * i + c // 2
                dve.wait_ge(weighed, g + 1)
                dve.wait_ge(inv_back[s], DMA * heads * (nth + 1))
                if any_before:
                    dve.wait_ge(out_stored[s], DMA * heads * nth)
                for h in range(heads):
                    own = slice(h * col, h * col + head_rows)
                    if heads * head_rows == P:
                        own = slice(0, P)
                    last = nc.vector.tensor_tensor(out[own, s, :], acc[own, 0:qchunk], invB[own, s, :], ALU.mult)
                    if heads * head_rows == P:
                        break
                last.then_inc(normed, 1)

            def body(i, slot, first, final):
                if first:
                    maximum(i, slot, 0)
                for u in range(U):
                    if u + 1 < U:
                        maximum(i, slot, u + 1)
                    elif not final:
                        maximum(i + 1, 1 - slot, 0)
                    c, r = divmod(u, UPC)
                    if r == 0 and not (first and c == 0):
                        invert(NC * i + c - 1, slot if c else 1 - slot, (c - 1) % NC)
                    if r == 0 and not (first and c < 2):
                        normalise(*((i, c - 2) if c >= 2 else (i - 1, c - 2 + NC)), not (first and c < 4))
                    if not (first and u == 0):
                        last_c = (u - 1) // UPC
                        copy(NC * i + last_c, last_c % NC, U * i + u - 1, (u - 1) % U, not (first and last_c < 2))
                    if r == 1 and not (first and c == 0):
                        inv_copy(NC * i + c - 1, (c - 1) % NC)

            iterations(dve, body)
            invert(G - 1, 1, NC - 1)
            normalise(NI - 1, NC - 2, True)
            copy(G - 1, NC - 1, U * NI - 1, U - 1, True)
            inv_copy(G - 1, NC - 1)
            normalise(NI - 1, NC - 1, True)


def narrow_attention_stage(nc, ident, q_d, k_d, v_d, o_d, l_d, max_d):
    HEADS, R = 16, 8
    HG = 4
    COL = P // HG
    NG = HEADS // HG
    Q_PARTS, K_PARTS = (0, 0, 1, 1, 0, 2), (0, 1, 0, 1, 2, 0)
    STACK = len(Q_PARTS) * R
    SHIFT = 64
    NI = BATCH * NG
    QT, KT = SEQ // P, SEQ // P
    NQ = SEQ // CH
    PAIRS = NQ * KT
    U = 2 * PAIRS
    ITEMS = HG * QT * 2
    NPROB = 8
    AHEAD = 6
    PER_PAIR = ITEMS // PAIRS
    assert U % NPROB == 0 and NI % 2 == 0
    with Stage(nc, "attn1") as st:
        qm, km = st.sb("qm", [P, 2, HG, SEQ], BF16), st.sb("km", [P, 2, HG, SEQ], BF16)
        qe, ke = st.sb("qe", [P, 2, HG, SEQ], BF16), st.sb("ke", [P, 2, HG, SEQ], BF16)
        v = st.sb("v", [P, 2, KT, HG, COL])
        prob = st.sb("prob", [P, NPROB, 2, CH])
        half_max = st.sb("half_max", [P, ITEMS // 2, 2])
        nmax = st.sb("nmax", [P, ITEMS // 2])
        nmaxT = st.sb("nmaxT", [ITEMS // 2, P], BF16)
        out = st.sb("out", [P, NQ, CH])
        peek = st.ps("peek", [P, 2, CH])
        score = st.ps("score", [P, 2, 2, CH])
        acc = st.ps("acc", [P, NQ, CH])
        loaded_m, loaded_e, shift_in = ([st.sem(f"{n}{s}") for s in range(2)] for n in ("loaded_m", "loaded_e", "shift_in"))
        shift_out, stored = st.sem("shift_out"), st.sem("stored")
        zeroed, peeked, maxed, merged, scored, exped, weighed, read_out, max_ready = (
            st.sem(n) for n in ("zeroed", "peeked", "maxed", "merged", "scored", "exped", "weighed", "read_out", "max_ready"))
        block = st.block()
        LOADS_M, LOADS_E = 2 * len(Q_PARTS), 2 * len(Q_PARTS) + HG
        STORES = 2 * HG
        MSTEPS = ITEMS + 1

        def peek_items(i, u):
            first = (u + AHEAD) % U // 2 * PER_PAIR
            return i + (1 if u < U - AHEAD else 2), range(first, first + 1) if u % 2 == 0 else range(first + 1, first + PER_PAIR)

        def iterations(eng, body):
            body(0, 0, True, False)
            with eng.Fori(0, (NI - 2) // 2) as j:
                body(2 * j + 1, 1, False, False)
                body(2 * j + 2, 0, False, False)
            body(NI - 1, 1, False, True)

        @block.sync
        def _(sp):
            def load_stack(dst, src, order, i, slot, sem):
                b, g = i // NG % BATCH, i % NG
                for blk, part in enumerate(order):
                    sp.dma_start(dst[blk * R:(blk + 1) * R, slot, :, :],
                                 src[part][bass.ds(g * HG * R, HG * R), bass.ds(b * SEQ, SEQ)].rearrange("(h r) t -> r h t", r=R)
                                 ).then_inc(sem, DMA)

            def load_m(i, slot):
                load_stack(qm, q_d, Q_PARTS, i, slot, loaded_m[slot])
                load_stack(km, k_d, K_PARTS, i, slot, loaded_m[slot])

            def load_e(i, slot):
                b, g = i // NG, i % NG
                load_stack(qe, q_d, Q_PARTS, i, slot, loaded_e[slot])
                load_stack(ke, k_d, K_PARTS, i, slot, loaded_e[slot])
                for h in range(HG):
                    sp.dma_start(v[:, slot, :, h, 0:R],
                                 v_d[bass.ds(g, 1), bass.ds(b * SEQ, SEQ), h * R:(h + 1) * R].rearrange("a (t p) e -> p (a t) e", p=P)
                                 ).then_inc(loaded_e[slot], DMA)

            def shift(i, slot):
                sp.wait_ge(max_ready, i + 1)
                sp.dma_start(max_d[slot], nmaxT[:]).then_inc(shift_out, DMA)
                sp.wait_ge(shift_out, DMA * (i + 1))
                sp.dma_start(qe[SHIFT:SHIFT + 1, slot, :, :],
                             max_d[slot].rearrange("(a h t) p -> a h (t p)", a=1, h=HG)).then_inc(shift_in[slot], DMA)

            def store(i, half):
                b, g = i // NG, i % NG
                sp.wait_ge(read_out, NQ * i + half + 1)
                for n, dst in enumerate((o_d, l_d)):
                    for h in range(HG):
                        sp.dma_start(dst.rearrange("(g h r) t -> h g r t", h=HG, r=R)[
                                         h, bass.ds(g, 1), :, bass.ds(b * SEQ + half * CH, CH)].rearrange("a r t -> (a r) t"),
                                     out[h * COL + n * R:h * COL + (n + 1) * R, half, :]).then_inc(stored, DMA)

            def body(i, slot, first, final):
                if not final:
                    if not first:
                        sp.wait_ge(weighed, PAIRS * i)
                    load_e(i + 1, 1 - slot)
                    sp.wait_ge(peeked, MSTEPS * (i + 1))
                    load_m(i + 2, slot)
                if not first:
                    store(i - 1, 1)
                store(i, 0)
                if not final:
                    shift(i + 1, 1 - slot)

            sp.wait_ge(zeroed, 6)
            load_m(0, 0)
            load_e(0, 0)
            load_m(1, 1)
            shift(0, 0)
            iterations(sp, body)
            store(NI - 1, 1)
            sp.wait_ge(stored, DMA * STORES * NQ * NI)
            sp.wait_ge(loaded_m[0], DMA * LOADS_M * (NI // 2 + 1))

        @block.gpsimd
        def _(pool):
            nc.gpsimd.memset(v[:], 1.0).then_inc(zeroed, 1)
            nc.gpsimd.memset(qe[:], 0.0).then_inc(zeroed, 1)

        @block.tensor
        def _(pe):
            mm = nc.tensor.matmul

            def peek_step(i, slot, k, first):
                if k == 0:
                    pe.wait_ge(loaded_m[slot], DMA * LOADS_M * (i // 2 + 1))
                    if not first:
                        pe.wait_ge(max_ready, i)
                elif k == ITEMS:
                    pe.wait_ge(merged, i + 1)
                    nc.tensor.transpose(peek[0:ITEMS // 2, 0, 0:P], nmax[:], ident[:]).then_inc(peeked, 1)
                    return
                elif not (first and k == 1):
                    pe.wait_ge(maxed, ITEMS * i + k - 1)
                h, t, half = k // (2 * QT), k // 2 % QT, k % 2
                mm(peek[:, half, :], qm[:, slot, h, t * P:(t + 1) * P], km[:, slot, h, half * CH:(half + 1) * CH],
                   start=True, stop=True).then_inc(peeked, 1)

            def score_unit(i, slot, u, first):
                pair, hp = u // 2, u % 2
                half, t = pair // KT, pair % KT
                if u == 0:
                    pe.wait_ge(loaded_e[slot], DMA * LOADS_E * (i // 2 + 1))
                    pe.wait_ge(shift_in[slot], DMA * (i // 2 + 1))
                if not (first and u < 2):
                    pe.wait_ge(exped, U * i + u - 1)
                for n in range(2):
                    h = 2 * hp + n
                    last = mm(score[:, u % 2, n, :], ke[:, slot, h, t * P:(t + 1) * P], qe[:, slot, h, half * CH:(half + 1) * CH],
                              start=True, stop=True)
                last.then_inc(scored, 1)

            def weigh(i, slot, pair, first):
                half, t = pair // KT, pair % KT
                pe.wait_ge(exped, U * i + 2 * pair + 2)
                if t == 0 and not first:
                    pe.wait_ge(read_out, NQ * i + half - 1)
                for h in range(HG):
                    last = mm(acc[h * COL:(h + 1) * COL, half, :], v[:, slot, t, h, :],
                              prob[:, (2 * pair + h // 2) % NPROB, h % 2, :], start=(t == 0), stop=(t == KT - 1))
                last.then_inc(weighed, 1)

            def body(i, slot, first, final):
                for u in range(U):
                    n, items = peek_items(i, u)
                    items = [] if final else items
                    peek_slot = 1 - slot if u < U - AHEAD else slot
                    if u == U - AHEAD and not final:
                        peek_step(i + 1, 1 - slot, ITEMS, False)
                    elif not final:
                        peek_step(n, peek_slot, items[0], False)
                    if u + 1 < U:
                        score_unit(i, slot, u + 1, first)
                    elif not final:
                        score_unit(i + 1, 1 - slot, 0, False)
                    if u == U - AHEAD and not final:
                        peek_step(n, peek_slot, items[0], False)
                    for k in items[1:-1]:
                        peek_step(n, peek_slot, k, False)
                    if u == 1 and not first:
                        weigh(i - 1, 1 - slot, PAIRS - 1, False)
                    if u % 2 and u >= 3:
                        weigh(i, slot, (u - 3) // 2, first)
                    if u % 2 and not final:
                        peek_step(n, peek_slot, items[-1], False)

            pe.wait_ge(zeroed, 6)
            for k in range(ITEMS + 1):
                peek_step(0, 0, k, True)
            for k in range(AHEAD // 2 * PER_PAIR):
                peek_step(1, 1, k, False)
            score_unit(0, 0, 0, True)
            iterations(pe, body)
            weigh(NI - 1, 1, PAIRS - 1, False)

        @block.scalar
        def _(act):
            def read(i, half, any_before):
                act.wait_ge(weighed, PAIRS * i + (half + 1) * KT)
                if any_before:
                    act.wait_ge(stored, DMA * STORES * (NQ * i + half))
                nc.scalar.activation(out[:, half, :], acc[:, half, :], ACT.Copy).then_inc(read_out, 1)

            def body(i, slot, first, final):
                for u in range(U):
                    act.wait_ge(scored, U * i + u + 1)
                    if not (first and u < NPROB):
                        act.wait_ge(weighed, PAIRS * i + (u - NPROB) // 2 + 1)
                    nc.scalar.activation(prob[:, u % NPROB, :, :], score[:, u % 2, :, :], ACT.Exp).then_inc(exped, 1)
                    if u == 3 and not first:
                        read(i - 1, 1, True)
                    if u == 2 * KT + 3:
                        read(i, 0, not first)

            iterations(act, body)
            read(NI - 1, 1, True)

        @block.vector
        def _(dve):
            V = nc.vector

            def peek_step(i, k):
                dve.wait_ge(peeked, MSTEPS * i + k + 1)
                V.tensor_reduce(half_max[:, k // 2, k % 2:k % 2 + 1], peek[:, k % 2, :], AX.X, ALU.max, negate=True
                                ).then_inc(maxed, 1)

            def merge(i, any_before):
                dve.wait_ge(maxed, ITEMS * (i + 1))
                V.tensor_tensor(nmax[:].unsqueeze(2), half_max[:, :, 0:1], half_max[:, :, 1:2], ALU.min).then_inc(merged, 1)
                dve.wait_ge(peeked, MSTEPS * (i + 1))
                if any_before:
                    dve.wait_ge(shift_out, DMA * i)
                V.tensor_copy(nmaxT[:], peek[0:ITEMS // 2, 0, 0:P]).then_inc(max_ready, 1)

            def body(i, slot, first, final):
                if final:
                    return
                for u in range(U):
                    if u == U - AHEAD:
                        merge(i + 1, True)
                    n, items = peek_items(i, u)
                    for k in items:
                        peek_step(n, k)

            for n, t in enumerate((qm, km, ke)):
                V.memset(t[:], 0.0).then_inc(zeroed, 1)
            dve.wait_ge(zeroed, 5)
            V.memset(ke[SHIFT:SHIFT + 1, :, :, :], 1.0).then_inc(zeroed, 1)
            for k in range(ITEMS):
                peek_step(0, k)
            merge(0, False)
            for k in range(AHEAD // 2 * PER_PAIR):
                peek_step(1, k)
            iterations(dve, body)


def broadcast_rows(vec, n=P):
    return vec.partition_broadcast(n)


def output_projection(nc, name, o_d, sums_d, scale, w, bias, resid_d, s_d):
    KH = o_d.shape[0] // P
    with Stage(nc, name) as st:
        o = st.sb("o", [P, 2, KH, CH])
        wt = st.sb("wt", [P, KH, D])
        bias_b = st.sb("bias_b", [P, D])
        res = st.sb("res", [P, 2, TPC, D])
        sums = st.sb("sums", [P, 2, KH, CH]) if sums_d is not None else None
        y = st.sb("y", [P, 2, TPC, D])
        acc = st.ps("acc", [P, 2, TPC, D])
        consts, inverted, divided = (st.sem(n) for n in ("consts", "inverted", "divided"))
        o_loaded, r_loaded, stored = ([st.sem(f"{n}{s}") for s in range(2)] for n in ("o_loaded", "r_loaded", "stored"))
        projected, summed, biased = st.sem("projected"), st.sem("summed"), st.sem("biased")
        block = st.block()

        def iterations(eng, body):
            body(0, 0, True)
            body(1, 1, True)
            with eng.Fori(1, NCH // 2) as j:
                body(2 * j, 0, False)
                body(2 * j + 1, 1, False)

        @block.sync
        def _(sp):
            sp.dma_start(wt[:], w.rearrange("(k p) d -> p k d", p=P)).then_inc(consts, DMA)
            sp.dma_start(bias_b[:], broadcast_rows(bias)).then_inc(consts, DMA)

            def load(i, slot, first):
                if not first:
                    sp.wait_ge(projected, i - 1)
                sp.dma_start(o[:, slot, :, :], o_d.rearrange("(k p) t -> p k t", p=P)[:, :, bass.ds(i * CH, CH)]
                             ).then_inc(o_loaded[slot], DMA)
                if sums_d is not None:
                    sp.dma_start(sums[:, slot, :, :], sums_d.rearrange("(k p) t -> p k t", p=P)[:, :, bass.ds(i * CH, CH)]
                                 ).then_inc(o_loaded[slot], DMA)
                if resid_d is not None:
                    if not first:
                        sp.wait_ge(summed, i - 1)
                    sp.dma_start(res[:, slot, :, :], rows(resid_d)[:, bass.ds(i * TPC, TPC), :]).then_inc(r_loaded[slot], DMA)
            iterations(sp, load)
            for s in range(2):
                sp.wait_ge(stored[s], DMA * NCH // 2)

        @block.tensor
        def _(pe):
            pe.wait_ge(consts, 2 * DMA)

            def body(i, slot, first):
                if sums_d is not None:
                    pe.wait_ge(divided, i + 2)
                else:
                    pe.wait_ge(o_loaded[slot], DMA * ((i - slot) // 2 + 1))
                if not first:
                    pe.wait_ge(summed, i - 1)
                for t in range(TPC):
                    for h in range(KH):
                        last = nc.tensor.matmul(acc[:, slot, t, :], o[:, slot, h, t * P:(t + 1) * P], wt[:, h, :],
                                                start=(h == 0), stop=(h == KH - 1))
                last.then_inc(projected, 1)
            iterations(pe, body)

        @block.vector
        def _(dve):
            dve.wait_ge(consts, 2 * DMA)
            if sums_d is not None:
                nc.vector.tensor_scalar(wt[:], wt[:], scale, None, ALU.mult).then_inc(divided, 1)

            def divide(i, slot):
                dve.wait_ge(o_loaded[slot], 2 * DMA * ((i - slot) // 2 + 1))
                nc.vector.reciprocal(sums[:, slot, :, :], sums[:, slot, :, :]).then_inc(inverted, 1)
                dve.wait_ge(inverted, i + 1)
                nc.vector.tensor_tensor(o[:, slot, :, :], o[:, slot, :, :], sums[:, slot, :, :], ALU.mult).then_inc(divided, 1)

            def body(i, slot, first):
                if sums_d is not None:
                    divide(i, slot)
                dve.wait_ge(projected, i + 1)
                if not first:
                    dve.wait_ge(stored[slot], DMA * ((i - slot) // 2))
                ins = nc.vector.tensor_tensor(y[:, slot, :, :], acc[:, slot, :, :],
                                              bias_b[:].unsqueeze(1).to_broadcast([P, TPC, D]), ALU.add)
                if resid_d is not None:
                    ins.then_inc(biased, 1)
                    dve.wait_ge(biased, i + 1)
                    dve.wait_ge(r_loaded[slot], DMA * ((i - slot) // 2 + 1))
                    ins = nc.vector.tensor_tensor(y[:, slot, :, :], y[:, slot, :, :], res[:, slot, :, :], ALU.add)
                ins.then_inc(summed, 1)
            iterations(dve, body)

        @block.scalar
        def _(act):
            def body(i, slot, first):
                act.wait_ge(summed, i + 1)
                act.dma_start(rows(s_d)[:, bass.ds(i * TPC, TPC), :], y[:, slot, :, :]).then_inc(stored[slot], DMA)
            iterations(act, body)


def combine_stage(nc, name, ident, x_d, s_d, s_norm, f_d, f_turned, f_norm, x_out, xn_d, xnT_d, picks=None):
    NG = 4
    GT = NT // NG
    wide = [P, GT, D]
    with Stage(nc, name) as st:
        x, s, f = (st.sb(n, [P, NT, D]) for n in ("x", "s", "f"))
        fT = st.sb("fT", [P, TOK]) if f_turned else None
        if picks:
            f2, idx, weight = st.sb("f2", [P, NT, D]), st.sb("idx", [P, 2, NT], I32), st.sb("weight", [P, 2, NT])
            picks_loaded = st.sem("picks_loaded")
            gathered = [st.sem(f"gathered{g}") for g in range(NG)]
        sq = st.sb("sq", wide)
        gate = st.sb("gate", wide)
        total, nmean, var, std, rstd = (st.sb(n, [P, GT]) for n in ("total", "nmean", "var", "std", "rstd"))
        affine = {id(n): (st.sb(f"gamma{m}", [P, D]), st.sb(f"beta{m}", [P, D])) for m, n in enumerate((s_norm, f_norm)) if n}
        xT = st.sb("xT", [P, 2, GT * P])
        ftp = st.ps("ftp", wide)
        tp = st.ps("tp", [P, 2, GT * P])
        consts, dve_step, f_tp = st.sem("consts"), st.sem("dve_step"), st.sem("f_tp")
        loaded = [st.sem(f"loaded{g}") for g in range(NG)]
        var_ready, std_ready, f_ready, gated, xn_ready, x_ready = (
            st.sem(n) for n in ("var_ready", "std_ready", "f_ready", "gated", "xn_ready", "x_ready"))
        turned, evacuated, storedT, stored = (st.sem(n) for n in ("turned", "evacuated", "storedT", "stored"))
        block = st.block()
        last_stage = xn_d is None
        NORMS = bool(s_norm) + bool(f_norm) + (not last_stage)
        grp = lambda g: slice(g * GT, (g + 1) * GT)

        LOADS = 2 if picks else 3

        @block.gpsimd
        def _(pool):
            if picks:
                pool.wait_ge(picks_loaded, 2 * DMA)
                for g in range(NG):
                    for t in range(g * GT, (g + 1) * GT):
                        for j, dst in enumerate((f, f2)):
                            pool.indirect_dma_start(out=dst[:, t, :], out_offset=None, in_=f_d[:, :], in_offset=bass.IndirectOffsetOnAxis(
                                ap=idx[:, j, t:t + 1].bitcast(U32), axis=0)).then_inc(gathered[g], DMA)

        @block.sync
        def _(sp):
            if picks:
                for dst, src in zip((idx, weight), picks):
                    sp.dma_start(dst[:], src[:]).then_inc(picks_loaded, DMA)
            for n in (s_norm, f_norm):
                if n:
                    for t, v in zip(affine[id(n)], n[:2]):
                        sp.dma_start(t[:], broadcast_rows(v)).then_inc(consts, DMA)
            for g in range(NG):
                sp.dma_start(x[:, grp(g), :], rows(x_d)[:, grp(g), :]).then_inc(loaded[g], DMA)
                sp.dma_start(s[:, grp(g), :], rows(s_d)[:, grp(g), :]).then_inc(loaded[g], DMA)
                if picks:
                    continue
                if f_turned:
                    sp.dma_start(fT[:, g * GT * P:(g + 1) * GT * P], f_d[:, g * GT * P:(g + 1) * GT * P]).then_inc(loaded[g], DMA)
                else:
                    sp.dma_start(f[:, grp(g), :], rows(f_d)[:, grp(g), :]).then_inc(loaded[g], DMA)
            for g in range(NG):
                sp.wait_ge(x_ready, g + 1)
                sp.dma_start(rows(x_out)[:, grp(g), :], x[:, grp(g), :]).then_inc(stored, DMA)
                if not last_stage:
                    sp.wait_ge(xn_ready, g + 1)
                    sp.dma_start(rows(xn_d)[:, grp(g), :], s[:, grp(g), :]).then_inc(stored, DMA)
                    sp.wait_ge(evacuated, g + 1)
                    sp.dma_start(xnT_d[:, g * GT * P:(g + 1) * GT * P], xT[:, g % 2, :]).then_inc(storedT, DMA)
                    sp.wait_ge(storedT, DMA * (g + 1))
            sp.wait_ge(stored, DMA * NG * (1 if last_stage else 2))

        @block.vector
        def _(dve):
            link = Chain(dve, dve_step)
            roots = [0]

            def normalise(out, src, norm, eps):
                link(nc.vector.reduce_sum(total[:], src, AX.X))
                link(nc.vector.tensor_scalar(nmean[:], total[:], -1.0 / D, None, ALU.mult))
                link(nc.vector.tensor_tensor(out, src, over(nmean[:].unsqueeze(2), wide), ALU.add))
                link(nc.vector.tensor_tensor(sq[:], out, out, ALU.mult))
                link(nc.vector.reduce_sum(var[:], sq[:], AX.X))
                nc.vector.tensor_scalar(var[:], var[:], 1.0 / D, eps, ALU.mult, ALU.add).then_inc(var_ready, 1)
                roots[0] += 1
                dve.wait_ge(std_ready, roots[0])
                link(nc.vector.reciprocal(rstd[:], std[:]))
                ins = nc.vector.tensor_tensor(out, out, over(rstd[:].unsqueeze(2), wide), ALU.mult)
                if norm:
                    gamma, beta = affine[id(norm)]
                    link(ins)
                    link(nc.vector.tensor_tensor(out, out, gamma[:].unsqueeze(1).to_broadcast(wide), ALU.mult))
                    ins = nc.vector.tensor_tensor(out, out, beta[:].unsqueeze(1).to_broadcast(wide), ALU.add)
                return ins

            if affine:
                dve.wait_ge(consts, 2 * DMA * len(affine))
            for g in range(NG):
                dve.wait_ge(loaded[g], LOADS * DMA)
                if s_norm:
                    link(normalise(s[:, grp(g), :], s[:, grp(g), :], s_norm, s_norm[2]))
                if f_turned:
                    dve.wait_ge(f_tp, g + 1)
                    src = ftp[:]
                else:
                    src = f[:, grp(g), :]
                if picks:
                    dve.wait_ge(picks_loaded, 2 * DMA)
                    dve.wait_ge(gathered[g], 2 * GT * DMA)
                    for j, t in enumerate((f, f2)):
                        link(nc.vector.tensor_tensor(t[:, grp(g), :], t[:, grp(g), :], over(weight[:, j, grp(g)].unsqueeze(2), wide), ALU.mult))
                    ins = nc.vector.tensor_tensor(src, src, f2[:, grp(g), :], ALU.add)
                    if f_norm:
                        link(ins)
                    else:
                        ins.then_inc(f_ready, 1)
                if f_norm:
                    normalise(f[:, grp(g), :], src, f_norm, f_norm[2]).then_inc(f_ready, 1)
                elif f_turned:
                    nc.vector.tensor_copy(f[:, grp(g), :], src).then_inc(f_ready, 1)
                dve.wait_ge(gated, g + 1)
                link(nc.vector.tensor_tensor(s[:, grp(g), :], s[:, grp(g), :], gate[:], ALU.mult))
                last = nc.vector.tensor_tensor(x[:, grp(g), :], x[:, grp(g), :], s[:, grp(g), :], ALU.add)
                last.then_inc(x_ready, 1)
                dve.wait_ge(x_ready, g + 1)
                if not last_stage:
                    normalise(s[:, grp(g), :], x[:, grp(g), :], None, 1e-5).then_inc(xn_ready, 1)

        @block.tensor
        def _(pe):
            def turn_f(g):
                pe.wait_ge(loaded[g], 3 * DMA)
                if g:
                    pe.wait_ge(f_ready, g)
                for t in range(GT):
                    last = nc.tensor.transpose(ftp[:, t, :], fT[:, (g * GT + t) * P:(g * GT + t + 1) * P], ident[:])
                last.then_inc(f_tp, 1)
            for g in range(NG):
                if f_turned:
                    turn_f(g)
                if not last_stage:
                    pe.wait_ge(xn_ready, g + 1)
                    if g >= 2:
                        pe.wait_ge(evacuated, g - 1)
                    for t in range(GT):
                        last = nc.tensor.transpose(tp[:, g % 2, t * P:(t + 1) * P], s[:, g * GT + t, :], ident[:])
                    last.then_inc(turned, 1)

        @block.scalar
        def _(act):
            n = [0]

            def root():
                n[0] += 1
                act.wait_ge(var_ready, n[0])
                nc.scalar.activation(std[:], var[:], ACT.Sqrt).then_inc(std_ready, 1)
            for g in range(NG):
                if s_norm:
                    root()
                if f_norm:
                    root()
                if f_norm or f_turned or picks:
                    act.wait_ge(f_ready, g + 1)
                else:
                    act.wait_ge(loaded[g], 3 * DMA)
                if g:
                    act.wait_ge(x_ready, g)
                nc.scalar.activation(gate[:], f[:, grp(g), :], ACT.Silu).then_inc(gated, 1)
                if not last_stage:
                    root()
                    act.wait_ge(turned, g + 1)
                    if g >= 2:
                        act.wait_ge(storedT, DMA * (g - 1))
                    nc.scalar.activation(xT[:, g % 2, :], tp[:, g % 2, :], ACT.Copy).then_inc(evacuated, 1)


def routing_stage(nc, name, ident, kind, xnT_d, w, bias, c_d, cT_d):
    grouped = kind == "grouped"
    E = 32 if grouped else 8
    EP = 32
    PARTS = 3
    CAP = int(1.25 * TOK / 8)
    with Stage(nc, name) as st:
        xnT = st.sb("xnT", [P, TOK])
        wr, wT = st.sb("wr", [EP, D]), st.sb("wT", [P, E])
        bias_b = st.sb("bias_b", [P, E])
        score, pick, tmp = (st.sb(n, [P, NT, E]) for n in ("score", "pick", "tmp"))
        comb = st.sb("comb", [P, NT, EP])
        rest = st.sb("rest", [P, NT, EP])
        parts = st.sb("parts", [P, NT, PARTS, EP], BF16)
        ident16 = st.sb("ident16", [P, P], BF16)
        best = st.sb("best", [P, NT, 8])
        gs = [st.sb(f"gs{n}", [P, NT * 8]) for n in range(5)]
        pair, pair2 = st.sb("pair", [P, NT, 8, 8]), st.sb("pair2", [P, NT, 8, 8])
        before = st.sb("before", [P, 8, 8])
        rank, rank2 = st.sb("rank", [P, NT, 8]), st.sb("rank2", [P, NT, 8])
        red = st.sb("red", [P, NT])
        earlier, ones = st.sb("earlier", [P, P]), st.sb("ones", [P, P])
        cT = st.sb("cT", [PARTS * EP, TOK], BF16)
        cF = st.sb("cF", [EP, TOK])
        lg = st.ps("lg", [P, NT, EP])
        tr = st.ps("tr", [P, 2, CH])
        trb = st.ps("trb", [PARTS * EP, 2, 8, P], BF16)
        posp = st.ps("posp", [P, 2, CH])
        x_loaded, consts, made, stored = (st.sem(n) for n in ("x_loaded", "consts", "made", "stored"))
        w_turned, w_ready, logits, dve_step, act_in, act_out = (
            st.sem(n) for n in ("w_turned", "w_ready", "logits", "dve_step", "act_in", "act_out"))
        mask_ready, counted, parts_ready, f_turned, b_turned, f_copied, b_copied = (
            st.sem(n) for n in ("mask_ready", "counted", "parts_ready", "f_turned", "b_turned", "f_copied", "b_copied"))
        block = st.block()
        NCONST = 1 + (bias is not None)

        @block.sync
        def _(sp):
            sp.dma_start(wr[0:32, :] if grouped else wT[:], w).then_inc(consts, DMA)
            if bias is not None:
                sp.dma_start(bias_b[:], broadcast_rows(bias)).then_inc(consts, DMA)
            sp.dma_start(xnT[:], xnT_d[:, :]).then_inc(x_loaded, DMA)
            sp.wait_ge(f_copied, NT // 4)
            sp.dma_start(c_d[:, :], cF[:]).then_inc(stored, DMA)
            sp.wait_ge(b_copied, NT // 8)
            sp.dma_start(cT_d[:, :], cT[:]).then_inc(stored, DMA)
            sp.wait_ge(stored, 2 * DMA)

        @block.gpsimd
        def _(pool):
            nc.gpsimd.memset(before[:], 1.0).then_inc(made, 1)
            nc.gpsimd.memset(earlier[:], 1.0).then_inc(made, 1)
            nc.gpsimd.memset(ones[:], 1.0).then_inc(made, 1)
            nc.gpsimd.memset(comb[:], 0.0).then_inc(made, 1)
            nc.gpsimd.tensor_copy(ident16[:], ident[:]).then_inc(made, 1)
            pool.wait_ge(made, 5)
            nc.gpsimd.affine_select(out=before[:], in_=before[:], compare_op=ALU.is_ge, fill=0.0, base=-1,
                                    pattern=[[1, 8], [-1, 8]], channel_multiplier=0).then_inc(made, 1)
            nc.gpsimd.affine_select(out=earlier[:], in_=earlier[:], compare_op=ALU.is_ge, fill=0.0, base=-1,
                                    pattern=[[1, P]], channel_multiplier=-1).then_inc(made, 1)

        @block.tensor
        def _(pe):
            if grouped:
                pe.wait_ge(consts, NCONST * DMA)
                nc.tensor.transpose(tr[:, 0, 0:32], wr[0:32, :], ident[0:32, 0:32]).then_inc(w_turned, 1)
                pe.wait_ge(w_ready, 1)
            else:
                pe.wait_ge(consts, NCONST * DMA)
            pe.wait_ge(x_loaded, DMA)
            for t in range(NT):
                last = nc.tensor.matmul(lg[:, t, 0:E], xnT[:, t * P:(t + 1) * P], wT[:], start=True, stop=True)
            last.then_inc(logits, 1)
            if kind == "capacity":
                pe.wait_ge(mask_ready, 1)
                m = pick[:].rearrange("p t e -> p (t e)")
                nc.tensor.matmul(posp[:, 0, 0:NT * E], earlier[:], m, start=True, stop=True)
                nc.tensor.matmul(posp[:, 1, 0:NT * E], ones[:], m, start=True, stop=True).then_inc(counted, 1)
            pe.wait_ge(parts_ready, 1)
            for t in range(NT):
                if t % 4 == 0 and t >= 8:
                    pe.wait_ge(f_copied, t // 4 - 1)
                last = nc.tensor.transpose(tr[0:EP, t // 4 % 2, t % 4 * P:(t % 4 + 1) * P], comb[:, t, :], ident[:])
                if t % 4 == 3:
                    last.then_inc(f_turned, 1)
            for t in range(NT):
                if t % 8 == 0 and t >= 16:
                    pe.wait_ge(b_copied, t // 8 - 1)
                last = nc.tensor.transpose(trb[:, t // 8 % 2, t % 8, :], parts[:, t, :, :].rearrange("p a e -> p (a e)"), ident16[:])
                if t % 8 == 7:
                    last.then_inc(b_turned, 1)

        @block.scalar
        def _(act):
            if grouped:
                act.wait_ge(logits, 1)
                nc.scalar.activation(score[:], lg[:, :, 0:E], ACT.Sigmoid).then_inc(act_out, 1)
            else:
                act.wait_ge(act_in, 1)
                nc.scalar.activation(score[:], tmp[:], ACT.Exp).then_inc(act_out, 1)
            for n in range(NT // 4):
                act.wait_ge(f_turned, n + 1)
                nc.scalar.activation(cF[:, n * CH:(n + 1) * CH], tr[0:EP, n % 2, :], ACT.Copy).then_inc(f_copied, 1)

        @block.vector
        def _(dve):
            link = Chain(dve, dve_step)
            V = nc.vector
            full = [P, NT, E]
            per_tok = lambda a: over(a[:].unsqueeze(2), full)

            def ranks(src):
                four = [P, NT, 8, 8]
                vi, vj = over(src.unsqueeze(3), four), src.unsqueeze(2).to_broadcast(four)
                link(V.tensor_tensor(pair[:], vj, vi, ALU.is_gt))
                link(V.tensor_tensor(pair2[:], vj, vi, ALU.is_equal))
                flat = lambda a: a[:].rearrange("p t i j -> p t (i j)")
                link(V.tensor_tensor(flat(pair2), flat(pair2),
                                     before[:].rearrange("p i j -> p (i j)").unsqueeze(1).to_broadcast([P, NT, 64]), ALU.mult))
                link(V.tensor_tensor(flat(pair), flat(pair), flat(pair2), ALU.add))
                link(V.reduce_sum(rank[:], pair[:], AX.X))

            if grouped:
                dve.wait_ge(w_turned, 1)
                V.tensor_copy(wT[:], tr[:, 0, 0:32]).then_inc(w_ready, 1)
            dve.wait_ge(consts, NCONST * DMA)
            dve.wait_ge(made, 7)
            bias_f = bias_b[:].unsqueeze(1).to_broadcast(full)
            if grouped:
                dve.wait_ge(act_out, 1)
                link(V.tensor_tensor(tmp[:], score[:], bias_f, ALU.add))
                member = lambda j: tmp[:].rearrange("p t (g m) -> p (t g) m", m=4)[:, :, j]
                link(V.tensor_tensor(gs[0][:], member(0), member(1), ALU.max))
                link(V.tensor_tensor(gs[1][:], member(0), member(1), ALU.min))
                link(V.tensor_tensor(gs[2][:], member(2), member(3), ALU.max))
                link(V.tensor_tensor(gs[3][:], member(2), member(3), ALU.min))
                link(V.tensor_tensor(gs[1][:], gs[1][:], gs[3][:], ALU.max))
                link(V.tensor_tensor(gs[3][:], gs[0][:], gs[2][:], ALU.min))
                link(V.tensor_tensor(gs[4][:], gs[0][:], gs[2][:], ALU.max))
                link(V.tensor_tensor(gs[3][:], gs[3][:], gs[1][:], ALU.max))
                link(V.tensor_tensor(gs[0][:], gs[4][:], gs[3][:], ALU.add))
                ranks(gs[0][:].rearrange("p (t g) -> p t g", g=8))
                link(V.tensor_scalar(rank[:], rank[:], 4.0, None, ALU.is_lt))
                link(V.tensor_tensor(tmp[:].rearrange("p t (g m) -> p (t g) m", m=4), tmp[:].rearrange("p t (g m) -> p (t g) m", m=4),
                                     over(rank[:].rearrange("p t g -> p (t g)").unsqueeze(2), [P, NT * 8, 4]), ALU.mult))
                for t in range(NT):
                    last = V.max(best[:, t, :], tmp[:, t, :])
                link(last)
                TAKEN = -1e30
                for t in range(NT):
                    last = V.match_replace(pick[:, t, :], best[:, t, :], tmp[:, t, :], TAKEN)
                link(last)
                link(V.tensor_scalar(pick[:], pick[:], TAKEN / 2, None, ALU.is_lt))
                link(V.tensor_tensor(pick[:], pick[:], score[:], ALU.mult))
                link(V.reduce_sum(red[:], pick[:], AX.X))
                link(V.tensor_scalar(red[:], red[:], 1e-20, None, ALU.add))
                link(V.reciprocal(red[:], red[:]))
                link(V.tensor_scalar(red[:], red[:], 2.5, None, ALU.mult))
                link(V.tensor_tensor(comb[:], pick[:], per_tok(red), ALU.mult))
            else:
                dve.wait_ge(logits, 1)
                link(V.tensor_tensor(score[:], lg[:, :, 0:E], bias_f, ALU.add))
                link(V.reduce_max(red[:], score[:], AX.X))
                V.tensor_tensor(tmp[:], score[:], per_tok(red), ALU.subtract).then_inc(act_in, 1)
                dve.wait_ge(act_out, 1)
                link(V.reduce_sum(red[:], score[:], AX.X))
                link(V.reciprocal(red[:], red[:]))
                link(V.tensor_tensor(score[:], score[:], per_tok(red), ALU.mult))
                ranks(score[:])
                ins = V.tensor_scalar(pick[:], rank[:], 2.0, None, ALU.is_lt)
                if kind == "capacity":
                    ins.then_inc(mask_ready, 1)
                    dve.wait_ge(mask_ready, 1)
                    dve.wait_ge(counted, 1)
                    flat = lambda a: a[:].rearrange("p t e -> p (t e)")
                    a, b = rank, rank2
                    link(V.memset(a[:, 0, :], 0.0))
                    link(V.tensor_copy(a[:, 1:NT, :], posp[:, 1, 0:NT * E].rearrange("p (t e) -> p t e", e=E)[:, 0:NT - 1, :]))
                    step = 1
                    while step < NT:
                        link(V.tensor_copy(b[:, 0:step, :], a[:, 0:step, :]))
                        link(V.tensor_tensor(b[:, step:NT, :], a[:, step:NT, :], a[:, 0:NT - step, :], ALU.add))
                        a, b = b, a
                        step *= 2
                    link(V.tensor_tensor(flat(a), posp[:, 0, 0:NT * E], flat(a), ALU.add))
                    link(V.tensor_scalar(a[:], a[:], float(CAP), None, ALU.is_lt))
                    ins = V.tensor_tensor(pick[:], pick[:], a[:], ALU.mult)
                link(ins)
                link(V.tensor_tensor(pick[:], pick[:], score[:], ALU.mult))
                link(V.reduce_sum(red[:], pick[:], AX.X))
                if kind == "capacity":
                    link(V.tensor_scalar(red[:], red[:], 1e-6, None, ALU.max))
                else:
                    link(V.tensor_scalar(red[:], red[:], 1e-8, None, ALU.add))
                link(V.reciprocal(red[:], red[:]))
                link(V.tensor_tensor(comb[:, :, 0:E], pick[:], per_tok(red), ALU.mult))
            link(V.tensor_copy(parts[:, :, 0, :], comb[:]))
            link(V.tensor_tensor(rest[:], comb[:], parts[:, :, 0, :], ALU.subtract))
            link(V.tensor_copy(parts[:, :, 1, :], rest[:]))
            link(V.tensor_tensor(rest[:], rest[:], parts[:, :, 1, :], ALU.subtract))
            V.tensor_copy(parts[:, :, 2, :], rest[:]).then_inc(parts_ready, 1)
            for n in range(NT // 8):
                dve.wait_ge(b_turned, n + 1)
                V.tensor_copy(cT[:, n * 8 * P:(n + 1) * 8 * P].rearrange("r (t p) -> r t p", p=P), trb[:, n % 2, :, :]).then_inc(b_copied, 1)


def experts_stage(nc, name, ident, kind, xnT_d, c_d, cT_d, weights, fT_d):
    silu = kind == "silu"
    E = 32 if silu else 8
    HT = 17 if silu else 32
    NSEL = 16 if silu else 8
    with Stage(nc, name) as st:
        xnT = st.sb("xnT", [P, TOK])
        cT = st.sb("cT", [96, TOK], BF16)
        cF = st.sb("cF", [32, TOK])
        sel = st.sb("sel", [96, NSEL * P], BF16)
        up_w = [st.sb(f"up_w{n}", [P, HT * P]) for n in range(2 if silu else 1)]
        down_w = st.sb("down_w", [P, HT, D])
        raw = st.sb("raw", [P, HT, P]) if silu else None
        b1r, b1 = st.sb("b1r", [32, P]), st.sb("b1", [P, 32])
        b2 = st.sb("b2", [8, D])
        a = st.sb("a", [P, 2, CH])
        g = st.sb("g", [P, 2, CH])
        h = st.sb("h", [P, 2, CH])
        out = st.sb("out", [P, 2, CH])
        up = [st.ps(f"up{n}", [P, 2, CH]) for n in range(2 if silu else 1)]
        rep = st.ps("rep", [P, 2, CH])
        acc = st.ps("acc", [P, CH])
        x_loaded, made, acted, tmp_ready, mixed, summed, copied = (
            st.sem(n) for n in ("x_loaded", "made", "acted", "tmp_ready", "mixed", "summed", "copied"))
        first_up, second_up, repeated, w_turned, w_copied, sel_made = (
            st.sem(n) for n in ("first_up", "second_up", "repeated", "w_turned", "w_copied", "sel_made"))
        consts = [st.sem(f"consts{n}") for n in range(3)]
        stored = [st.sem(f"stored{n}") for n in range(2)]
        block = st.block()
        XLOADS = 2 if silu else 3

        def iterations(eng, body):
            body(0, 0, True)
            body(1, 1, False)
            with eng.Fori(1, NCH // 2) as j:
                body(2 * j, 0, False)
                body(2 * j + 1, 1, False)

        @block.sync
        def _(sp):
            if silu:
                w_gate, w_up, w_down, sh_gate, sh_up, sh_down = weights
                for n, (src, sh) in enumerate(((w_gate, sh_gate), (w_up, sh_up), (w_down, sh_down))):
                    if n:
                        sp.wait_ge(w_copied, 5 * n)
                    if n < 2:
                        sp.dma_start(raw[:, 0:HT - 1, :], src.rearrange("(k e) i h -> (e i) k h", e=2)).then_inc(consts[n], DMA)
                    else:
                        sp.dma_start(raw[:, 0:HT - 1, :].rearrange("h k (e i) -> h (k e) i", e=2),
                                     src.rearrange("e h i -> h e i")).then_inc(consts[n], DMA)
                    sp.dma_start(raw[:, HT - 1, :], sh).then_inc(consts[n], DMA)
            else:
                w1, b1_d, w2, b2_d = weights
                sp.dma_start(b1r[:], b1_d.rearrange("e (k p) -> (e k) p", p=P)).then_inc(consts[0], DMA)
                sp.dma_start(up_w[0][:].rearrange("d (e f) -> d e f", e=E), w1.rearrange("e d f -> d e f")).then_inc(consts[1], DMA)
                sp.dma_start(b2[:], b2_d).then_inc(consts[1], DMA)
                sp.dma_start(down_w[:], w2.rearrange("e (k p) d -> p (e k) d", p=P)).then_inc(consts[2], DMA)
            sp.dma_start(xnT[:], xnT_d[:, :]).then_inc(x_loaded, DMA)
            sp.dma_start(cT[:], cT_d[:, :]).then_inc(x_loaded, DMA)
            if not silu:
                sp.dma_start(cF[:], c_d[:, :]).then_inc(x_loaded, DMA)

            def body(i, slot, first):
                sp.wait_ge(copied, i + 1)
                sp.dma_start(fT_d[:, bass.ds(i * CH, CH)], out[:, slot, :]).then_inc(stored[slot], DMA)
            iterations(sp, body)
            for s in range(2):
                sp.wait_ge(stored[s], DMA * NCH // 2)

        @block.gpsimd
        def _(pool):
            width = P // 2 if silu else P
            nc.gpsimd.memset(sel[:], 1.0).then_inc(made, 1)
            n = 1
            for part in range(3):
                own = sel[32 * part:32 * part + 32, :]
                for sign, base in ((1, 0), (-1, width - 1)):
                    pool.wait_ge(made, n)
                    nc.gpsimd.affine_select(out=own, in_=own, compare_op=ALU.is_ge, fill=0.0, base=base,
                                            pattern=[[sign, NSEL * P]], channel_multiplier=-sign * width).then_inc(made, 1)
                    n += 1

        @block.tensor
        def _(pe):
            if silu:
                n = 0
                for m in range(3):
                    pe.wait_ge(consts[m], 2 * DMA)
                    for t in range(HT):
                        if t % 4 == 0 and n >= 2:
                            pe.wait_ge(w_copied, n - 1)
                        last = nc.tensor.transpose(up[0][:, n % 2, t % 4 * P:(t % 4 + 1) * P], raw[:, t, :], ident[:])
                        if t % 4 == 3 or t == HT - 1:
                            last.then_inc(w_turned, 1)
                            n += 1
                pe.wait_ge(w_copied, n)
            else:
                pe.wait_ge(consts[0], DMA)
                nc.tensor.transpose(up[0][:, 0, 0:32], b1r[:], ident[0:32, 0:32]).then_inc(w_turned, 1)
                pe.wait_ge(w_copied, 1)
                pe.wait_ge(consts[1], 2 * DMA)
                pe.wait_ge(consts[2], DMA)
            pe.wait_ge(made, 7)
            pe.wait_ge(x_loaded, XLOADS * DMA)

            def down(i, slot, k):
                pe.wait_ge(mixed, i * HT + k + 1)
                if k == 0 and not (isinstance(i, int) and i == 0):
                    pe.wait_ge(copied, i)
                ins = nc.tensor.matmul(acc[:], down_w[:, k, :], h[:, (slot * HT + k) % 2, :],
                                       start=(k == 0), stop=(silu and k == HT - 1))
                return ins

            def body(i, slot, first):
                tok = bass.ds(i * CH, CH)
                for k in range(HT):
                    s = (slot * HT + k) % 2
                    n = i * HT + k
                    if not (first and k < 2):
                        pe.wait_ge(acted, n - 1)
                    nc.tensor.matmul(up[0][:, s, :], up_w[0][:, k * P:(k + 1) * P], xnT[:, tok],
                                     start=True, stop=True).then_inc(first_up, 1)
                    if silu:
                        if not (first and k < 2):
                            pe.wait_ge(mixed, n - 1)
                        ins = nc.tensor.matmul(up[1][:, s, :], up_w[1][:, k * P:(k + 1) * P], xnT[:, tok], start=True, stop=True)
                        if k < NSEL:
                            ins = nc.tensor.matmul(rep[:, s, :], sel[:, k * P:(k + 1) * P], cT[:, tok], start=True, stop=True)
                        ins.then_inc(second_up, 1)
                    elif k % 4 == 0:
                        e = k // 4
                        if not (first and e < 2):
                            pe.wait_ge(mixed, n - 4)
                        nc.tensor.matmul(rep[:, e % 2, :], sel[:, e * P:(e + 1) * P], cT[:, tok],
                                         start=True, stop=True).then_inc(second_up, 1)
                    if k:
                        down(i, slot, k - 1)
                ins = down(i, slot, HT - 1)
                if not silu:
                    ins = nc.tensor.matmul(acc[:], b2[:], cF[0:8, tok], start=False, stop=True)
                ins.then_inc(summed, 1)

            iterations(pe, body)

        @block.scalar
        def _(act):
            if silu:
                n = 0
                for m, dst in enumerate((up_w[0][:], up_w[1][:], down_w[:].rearrange("p k d -> p (k d)"))):
                    for t in range(0, HT, 4):
                        width = min(4, HT - t) * P
                        act.wait_ge(w_turned, n + 1)
                        nc.scalar.activation(dst[:, t * P:t * P + width], up[0][:, n % 2, 0:width], ACT.Copy).then_inc(w_copied, 1)
                        n += 1
            else:
                act.wait_ge(w_turned, 1)
                nc.scalar.activation(b1[:], up[0][:, 0, 0:32], ACT.Copy).then_inc(w_copied, 1)
                act.wait_ge(w_copied, 1)

            def body(i, slot, first):
                for k in range(HT):
                    s = (slot * HT + k) % 2
                    n = i * HT + k
                    act.wait_ge(first_up, n + 1)
                    if not (first and k < 2):
                        act.wait_ge(mixed, n - 1)
                    if silu:
                        ins = nc.scalar.activation(a[:, s, :], up[0][:, s, :], ACT.Silu)
                    else:
                        ins = nc.scalar.activation(a[:, s, :], up[0][:, s, :], ACT.Gelu, bias=b1[:, k:k + 1])
                    ins.then_inc(acted, 1)
                act.wait_ge(summed, i + 1)
                if not first and not (isinstance(i, int) and i < 2):
                    act.wait_ge(stored[slot], DMA * ((i - slot) // 2))
                nc.scalar.activation(out[:, slot, :], acc[:], ACT.Copy).then_inc(copied, 1)
            iterations(act, body)

        @block.vector
        def _(dve):
            def body(i, slot, first):
                for k in range(HT):
                    s = (slot * HT + k) % 2
                    n = i * HT + k
                    dve.wait_ge(acted, n + 1)
                    if silu:
                        dve.wait_ge(second_up, n + 1)
                        if k < NSEL:
                            nc.vector.tensor_tensor(g[:, s, :], up[1][:, s, :], a[:, s, :], ALU.mult).then_inc(tmp_ready, 1)
                            dve.wait_ge(tmp_ready, i * NSEL + k + 1)
                            ins = nc.vector.tensor_tensor(h[:, s, :], rep[:, s, :], g[:, s, :], ALU.mult)
                        else:
                            ins = nc.vector.tensor_tensor(h[:, s, :], up[1][:, s, :], a[:, s, :], ALU.mult)
                    else:
                        dve.wait_ge(second_up, i * NSEL + k // 4 + 1)
                        ins = nc.vector.tensor_tensor(h[:, s, :], rep[:, k // 4 % 2, :], a[:, s, :], ALU.mult)
                    ins.then_inc(mixed, 1)
            iterations(dve, body)


def dispatch_stage(nc, name, kind, xn_d, xnT_d, w, bias, blocks, xs_d, idx_d, weight_d, expert_d):
    E = 8
    capacity = kind == "capacity"
    CAP = int(1.25 * TOK / E)
    SLOTS = blocks * P
    FAR = 65536.0
    NZ = 4
    with Stage(nc, name) as st:
        xnT, xn = st.sb("xnT", [P, TOK]), st.sb("xn", [P, NT, D])
        zero = st.sb("zero", [P, blocks // NZ * D])
        wr, bias_b = st.sb("wr", [P, E]), st.sb("bias_b", [P, E])
        full = [P, NT, E]
        score, shifted, mask, hot, weight, keep, rank, place, place2 = (
            st.sb(n, full) for n in ("score", "shifted", "mask", "hot", "weight", "keep", "rank", "place", "place2"))
        pair, pair2 = st.sb("pair", [P, NT, E, E]), st.sb("pair2", [P, NT, E, E])
        before = st.sb("before", [P, E, E])
        earlier, ones = st.sb("earlier", [P, P]), st.sb("ones", [P, P])
        red = st.sb("red", [P, NT])
        count, room, start, end = (st.sb(n, [P, E]) for n in ("count", "room", "start", "end"))
        begun = st.sb("begun", [P, E, NT])
        spread = st.sb("spread", [P, E, E])
        slot, kept, send = (st.sb(n, [P, 2, NT]) for n in ("slot", "kept", "send"))
        wsel = st.sb("wsel", [P, 2, NT])
        send_i, slot_i = st.sb("send_i", [P, 2, NT], I32), st.sb("slot_i", [P, 2, NT], I32)
        first_i, first = st.sb("first_i", [P, blocks], I32), st.sb("first", [P, blocks])
        past, owner, owner_i = st.sb("past", [1, blocks, E]), st.sb("owner", [1, blocks]), st.sb("owner_i", [1, blocks], I32)
        lg = st.ps("lg", [P, NT, E])
        ranked = st.ps("ranked", [P, NT, E])
        tallied = st.ps("tallied", [P, NT, E])
        names = ("x_loaded", "consts", "made", "zero_made", "zeroed", "logits", "shifted_ready", "exped", "dve_step", "mask_ready",
                 "counted", "send_ready", "sent", "maps_ready", "stored", "xn_loaded")
        (x_loaded, consts, made, zero_made, zeroed, logits, shifted_ready, exped, dve_step, mask_ready, counted, send_ready, sent,
         maps_ready, stored, xn_loaded) = (st.sem(n) for n in names)
        block = st.block()

        @block.sync
        def _(sp):
            sp.dma_start(wr[:], w).then_inc(consts, DMA)
            sp.dma_start(bias_b[:], broadcast_rows(bias)).then_inc(consts, DMA)
            sp.dma_start(xnT[:], xnT_d[:, :]).then_inc(x_loaded, DMA)
            sp.dma_start(xn[:], rows(xn_d)).then_inc(xn_loaded, DMA)
            sp.wait_ge(zero_made, 1)
            for n in range(NZ):
                sp.dma_start(xs_d.rearrange("(n p r) d -> n p (r d)", n=NZ, p=P)[n], zero[:]).then_inc(zeroed, DMA)
            sp.wait_ge(maps_ready, 3)
            for dst, src in ((idx_d, slot_i), (weight_d, wsel), (expert_d, owner_i)):
                sp.dma_start(dst[:], src[:]).then_inc(stored, DMA)
            sp.wait_ge(stored, 3 * DMA)

        @block.gpsimd
        def _(pool):
            nc.gpsimd.memset(before[:], 1.0).then_inc(made, 1)
            nc.gpsimd.memset(earlier[:], 1.0).then_inc(made, 1)
            nc.gpsimd.memset(ones[:], 1.0).then_inc(made, 1)
            nc.gpsimd.iota(first_i[:], [[P, blocks]], base=0, channel_multiplier=0).then_inc(made, 1)
            pool.wait_ge(made, 4)
            nc.gpsimd.affine_select(out=before[:], in_=before[:], compare_op=ALU.is_ge, fill=0.0, base=-1,
                                    pattern=[[1, E], [-1, E]], channel_multiplier=0).then_inc(made, 1)
            nc.gpsimd.affine_select(out=earlier[:], in_=earlier[:], compare_op=ALU.is_ge, fill=0.0, base=-1,
                                    pattern=[[1, P]], channel_multiplier=-1).then_inc(made, 1)
            pool.wait_ge(xn_loaded, DMA)
            pool.wait_ge(zeroed, NZ * DMA)
            pool.wait_ge(send_ready, 1)
            for j in range(2):
                for t in range(NT):
                    pool.indirect_dma_start(out=xs_d[:, :], out_offset=bass.IndirectOffsetOnAxis(
                                                ap=send_i[:, j, t:t + 1].bitcast(U32), axis=0),
                                            in_=xn[:, t, :], in_offset=None, bounds_check=SLOTS - 1, oob_is_err=False).then_inc(sent, DMA)
            pool.wait_ge(sent, 2 * NT * DMA)

        @block.tensor
        def _(pe):
            mm = nc.tensor.matmul
            pe.wait_ge(consts, 2 * DMA)
            pe.wait_ge(x_loaded, DMA)
            for t in range(NT):
                last = mm(lg[:, t, :], xnT[:, t * P:(t + 1) * P], wr[:], start=True, stop=True)
            last.then_inc(logits, 1)
            pe.wait_ge(mask_ready, 1)
            flat = lambda a: a[:].rearrange("p t e -> p (t e)")
            mm(flat(ranked), earlier[:], flat(mask), start=True, stop=True)
            mm(flat(tallied), ones[:], flat(mask), start=True, stop=True).then_inc(counted, 1)

        @block.scalar
        def _(act):
            act.wait_ge(shifted_ready, 1)
            nc.scalar.activation(score[:], shifted[:], ACT.Exp).then_inc(exped, 1)

        @block.vector
        def _(dve):
            V = nc.vector
            link = Chain(dve, dve_step)
            per_tok = lambda a: over(a[:].unsqueeze(2), full)
            per_expert = lambda a: a[:].unsqueeze(1).to_broadcast(full)
            four = [P, NT, E, E]
            V.memset(zero[:], 0.0).then_inc(zero_made, 1)
            dve.wait_ge(consts, 2 * DMA)
            dve.wait_ge(made, 6)
            link(V.tensor_copy(first[:], first_i[:]))
            dve.wait_ge(logits, 1)
            link(V.tensor_tensor(score[:], lg[:], per_expert(bias_b), ALU.add))
            link(V.reduce_max(red[:], score[:], AX.X))
            V.tensor_tensor(shifted[:], score[:], per_tok(red), ALU.subtract).then_inc(shifted_ready, 1)
            dve.wait_ge(exped, 1)
            link(V.reduce_sum(red[:], score[:], AX.X))
            link(V.reciprocal(red[:], red[:]))
            link(V.tensor_tensor(score[:], score[:], per_tok(red), ALU.mult))
            si, sj = over(score[:].unsqueeze(3), four), score[:].unsqueeze(2).to_broadcast(four)
            flat = lambda a: a[:].rearrange("p t i j -> p t (i j)")
            link(V.tensor_tensor(pair2[:], sj, si, ALU.is_equal))
            link(V.tensor_tensor(flat(pair2), flat(pair2),
                                 before[:].rearrange("p i j -> p (i j)").unsqueeze(1).to_broadcast([P, NT, E * E]), ALU.mult))
            link(V.tensor_tensor(pair[:], sj, si, ALU.is_gt))
            link(V.tensor_tensor(flat(pair), flat(pair), flat(pair2), ALU.add))
            link(V.reduce_sum(rank[:], pair[:], AX.X))
            V.tensor_scalar(mask[:], rank[:], 2.0, None, ALU.is_lt).then_inc(mask_ready, 1)
            dve.wait_ge(mask_ready, 1)
            dve.wait_ge(counted, 1)
            a, b = place, place2
            link(V.memset(a[:, 0, :], 0.0))
            link(V.tensor_copy(a[:, 1:NT, :], tallied[:, 0:NT - 1, :]))
            step = 1
            while step < NT:
                link(V.tensor_copy(b[:, 0:step, :], a[:, 0:step, :]))
                link(V.tensor_tensor(b[:, step:NT, :], a[:, step:NT, :], a[:, 0:NT - step, :], ALU.add))
                a, b = b, a
                step *= 2
            if capacity:
                link(V.memset(room[:], float(CAP)))
            else:
                link(V.tensor_tensor(count[:], a[:, NT - 1, :], tallied[:, NT - 1, :], ALU.add))
                link(V.tensor_tensor(begun[:], first[:, 0:NT].unsqueeze(1).to_broadcast([P, E, NT]), over(count[:].unsqueeze(2), [P, E, NT]),
                                     ALU.is_lt))
                link(V.reduce_sum(room[:], begun[:], AX.X))
                link(V.tensor_scalar(room[:], room[:], float(P), None, ALU.mult))
            link(V.tensor_tensor(spread[:], before[:], room[:].unsqueeze(1).to_broadcast([P, E, E]), ALU.mult))
            link(V.reduce_sum(start[:], spread[:], AX.X))
            link(V.tensor_tensor(end[:], start[:], room[:], ALU.add))
            link(V.tensor_tensor(a[:], ranked[:], a[:], ALU.add))
            if capacity:
                link(V.tensor_scalar(keep[:], a[:], float(CAP), None, ALU.is_lt))
                link(V.tensor_tensor(mask[:], mask[:], keep[:], ALU.mult))
            link(V.tensor_tensor(a[:], a[:], per_expert(start), ALU.add))
            for j in range(2):
                link(V.tensor_scalar(hot[:], rank[:], float(j), None, ALU.is_equal))
                link(V.tensor_tensor(shifted[:], hot[:], a[:], ALU.mult))
                link(V.reduce_sum(slot[:, j, :], shifted[:], AX.X))
                if capacity:
                    link(V.tensor_tensor(shifted[:], hot[:], keep[:], ALU.mult))
                    link(V.reduce_sum(kept[:, j, :], shifted[:], AX.X))
            if capacity:
                link(V.tensor_scalar(send[:], kept[:], -FAR, FAR, ALU.mult, ALU.add))
                link(V.tensor_tensor(send[:], send[:], slot[:], ALU.add))
                link(V.tensor_scalar(slot[:], slot[:], SLOTS - 1.0, None, ALU.min))
            else:
                link(V.tensor_copy(send[:], slot[:]))
            V.tensor_copy(send_i[:], send[:]).then_inc(send_ready, 1)
            V.tensor_copy(slot_i[:], slot[:]).then_inc(maps_ready, 1)
            link(V.tensor_tensor(weight[:], mask[:], score[:], ALU.mult))
            link(V.reduce_sum(red[:], weight[:], AX.X))
            if capacity:
                link(V.tensor_scalar(red[:], red[:], 1e-6, None, ALU.max))
            else:
                link(V.tensor_scalar(red[:], red[:], 1e-8, None, ALU.add))
            link(V.reciprocal(red[:], red[:]))
            link(V.tensor_tensor(weight[:], weight[:], per_tok(red), ALU.mult))
            for j in range(2):
                link(V.tensor_scalar(hot[:], rank[:], float(j), None, ALU.is_equal))
                link(V.tensor_tensor(shifted[:], hot[:], weight[:], ALU.mult))
                last = V.reduce_sum(wsel[:, j, :], shifted[:], AX.X)
            last.then_inc(maps_ready, 1)
            link(V.tensor_tensor(past[:], over(first[0:1, :].unsqueeze(2), [1, blocks, E]), end[0:1, :].unsqueeze(1).to_broadcast([1, blocks, E]),
                                 ALU.is_ge))
            link(V.reduce_sum(owner[:], past[:], AX.X))
            link(V.tensor_scalar(owner[:], owner[:], E - 1.0, None, ALU.min))
            V.tensor_copy(owner_i[:], owner[:]).then_inc(maps_ready, 1)


def sorted_experts_stage(nc, name, ident, blocks, xs_d, expert_d, weights, y_d):
    E = 8
    F = 4 * D
    FT = F // P
    UNROLL = 4
    NL = blocks // UNROLL
    assert blocks % UNROLL == 0 and NL >= 3
    with Stage(nc, name) as st:
        x, y = st.sb("x", [P, UNROLL, D]), st.sb("y", [P, blocks, D])
        w1, w2 = st.sb("w1", [P, E * F]), st.sb("w2", [P, E * FT * D])
        b1, b2 = st.sb("b1", [P, E * F]), st.sb("b2", [P, E * D])
        expert = st.sb("expert", [1, blocks], I32)
        xT = st.sb("xT", [P, 2, P])
        pre, hid = st.sb("pre", [P, 2, F]), st.sb("hid", [P, 2, F])
        hidT = st.sb("hidT", [P, 2, F])
        xt = st.ps("xt", [P, 2, CH])
        up = st.ps("up", [P, 2, F])
        ht = st.ps("ht", [P, 2, F])
        out = st.ps("out", [P, 2, CH])
        names = ("consts", "x_turned", "x_copied", "projected", "biased", "gelu_done", "h_turned", "h_copied", "summed", "y_ready")
        (consts, x_turned, x_copied, projected, biased, gelu_done, h_turned, h_copied, summed, y_ready) = (st.sem(n) for n in names)
        stored, loaded = st.sem("stored"), [st.sem(f"loaded{u}") for u in range(UNROLL)]
        block = st.block()
        NCONST = 5

        def iterations(eng, body):
            for u in range(UNROLL):
                body(u, u, True, False)
            with eng.Fori(1, NL - 1) as j:
                for u in range(UNROLL):
                    body(UNROLL * j + u, u, False, False)
            for u in range(UNROLL):
                body(blocks - UNROLL + u, u, False, True)

        @block.sync
        def _(sp):
            sp.dma_start(expert[:], expert_d[:]).then_inc(consts, DMA)
            for n in range(UNROLL):
                sp.dma_start(x[:, n, :], xs_d[n * P:(n + 1) * P, :]).then_inc(loaded[n], DMA)
            w1_d, b1_d, w2_d, b2_d = weights
            sp.dma_start(w1[:].rearrange("d (e f) -> d e f", e=E), w1_d.rearrange("e d f -> d e f")).then_inc(consts, DMA)
            sp.dma_start(b1[:], broadcast_rows(b1_d.rearrange("e f -> (e f)"))).then_inc(consts, DMA)
            sp.dma_start(w2[:].rearrange("p (k d) -> p k d", d=D), w2_d.rearrange("e (k p) d -> p (e k) d", p=P)).then_inc(consts, DMA)
            sp.dma_start(b2[:], broadcast_rows(b2_d.rearrange("e d -> (e d)"))).then_inc(consts, DMA)
            with sp.Fori(1, NL) as l:
                for u in range(UNROLL):
                    sp.wait_ge(x_turned, UNROLL * (l - 1) + u + 1)
                    sp.dma_start(x[:, u, :], xs_d[bass.ds((UNROLL * l + u) * P, P), :]).then_inc(loaded[u], DMA)

        @block.gpsimd
        def _(pool):
            with pool.Fori(0, NL) as l:
                pool.wait_ge(y_ready, UNROLL * (l + 1))
                pool.dma_start(rows(y_d)[:, bass.ds(l * UNROLL, UNROLL), :], y[:, bass.ds(l * UNROLL, UNROLL), :]).then_inc(stored, DMA)
            pool.wait_ge(stored, DMA * NL)

        def expert_of(eng, n):
            return eng.value_load(expert[0:1, bass.ds(n, 1)], min_val=0, max_val=E - 1)

        @block.tensor
        def _(pe):
            mm = nc.tensor.matmul

            def turn_x(n, u, any_before):
                pe.wait_ge(loaded[u], DMA * ((n - u) // UNROLL + 1))
                if any_before:
                    pe.wait_ge(x_copied, n - 1)
                nc.tensor.transpose(xt[:, u % 2, 0:P], x[:, u, :], ident[:]).then_inc(x_turned, 1)

            def project(n, s, any_before):
                e = expert_of(pe, n)
                pe.wait_ge(x_copied, n + 1)
                if any_before:
                    pe.wait_ge(biased, n - 1)
                mm(up[:, s, :], xT[:, s, :], w1[:, bass.ds(e * F, F)], start=True, stop=True).then_inc(projected, 1)

            def turn_h(n, s, any_before):
                pe.wait_ge(gelu_done, n + 1)
                if any_before:
                    pe.wait_ge(h_copied, n - 1)
                for k in range(FT):
                    last = nc.tensor.transpose(ht[:, s, k * P:(k + 1) * P], hid[:, s, k * P:(k + 1) * P], ident[:])
                last.then_inc(h_turned, 1)

            def down(n, s, any_before):
                e = expert_of(pe, n)
                pe.wait_ge(h_copied, n + 1)
                if any_before:
                    pe.wait_ge(y_ready, n - 1)
                for k in range(FT):
                    last = mm(out[:, s, 0:D], hidT[:, s, k * P:(k + 1) * P], w2[:, bass.ds(e * F + k * D, D)], start=(k == 0), stop=(k == FT - 1))
                last.then_inc(summed, 1)

            def body(n, u, first, final):
                s = u % 2
                if not (final and u >= UNROLL - 2):
                    turn_x(n + 2, (u + 2) % UNROLL, True)
                if not (final and u == UNROLL - 1):
                    project(n + 1, 1 - s, not (first and u == 0))
                turn_h(n, s, not (first and u < 2))
                if not (first and u == 0):
                    down(n - 1, 1 - s, not (first and u < 3))

            pe.wait_ge(consts, NCONST * DMA)
            turn_x(0, 0, False)
            turn_x(1, 1, False)
            project(0, 0, False)
            iterations(pe, body)
            down(blocks - 1, 1, True)

        @block.scalar
        def _(act):
            def copy_x(n, s, any_before):
                act.wait_ge(x_turned, n + 1)
                if any_before:
                    act.wait_ge(projected, n - 1)
                nc.scalar.activation(xT[:, s, :], xt[:, s, 0:P], ACT.Copy).then_inc(x_copied, 1)

            def body(n, u, first, final):
                s = u % 2
                act.wait_ge(biased, n + 1)
                if not (first and u < 2):
                    act.wait_ge(h_turned, n - 1)
                nc.scalar.activation(hid[:, s, :], pre[:, s, :], ACT.Gelu).then_inc(gelu_done, 1)
                if not (final and u >= UNROLL - 2):
                    copy_x(n + 2, s, True)
                act.wait_ge(h_turned, n + 1)
                if not (first and u < 2):
                    act.wait_ge(summed, n - 1)
                nc.scalar.activation(hidT[:, s, :], ht[:, s, :], ACT.Copy).then_inc(h_copied, 1)

            copy_x(0, 0, False)
            copy_x(1, 1, False)
            iterations(act, body)

        @block.vector
        def _(dve):
            V = nc.vector

            def add_bias(n, s, any_before):
                e = expert_of(dve, n)
                dve.wait_ge(projected, n + 1)
                if any_before:
                    dve.wait_ge(gelu_done, n - 1)
                V.tensor_tensor(pre[:, s, :], up[:, s, :], b1[:, bass.ds(e * F, F)], ALU.add).then_inc(biased, 1)

            def finish(n, s):
                e = expert_of(dve, n)
                dve.wait_ge(summed, n + 1)
                V.tensor_tensor(y[:, bass.ds(n, 1), :].rearrange("p a d -> p (a d)"), out[:, s, 0:D], b2[:, bass.ds(e * D, D)],
                                ALU.add).then_inc(y_ready, 1)

            def body(n, u, first, final):
                s = u % 2
                if not (final and u == UNROLL - 1):
                    add_bias(n + 1, 1 - s, not (first and u == 0))
                if not (first and u == 0):
                    finish(n - 1, 1 - s)

            dve.wait_ge(consts, NCONST * DMA)
            add_bias(0, 0, False)
            iterations(dve, body)
            finish(blocks - 1, 1)


def column(vec):
    return vec.rearrange("(p a) -> p a", a=1)


def project_l1(nc, xnT_d, w_qkv, b_qkv, q_d, k_d, v_d):
    HEADS, HD, GROUP = 16, 8, 4
    with Stage(nc, "proj1") as st:
        xnT = st.sb("xnT", [P, TOK])
        w, b_col, bv_b = st.sb("w", [P, 3 * D]), st.sb("b_col", [P, 2]), st.sb("bv_b", [P, D])
        full, rest = st.sb("full", [P, 2, CH]), st.sb("rest", [P, 2, CH])
        part = [st.sb(f"part{n}", [P, 2, TOK], BF16) for n in range(3)]
        v = st.sb("v", [P, NT, D])
        ps = st.ps("ps", [P, 4, CH])
        x_loaded, consts, made, full_ready, step, parts_ready, v_ready, stored = (
            st.sem(n) for n in ("x_loaded", "consts", "made", "full_ready", "step", "parts_ready", "v_ready", "stored"))
        block = st.block()

        @block.sync
        def _(sp):
            sp.dma_start(w[:], w_qkv).then_inc(consts, DMA)
            for j in range(2):
                sp.dma_start(b_col[:, j:j + 1], column(b_qkv[j * D:(j + 1) * D])).then_inc(consts, DMA)
            sp.dma_start(bv_b[:], broadcast_rows(b_qkv[2 * D:3 * D])).then_inc(consts, DMA)
            sp.dma_start(xnT[:], xnT_d[:, :]).then_inc(x_loaded, DMA)
            n = 0
            for j, dst in enumerate((q_d, k_d)):
                sp.wait_ge(parts_ready, NCH * (j + 1))
                for which in range(3):
                    sp.dma_start(dst[which], part[which][:, j, :]).then_inc(stored, DMA)
                    n += 1
            sp.wait_ge(v_ready, NCH)
            for g in range(HEADS // GROUP):
                sp.dma_start(v_d[g].rearrange("(t p) e -> p t e", p=P), v[:, :, g * GROUP * HD:(g + 1) * GROUP * HD]).then_inc(stored, DMA)
                n += 1
            sp.wait_ge(stored, DMA * n)

        @block.tensor
        def _(pe):
            pe.wait_ge(consts, 4 * DMA)
            pe.wait_ge(x_loaded, DMA)
            for n in range(3 * NCH):
                j, c = divmod(n, NCH)
                if n >= 4:
                    if (n - 4) // NCH < 2:
                        pe.wait_ge(full_ready, n - 3)
                    else:
                        pe.wait_ge(v_ready, n - 4 - 2 * NCH + 1)
                if j < 2:
                    last = nc.tensor.matmul(ps[:, n % 4, :], w[:, j * D:(j + 1) * D], xnT[:, c * CH:(c + 1) * CH],
                                            start=True, stop=True)
                else:
                    for t in range(TPC):
                        last = nc.tensor.matmul(ps[:, n % 4, t * P:(t + 1) * P], xnT[:, (c * TPC + t) * P:(c * TPC + t + 1) * P],
                                                w[:, 2 * D:3 * D], start=True, stop=True)
                last.then_inc(made, 1)

        @block.scalar
        def _(act):
            act.wait_ge(consts, 4 * DMA)
            for n in range(2 * NCH):
                act.wait_ge(made, n + 1)
                if n >= 2:
                    act.wait_ge(parts_ready, n - 1)
                nc.scalar.activation(full[:, n % 2, :], ps[:, n % 4, :], ACT.Identity,
                                     bias=b_col[:, n // NCH:n // NCH + 1]).then_inc(full_ready, 1)

        @block.vector
        def _(dve):
            link = Chain(dve, step)
            V = nc.vector
            dve.wait_ge(consts, 4 * DMA)
            for n in range(2 * NCH):
                j, c = divmod(n, NCH)
                cols = slice(c * CH, (c + 1) * CH)
                x, r = full[:, n % 2, :], rest[:, n % 2, :]
                dve.wait_ge(full_ready, n + 1)
                link(V.tensor_copy(part[0][:, j, cols], x))
                link(V.tensor_tensor(r, x, part[0][:, j, cols], ALU.subtract))
                link(V.tensor_copy(part[1][:, j, cols], r))
                V.tensor_tensor(part[2][:, j, cols], r, part[1][:, j, cols], ALU.subtract).then_inc(parts_ready, 1)
            for c in range(NCH):
                n = 2 * NCH + c
                dve.wait_ge(made, n + 1)
                V.tensor_tensor(v[:, c * TPC:(c + 1) * TPC, :], ps[:, n % 4, :].rearrange("p (t e) -> p t e", t=TPC),
                                bv_b[:].unsqueeze(1).to_broadcast([P, TPC, D]), ALU.add).then_inc(v_ready, 1)


def ssm_stage(nc, ident, xnT_d, A_r, A_i, B_r, B_i, C_r, C_i, skip, s_d):
    LOG = SEQ.bit_length() - 1
    with Stage(nc, "ssm") as st:
        u = st.sb("u", [P, BATCH, SEQ])
        par = st.sb("par", [P, 7])
        Er, Ei, Wr, Wi, decay, tmp, tmp2 = (st.sb(n, [P, SEQ]) for n in ("Er", "Ei", "Wr", "Wi", "decay", "tmp", "tmp2"))
        vr, vi, gr, gi = (st.sb(n, [P, SEQ]) for n in ("vr", "vi", "gr", "gi"))
        y = st.sb("y", [P, 2, SEQ])
        cols = st.sb("cols", [P, 16])
        s = st.sb("s", [P, 2, SEQ // P, D])
        tp = st.ps("tp", [P, 2, SEQ // P, D])
        loaded, consts, step, squared, rooted, y_ready, turned, copied = (
            st.sem(n) for n in ("loaded", "consts", "step", "squared", "rooted", "y_ready", "turned", "copied"))
        stored = [st.sem(f"stored{n}") for n in range(2)]
        block = st.block()

        @block.sync
        def _(sp):
            for n, vec in enumerate((A_r, A_i, B_r, B_i, C_r, C_i, skip)):
                sp.dma_start(par[:, n:n + 1], column(vec)).then_inc(consts, DMA)
            sp.dma_start(u[:], xnT_d.rearrange("d (b t) -> d b t", b=BATCH)).then_inc(loaded, DMA)
            for b in range(BATCH):
                sp.wait_ge(copied, b + 1)
                sp.dma_start(rows(s_d)[:, b * SEQ // P:(b + 1) * SEQ // P, :], s[:, b % 2, :, :]).then_inc(stored[b % 2], DMA)
            for n in range(2):
                sp.wait_ge(stored[n], DMA * BATCH // 2)

        @block.vector
        def _(dve):
            link = Chain(dve, step)
            V = nc.vector
            col = lambda n: cols[:, n:n + 1]
            ar, ai, br, bi, cr, ci, dd = (par[:, n:n + 1] for n in range(7))
            r2, none, inv, c, sn, t, t2, r, wr, wi, nsn, nwi, t3 = (col(n) for n in range(13))
            mul = lambda o, a, b: link(V.tensor_tensor(o, a, b, ALU.mult))
            add = lambda o, a, b: link(V.tensor_tensor(o, a, b, ALU.add))
            sub = lambda o, a, b: link(V.tensor_tensor(o, a, b, ALU.subtract))
            affine = lambda o, a, m, k: link(V.tensor_scalar(o, a, m, k, ALU.mult, ALU.add))

            def to_unit():
                mul(t, c, c)
                mul(t2, sn, sn)
                add(t, t, t2)
                affine(t, t, -0.5, 1.5)
                mul(c, c, t)
                mul(sn, sn, t)

            dve.wait_ge(consts, 7 * DMA)
            mul(t, ar, ar)
            mul(t2, ai, ai)
            add(r2, t, t2)
            link(V.tensor_scalar(none, r2, 1e-34, None, ALU.is_lt))
            V.tensor_scalar(r2, r2, 1e-34, None, ALU.max).then_inc(squared, 1)
            dve.wait_ge(rooted, 1)
            link(V.reciprocal(inv, t3))
            mul(c, ar, inv)
            mul(sn, ai, inv)
            affine(t, none, -1.0, 1.0)
            mul(c, c, t)
            mul(sn, sn, t)
            add(c, c, none)
            to_unit()
            to_unit()
            mul(t, ar, c)
            mul(t2, ai, sn)
            add(r, t, t2)
            mul(t, cr, br)
            mul(t2, ci, bi)
            sub(wr, t, t2)
            mul(t, cr, bi)
            mul(t2, ci, br)
            add(wi, t, t2)
            affine(nwi, wi, -1.0, 0.0)
            link(V.memset(decay[:], 1.0))
            link(V.tensor_scalar(decay[:], decay[:], r, None, ALU.mult))
            link(V.memset(Er[:, 0:1], 1.0))
            link(V.memset(Ei[:, 0:1], 0.0))
            for k in range(LOG):
                n = 1 << k
                affine(nsn, sn, -1.0, 0.0)
                link(V.tensor_scalar(tmp[:, 0:n], Er[:, 0:n], c, None, ALU.mult))
                link(V.tensor_scalar(tmp2[:, 0:n], Ei[:, 0:n], c, None, ALU.mult))
                link(V.scalar_tensor_tensor(out=Er[:, n:2 * n], in0=Ei[:, 0:n], scalar=nsn, in1=tmp[:, 0:n],
                                            op0=ALU.mult, op1=ALU.add))
                link(V.scalar_tensor_tensor(out=Ei[:, n:2 * n], in0=Er[:, 0:n], scalar=sn, in1=tmp2[:, 0:n],
                                            op0=ALU.mult, op1=ALU.add))
                mul(t, c, c)
                mul(t2, sn, sn)
                mul(t3, c, sn)
                sub(c, t, t2)
                affine(sn, t3, 2.0, 0.0)
                to_unit()
            link(V.tensor_scalar(tmp[:], Er[:], wr, None, ALU.mult))
            link(V.scalar_tensor_tensor(out=Wr[:], in0=Ei[:], scalar=nwi, in1=tmp[:], op0=ALU.mult, op1=ALU.add))
            link(V.tensor_scalar(tmp[:], Ei[:], wr, None, ALU.mult))
            link(V.scalar_tensor_tensor(out=Wi[:], in0=Er[:], scalar=wi, in1=tmp[:], op0=ALU.mult, op1=ALU.add))
            dve.wait_ge(loaded, DMA)
            for b in range(BATCH):
                link(V.tensor_tensor(vr[:], Er[:], u[:, b, :], ALU.mult))
                link(V.tensor_tensor(vi[:], Ei[:], u[:, b, :], ALU.mult))
                link(V.tensor_tensor_scan(gr[:], decay[:], vr[:], 0.0, ALU.mult, ALU.add))
                link(V.tensor_tensor_scan(gi[:], decay[:], vi[:], 0.0, ALU.mult, ALU.add))
                link(V.tensor_tensor(gr[:], gr[:], Wr[:], ALU.mult))
                link(V.tensor_tensor(gi[:], gi[:], Wi[:], ALU.mult))
                link(V.tensor_tensor(gr[:], gr[:], gi[:], ALU.add))
                if b >= 2:
                    dve.wait_ge(turned, b - 1)
                V.scalar_tensor_tensor(out=y[:, b % 2, :], in0=u[:, b, :], scalar=dd, in1=gr[:], op0=ALU.mult,
                                       op1=ALU.add).then_inc(y_ready, 1)

        @block.scalar
        def _(act):
            act.wait_ge(squared, 1)
            nc.scalar.activation(cols[:, 12:13], cols[:, 0:1], ACT.Sqrt).then_inc(rooted, 1)
            for b in range(BATCH):
                act.wait_ge(turned, b + 1)
                if b >= 2:
                    act.wait_ge(stored[b % 2], DMA)
                nc.scalar.activation(s[:, b % 2, :, :], tp[:, b % 2, :, :], ACT.Copy).then_inc(copied, 1)

        @block.tensor
        def _(pe):
            for b in range(BATCH):
                pe.wait_ge(y_ready, b + 1)
                if b >= 2:
                    pe.wait_ge(copied, b - 1)
                for t in range(SEQ // P):
                    last = nc.tensor.transpose(tp[:, b % 2, t, :], y[:, b % 2, t * P:(t + 1) * P], ident[:])
                last.then_inc(turned, 1)


def linear_attention_stage(nc, ident, xnT_d, Wq, bq, Wk, bk, Wv, bv, Wg, bg, Wo, bo, s_d):
    DH = 256
    HALF = DH // P
    NCHUNK = SEQ // P
    PIECES = 10
    with Stage(nc, "linattn") as st:
        xc = st.sb("xc", [P, BATCH, P])
        wq, wk, wg, wo = st.sb("wq", [P, DH]), st.sb("wk", [P, DH]), st.sb("wg", [P, DH]), st.sb("wo", [P, HALF, D])
        wkv = st.sb("wkv", [P, 2 * DH])
        b_col = st.sb("b_col", [P, 2, HALF])
        bkv, bgr, bor = st.sb("bkv", [1, 2 * DH]), st.sb("bgr", [1, DH]), st.sb("bor", [1, D])
        ones = st.sb("ones", [1, P])
        mask = st.sb("mask", [P, BATCH, P])
        qkT = st.sb("qkT", [P, 2, HALF, BATCH * P])
        kv = st.sb("kv", [P, BATCH, 2 * DH])
        gate = st.sb("gate", [P, BATCH, DH])
        sc, prob, probT = (st.sb(n, [P, BATCH, P]) for n in ("sc", "prob", "probT"))
        nmax, total = st.sb("nmax", [P, BATCH]), st.sb("total", [P, BATCH])
        state = st.sb("state", [P, BATCH, HALF, DH])
        mixed = st.sb("mixed", [P, BATCH, DH])
        mixedT = st.sb("mixedT", [P, HALF, BATCH * P])
        y = st.sb("y", [P, BATCH, D])
        piece = st.ps("piece", [P, 2, CH])
        pscore = st.ps("pscore", [P, BATCH, P])
        pturn = st.ps("pturn", [P, BATCH, P])
        pout = st.ps("pout", [P, BATCH, DH])
        pmix = st.ps("pmix", [P, HALF, BATCH * P])
        names = ("consts", "made", "x_loaded", "projected", "pieced", "scored", "shifted", "exped", "step", "p_ready", "p_turned",
                 "p_copied", "crossed", "gated", "summed", "added", "m_turned", "m_copied", "out_ready", "out_copied", "stored")
        (consts, made, x_loaded, projected, pieced, scored, shifted, exped, step, p_ready, p_turned, p_copied, crossed, gated, summed,
         added, m_turned, m_copied, out_ready, out_copied, stored) = (st.sem(n) for n in names)
        sig_done = st.sem("sig_done")
        block = st.block()
        NCONST = 14

        @block.sync
        def _(sp):
            for dst, src in ((wq[:], Wq), (wkv[:, 0:DH], Wk), (wkv[:, DH:2 * DH], Wv), (wg[:], Wg), (wk[:], Wk),
                             (wo[:], Wo.rearrange("(h p) d -> p h d", p=P)),
                             *((b_col[:, j, h:h + 1], column(v[h * P:(h + 1) * P])) for j, v in enumerate((bq, bk)) for h in range(HALF)),
                             (bkv[:, 0:DH], bk.rearrange("(a n) -> a n", a=1)), (bkv[:, DH:2 * DH], bv.rearrange("(a n) -> a n", a=1)),
                             (bgr[:], bg.rearrange("(a n) -> a n", a=1)), (bor[:], bo.rearrange("(a n) -> a n", a=1))):
                sp.dma_start(dst, src).then_inc(consts, DMA)

            def load(n):
                sp.dma_start(xc[:], xnT_d.rearrange("d (b t) -> d b t", b=BATCH)[:, :, bass.ds(n * P, P)]).then_inc(x_loaded, DMA)

            def store(n):
                sp.wait_ge(out_copied, n + 1)
                sp.dma_start(s_d.rearrange("(b t) d -> t b d", b=BATCH)[bass.ds(n * P, P), :, :], y[:]).then_inc(stored, DMA)

            load(0)
            with sp.Fori(0, NCHUNK - 1) as n:
                sp.wait_ge(projected, PIECES * n + PIECES)
                load(n + 1)
                store(n)
            store(NCHUNK - 1)
            sp.wait_ge(stored, DMA * NCHUNK)

        @block.gpsimd
        def _(pool):
            nc.gpsimd.memset(ones[:], 1.0).then_inc(made, 1)
            nc.gpsimd.memset(state[:], 0.0).then_inc(made, 1)
            nc.gpsimd.memset(mask[:], 0.0).then_inc(made, 1)
            pool.wait_ge(made, 3)
            nc.gpsimd.affine_select(out=mask[:], in_=mask[:], compare_op=ALU.is_ge, fill=-1e30, base=0,
                                    pattern=[[0, BATCH], [-1, P]], channel_multiplier=1).then_inc(made, 1)

        @block.tensor
        def _(pe):
            mm = nc.tensor.matmul
            pe.wait_ge(consts, NCONST * DMA)
            pe.wait_ge(made, 4)
            with pe.Fori(0, NCHUNK) as n:
                pe.wait_ge(x_loaded, DMA * n + DMA)
                xall = xc[:].rearrange("d b t -> d (b t)")
                for p in range(PIECES):
                    if p >= 2:
                        pe.wait_ge(pieced, PIECES * n + p - 1)
                    elif p == 0:
                        pe.wait_ge(added, BATCH * n)
                        pe.wait_ge(pieced, PIECES * n)
                    bank = piece[:, p % 2, :]
                    if p < 4:
                        w = (wq, wk)[p // 2]
                        last = mm(bank, w[:, p % 2 * P:(p % 2 + 1) * P], xall, start=True, stop=True)
                    elif p < 8:
                        mm(bank, xc[:, p - 4, :], wkv[:], start=True, stop=False)
                        last = mm(bank, ones[:], bkv[:], start=False, stop=True)
                    else:
                        for j in range(2):
                            part = bank[:, j * DH:(j + 1) * DH]
                            mm(part, xc[:, 2 * (p - 8) + j, :], wg[:], start=True, stop=False)
                            last = mm(part, ones[:], bgr[:], start=False, stop=True)
                    last.then_inc(projected, 1)
                for b in range(BATCH):
                    own = slice(b * P, (b + 1) * P)
                    for h in range(HALF):
                        last = mm(pscore[:, b, :], qkT[:, 0, h, own], qkT[:, 1, h, own], start=(h == 0), stop=(h == HALF - 1))
                last.then_inc(scored, 1)
                pe.wait_ge(p_ready, n + 1)
                pe.wait_ge(out_copied, n)
                for b in range(BATCH):
                    last = nc.tensor.transpose(pturn[:, b, :], prob[:, b, :], ident[:])
                last.then_inc(p_turned, 1)
                pe.wait_ge(p_copied, n + 1)
                pe.wait_ge(added, BATCH * n)
                for b in range(BATCH):
                    own = slice(b * P, (b + 1) * P)
                    mm(pout[:, b, :], probT[:, b, :], kv[:, b, DH:2 * DH], start=True, stop=False)
                    for h in range(HALF):
                        last = mm(pout[:, b, :], qkT[:, 0, h, own], state[:, b, h, :], start=False, stop=(h == HALF - 1))
                last.then_inc(crossed, 1)
                for b in range(BATCH):
                    if b >= 2:
                        pe.wait_ge(added, BATCH * n + b - 1)
                    else:
                        pe.wait_ge(pieced, PIECES * n + PIECES)
                    for h in range(HALF):
                        last = mm(piece[:, b % 2, h * DH:(h + 1) * DH], kv[:, b, h * P:(h + 1) * P], kv[:, b, DH:2 * DH],
                                  start=True, stop=True)
                    last.then_inc(summed, 1)
                pe.wait_ge(gated, n + 1)
                for h in range(HALF):
                    for b in range(BATCH):
                        last = nc.tensor.transpose(pmix[:, h, b * P:(b + 1) * P], mixed[:, b, h * P:(h + 1) * P], ident[:])
                last.then_inc(m_turned, 1)
                pe.wait_ge(m_copied, n + 1)
                for b in range(BATCH):
                    for h in range(HALF):
                        mm(pturn[:, b, :], mixedT[:, h, b * P:(b + 1) * P], wo[:, h, :], start=(h == 0), stop=False)
                    last = mm(pturn[:, b, :], ones[:], bor[:], start=False, stop=True)
                last.then_inc(out_ready, 1)

        @block.scalar
        def _(act):
            act.wait_ge(consts, NCONST * DMA)
            with act.Fori(0, NCHUNK) as n:
                for p in range(4):
                    act.wait_ge(projected, PIECES * n + p + 1)
                    if p == 0:
                        act.wait_ge(crossed, n)
                    nc.scalar.activation(qkT[:, p // 2, p % 2, :], piece[:, p % 2, :], ACT.Identity,
                                         bias=b_col[:, p // 2, p % 2:p % 2 + 1]).then_inc(pieced, 1)
                for p in range(8, PIECES):
                    act.wait_ge(projected, PIECES * n + p + 1)
                    act.wait_ge(pieced, PIECES * n + p)
                    if p == 8:
                        act.wait_ge(gated, n)
                    nc.scalar.activation(gate[:, 2 * (p - 8):2 * (p - 8) + 2, :], piece[:, p % 2, :].rearrange("t (b e) -> t b e", b=2),
                                         ACT.Sigmoid).then_inc(pieced, 1)
                act.wait_ge(shifted, n + 1)
                nc.scalar.activation(prob[:], sc[:], ACT.Exp).then_inc(exped, 1)
                act.wait_ge(m_turned, n + 1)
                nc.scalar.activation(mixedT[:], pmix[:], ACT.Copy).then_inc(m_copied, 1)
                act.wait_ge(out_ready, n + 1)
                act.wait_ge(stored, DMA * n)
                nc.scalar.activation(y[:], pturn[:], ACT.Copy).then_inc(out_copied, 1)

        @block.vector
        def _(dve):
            V = nc.vector
            wide = [P, BATCH, P]
            dve.wait_ge(made, 4)
            with dve.Fori(0, NCHUNK) as n:
                link = Chain(dve, step)
                STEPS = 4
                for b in range(BATCH):
                    dve.wait_ge(projected, PIECES * n + 4 + b + 1)
                    dve.wait_ge(pieced, PIECES * n + 4 + b)
                    if b == 0:
                        dve.wait_ge(summed, BATCH * n)
                    V.tensor_copy(kv[:, b, :], piece[:, b % 2, :]).then_inc(pieced, 1)
                dve.wait_ge(scored, n + 1)
                link(V.scalar_tensor_tensor(out=sc[:], in0=pscore[:], scalar=DH ** -0.5, in1=mask[:], op0=ALU.mult, op1=ALU.add),
                     STEPS * n)
                link(V.tensor_reduce(nmax[:], sc[:], AX.X, ALU.max, negate=True), STEPS * n)
                V.tensor_tensor(sc[:], sc[:], over(nmax[:].unsqueeze(2), wide), ALU.add).then_inc(shifted, 1)
                dve.wait_ge(exped, n + 1)
                link(V.reduce_sum(total[:], prob[:], AX.X), STEPS * n)
                link(V.reciprocal(total[:], total[:]), STEPS * n)
                V.tensor_tensor(prob[:], prob[:], over(total[:].unsqueeze(2), wide), ALU.mult).then_inc(p_ready, 1)
                dve.wait_ge(p_turned, n + 1)
                V.tensor_copy(probT[:], pturn[:]).then_inc(p_copied, 1)
                dve.wait_ge(crossed, n + 1)
                dve.wait_ge(pieced, PIECES * n + PIECES)
                V.tensor_tensor(mixed[:], pout[:], gate[:], ALU.mult).then_inc(gated, 1)
                for b in range(BATCH):
                    dve.wait_ge(summed, BATCH * n + b + 1)
                    V.tensor_tensor(state[:, b, :, :], piece[:, b % 2, :].rearrange("p (h e) -> p h e", h=HALF), state[:, b, :, :],
                                    ALU.add).then_inc(added, 1)


def shared_ffn_stage(nc, ident, xnT_d, sw1, sb1, sw2, sb2, sw3, sb3, ln_g, ln_b, f_d):
    H = 64
    wide = [P, TPC, H]
    with Stage(nc, "shared") as st:
        xc = st.sb("xc", [P, 2, CH])
        raw12, raw3 = st.sb("raw12", [P, D]), st.sb("raw3", [P, H])
        w12, w3 = st.sb("w12", [P, 2 * H]), st.sb("w3", [H + 1, D])
        b12, ones = st.sb("b12", [1, 2 * H]), st.sb("ones", [1, P])
        gamma, beta = st.sb("gamma", [P, H]), st.sb("beta", [P, H])
        a, z, sq = (st.sb(n, wide) for n in ("a", "z", "sq"))
        total, var, std = (st.sb(n, [P, TPC]) for n in ("total", "var", "std"))
        zT = st.sb("zT", [H + 1, CH])
        y = st.sb("y", [P, 2, TPC, D])
        wt = st.ps("wt", [P, 2, P])
        hid = st.ps("hid", [P, 2, TPC, 2 * H])
        zt = st.ps("zt", [P, CH])
        out = st.ps("out", [P, 2, TPC, D])
        names = ("consts", "made", "w_turned", "w_copied", "projected", "silu_done", "step", "var_ready", "std_ready", "z_ready",
                 "z_turned", "z_copied", "out_ready", "out_copied")
        (consts, made, w_turned, w_copied, projected, silu_done, step, var_ready, std_ready, z_ready, z_turned, z_copied, out_ready,
         out_copied) = (st.sem(n) for n in names)
        x_loaded, stored = ([st.sem(f"{n}{s}") for s in range(2)] for n in ("x_loaded", "stored"))
        block = st.block()
        NCONST = 8

        def iterations(eng, body):
            body(0, 0, True)
            body(1, 1, True)
            with eng.Fori(1, NCH // 2) as j:
                body(2 * j, 0, False)
                body(2 * j + 1, 1, False)

        @block.sync
        def _(sp):
            sp.wait_ge(made, 2)
            for dst, src in ((raw12[0:H, :], sw1), (raw12[H:2 * H, :], sw2), (raw3[:], sw3), (w3[H:H + 1, :], sb3.rearrange("(a n) -> a n", a=1)),
                             (b12[:, 0:H], sb1.rearrange("(a n) -> a n", a=1)), (b12[:, H:2 * H], sb2.rearrange("(a n) -> a n", a=1)),
                             (gamma[:], broadcast_rows(ln_g)), (beta[:], broadcast_rows(ln_b))):
                sp.dma_start(dst, src).then_inc(consts, DMA)

            def body(i, slot, first):
                if not first:
                    sp.wait_ge(projected, i - 1)
                sp.dma_start(xc[:, slot, :], xnT_d[:, bass.ds(i * CH, CH)]).then_inc(x_loaded[slot], DMA)
            iterations(sp, body)
            for s in range(2):
                sp.wait_ge(stored[s], DMA * NCH // 2)

        @block.gpsimd
        def _(pool):
            nc.gpsimd.memset(ones[:], 1.0).then_inc(made, 1)
            nc.gpsimd.memset(zT[H:H + 1, :], 1.0).then_inc(made, 1)

            def body(i, slot, first):
                pool.wait_ge(out_copied, i + 1)
                pool.dma_start(rows(f_d)[:, bass.ds(i * TPC, TPC), :], y[:, slot, :, :]).then_inc(stored[slot], DMA)
            iterations(pool, body)

        @block.tensor
        def _(pe):
            mm = nc.tensor.matmul
            pe.wait_ge(consts, NCONST * DMA)
            nc.tensor.transpose(wt[:, 0, :], raw12[:], ident[:]).then_inc(w_turned, 1)
            nc.tensor.transpose(wt[0:H, 1, :], raw3[:], ident[:]).then_inc(w_turned, 1)
            pe.wait_ge(w_copied, 2)

            def up(i, slot, first):
                pe.wait_ge(x_loaded[slot], DMA * ((i - slot) // 2 + 1))
                if not first:
                    pe.wait_ge(z_ready, i - 1)
                for t in range(TPC):
                    mm(hid[:, slot, t, :], xc[:, slot, t * P:(t + 1) * P], w12[:], start=True, stop=False)
                    last = mm(hid[:, slot, t, :], ones[:], b12[:], start=False, stop=True)
                last.then_inc(projected, 1)

            def body(i, slot, first):
                up(i, slot, first)
                pe.wait_ge(z_ready, i + 1)
                nc.tensor.transpose(zt[:, 0:P], z[:, 0:2, :].rearrange("p t h -> p (t h)"), ident[:])
                for t in range(1, TPC):
                    last = nc.tensor.transpose(zt[0:H, t * P:(t + 1) * P], z[:, t, :], ident[:])
                last.then_inc(z_turned, 1)
                pe.wait_ge(z_copied, i + 1)
                if not first:
                    pe.wait_ge(out_copied, i - 1)
                for t in range(TPC):
                    last = mm(out[:, slot, t, :], zT[:, t * P:(t + 1) * P], w3[:], start=True, stop=True)
                last.then_inc(out_ready, 1)
            iterations(pe, body)

        @block.scalar
        def _(act):
            act.wait_ge(w_turned, 2)
            nc.scalar.activation(w12[:], wt[:, 0, :], ACT.Copy).then_inc(w_copied, 1)
            nc.scalar.activation(w3[0:H, :], wt[0:H, 1, :], ACT.Copy).then_inc(w_copied, 1)

            def body(i, slot, first):
                act.wait_ge(projected, i + 1)
                if not (first and slot == 0):
                    act.wait_ge(z_ready, i)
                nc.scalar.activation(a[:], hid[:, slot, :, 0:H], ACT.Silu).then_inc(silu_done, 1)
                act.wait_ge(var_ready, i + 1)
                nc.scalar.activation(std[:], var[:], ACT.Sqrt).then_inc(std_ready, 1)
                act.wait_ge(z_turned, i + 1)
                nc.scalar.activation(zT[0:H, :], zt[0:H, :], ACT.Copy).then_inc(z_copied, 1)
                act.wait_ge(out_ready, i + 1)
                if not first:
                    act.wait_ge(stored[slot], DMA * ((i - slot) // 2))
                nc.scalar.activation(y[:, slot, :, :], out[:, slot, :, :], ACT.Copy).then_inc(out_copied, 1)
            iterations(act, body)

        @block.vector
        def _(dve):
            V = nc.vector
            dve.wait_ge(consts, NCONST * DMA)

            def body(i, slot, first):
                STEPS = 9
                link = Chain(dve, step)
                run = lambda ins: link(ins, STEPS * i)
                dve.wait_ge(silu_done, i + 1)
                if not (first and slot == 0):
                    dve.wait_ge(z_turned, i)
                run(V.tensor_tensor(z[:], hid[:, slot, :, H:2 * H], a[:], ALU.mult))
                run(V.reduce_sum(total[:], z[:], AX.X))
                run(V.tensor_scalar(total[:], total[:], -1.0 / H, None, ALU.mult))
                run(V.tensor_tensor(z[:], z[:], over(total[:].unsqueeze(2), wide), ALU.add))
                run(V.tensor_tensor(sq[:], z[:], z[:], ALU.mult))
                run(V.reduce_sum(var[:], sq[:], AX.X))
                V.tensor_scalar(var[:], var[:], 1.0 / H, 1e-5, ALU.mult, ALU.add).then_inc(var_ready, 1)
                dve.wait_ge(std_ready, i + 1)
                run(V.reciprocal(total[:], std[:]))
                run(V.tensor_tensor(z[:], z[:], over(total[:].unsqueeze(2), wide), ALU.mult))
                run(V.tensor_tensor(z[:], z[:], gamma[:].unsqueeze(1).to_broadcast(wide), ALU.mult))
                V.tensor_tensor(z[:], z[:], beta[:].unsqueeze(1).to_broadcast(wide), ALU.add).then_inc(z_ready, 1)
            iterations(dve, body)


def routed_ffn_stage(nc, ident, xn_d, f_d, index_b, index_t, sg_w, sg_b, eg_w, eg_b, exp_bias, ew1, eb1, ew2, eb2, ew3, eb3,
                     ln_g, ln_b):
    M = index_b.shape[0] // P
    E, H = 8, 64
    F = E * H
    FT = F // P
    with Stage(nc, "routed") as st:
        ib, it = st.sb("ib", [P, M], I32), st.sb("it", [P, M], I32)
        fb, ft, neg = (st.sb(n, [P, M]) for n in ("fb", "ft", "neg"))
        row = st.sb("row", [P, M], I32)
        x, old, new = (st.sb(n, [P, M, D]) for n in ("x", "old", "new"))
        xT = st.sb("xT", [P, M, P])
        raw = st.sb("raw", [P, 3, FT, P])
        w = st.sb("w", [P, 2, F])
        w3 = st.sb("w3", [P, FT, D])
        gr, gw, gbias = st.sb("gr", [E + 1, D]), st.sb("gw", [P, E + 1]), st.sb("gbias", [1, E + 1])
        xbias = st.sb("xbias", [P, E])
        b12, b3, ones = st.sb("b12", [1, 2, F]), st.sb("b3", [E, D]), st.sb("ones", [1, P])
        before = st.sb("before", [P, E, E])
        gamma, beta = st.sb("gamma", [P, H]), st.sb("beta", [P, H])
        sc = st.sb("sc", [P, M, E + 1])
        pick, hot, tmp = (st.sb(n, [P, M, E]) for n in ("pick", "hot", "tmp"))
        pair, pair2 = st.sb("pair", [P, M, E, E]), st.sb("pair2", [P, M, E, E])
        two = st.sb("two", [P, M, 2])
        red = st.sb("red", [P, M])
        a, z, sq = (st.sb(n, [P, M, E, H]) for n in ("a", "z", "sq"))
        total, var, std = (st.sb(n, [P, M, E]) for n in ("total", "var", "std"))
        zT, hotT = st.sb("zT", [P, M, FT, P]), st.sb("hotT", [E, M, P])
        turn = st.ps("turn", [P, 2, CH])
        score = st.ps("score", [P, M, E + 1])
        hid = st.ps("hid", [P, M, 2, F])
        out = st.ps("out", [P, M, D])
        names = ("consts", "made", "idx_loaded", "row_ready", "gathered", "turned", "copied", "scored", "sig_done", "step", "two_ready",
                 "two_done", "projected", "silu_done", "var_ready", "std_ready", "z_ready", "out_ready", "old_loaded", "new_ready", "stored")
        (consts, made, idx_loaded, row_ready, gathered, turned, copied, scored, sig_done, step, two_ready, two_done, projected,
         silu_done, var_ready, std_ready, z_ready, out_ready, old_loaded, new_ready, stored) = (st.sem(n) for n in names)
        block = st.block()
        NCONST = 13
        WTURNS = 3 + 1
        one = lambda v: v.rearrange("(a n) -> a n", a=1)

        @block.sync
        def _(sp):
            for m in range(M):
                for dst, src in ((ib, index_b), (it, index_t)):
                    sp.dma_start(dst[:, m:m + 1], column(src[m * P:(m + 1) * P])).then_inc(idx_loaded, DMA)
            for dst, src in ((raw[:, 0, :, :], ew1.rearrange("(k e) h d -> (e h) k d", e=2)),
                             (raw[:, 1, :, :], ew2.rearrange("(k e) h d -> (e h) k d", e=2)),
                             (raw[:, 2, :, :].rearrange("d k (e h) -> d (k e) h", e=2), ew3.rearrange("e d h -> d e h")),
                             (gr[0:E, :], eg_w), (gr[E:E + 1, :], sg_w), (gbias[:, 0:E], one(eg_b)), (gbias[:, E:E + 1], one(sg_b)),
                             (xbias[:], broadcast_rows(exp_bias)), (b12[:, 0, :], one(eb1.rearrange("e h -> (e h)"))),
                             (b12[:, 1, :], one(eb2.rearrange("e h -> (e h)"))), (b3[:], eb3),
                             (gamma[:], broadcast_rows(ln_g)), (beta[:], broadcast_rows(ln_b))):
                sp.dma_start(dst, src).then_inc(consts, DMA)

        @block.gpsimd
        def _(pool):
            nc.gpsimd.memset(ones[:], 1.0).then_inc(made, 1)
            nc.gpsimd.memset(before[:], 1.0).then_inc(made, 1)
            pool.wait_ge(made, 2)
            nc.gpsimd.affine_select(out=before[:], in_=before[:], compare_op=ALU.is_ge, fill=0.0, base=-1,
                                    pattern=[[1, E], [-1, E]], channel_multiplier=0).then_inc(made, 1)
            pool.wait_ge(row_ready, 1)
            at = lambda m: bass.IndirectOffsetOnAxis(ap=row[:, m:m + 1].bitcast(U32), axis=0)
            for m in range(M):
                pool.indirect_dma_start(out=x[:, m, :], out_offset=None, in_=xn_d[:, :], in_offset=at(m)).then_inc(gathered, DMA)
                pool.indirect_dma_start(out=old[:, m, :], out_offset=None, in_=f_d[:, :], in_offset=at(m)).then_inc(old_loaded, DMA)
            pool.wait_ge(new_ready, 1)
            for m in range(M):
                pool.indirect_dma_start(out=f_d[:, :], out_offset=at(m), in_=new[:, m, :], in_offset=None).then_inc(stored, DMA)
            pool.wait_ge(stored, DMA * M)

        @block.tensor
        def _(pe):
            mm = nc.tensor.matmul
            T = nc.tensor.transpose
            pe.wait_ge(consts, NCONST * DMA)
            for j in range(3):
                if j == 2:
                    pe.wait_ge(copied, 1)
                for k in range(FT):
                    last = T(turn[:, j % 2, k * P:(k + 1) * P], raw[:, j, k, :], ident[:])
                last.then_inc(turned, 1)
            pe.wait_ge(copied, 2)
            T(turn[:, 1, 0:E + 1], gr[:], ident[0:E + 1, 0:E + 1]).then_inc(turned, 1)
            pe.wait_ge(gathered, DMA * M)
            pe.wait_ge(copied, 3)
            for m in range(M):
                last = T(turn[:, 0, m * P:(m + 1) * P], x[:, m, :], ident[:])
            last.then_inc(turned, 1)
            pe.wait_ge(copied, 5)
            pe.wait_ge(made, 3)
            for m in range(M):
                mm(score[:, m, :], xT[:, m, :], gw[:], start=True, stop=False)
                last = mm(score[:, m, :], ones[:], gbias[:], start=False, stop=True)
            last.then_inc(scored, 1)
            for m in range(M):
                for j in range(2):
                    mm(hid[:, m, j, :], xT[:, m, :], w[:, j, :], start=True, stop=False)
                    last = mm(hid[:, m, j, :], ones[:], b12[:, j, :], start=False, stop=True)
            last.then_inc(projected, 1)
            pe.wait_ge(z_ready, 1)
            for m in range(M):
                for k in range(FT):
                    last = T(turn[:, m, k * P:(k + 1) * P], z[:, m, :, :].rearrange("p e h -> p (e h)")[:, k * P:(k + 1) * P], ident[:])
            last.then_inc(turned, 1)
            pe.wait_ge(copied, 6)
            for m in range(M):
                last = T(turn[0:E, 0, m * P:(m + 1) * P], hot[:, m, :], ident[:])
            last.then_inc(turned, 1)
            pe.wait_ge(copied, 7)
            for m in range(M):
                for k in range(FT):
                    mm(out[:, m, :], zT[:, m, k, :], w3[:, k, :], start=(k == 0), stop=False)
                last = mm(out[:, m, :], hotT[:, m, :], b3[:], start=False, stop=True)
            last.then_inc(out_ready, 1)

        @block.scalar
        def _(act):
            copy = lambda o, i: nc.scalar.activation(o, i, ACT.Copy).then_inc(copied, 1)
            for n, (dst, src) in enumerate(((w[:, 0, :], turn[:, 0, :]), (w[:, 1, :], turn[:, 1, :]),
                                            (w3[:].rearrange("p k d -> p (k d)"), turn[:, 0, :]), (gw[:], turn[:, 1, 0:E + 1]),
                                            (xT[:].rearrange("p m t -> p (m t)"), turn[:, 0, 0:M * P]))):
                act.wait_ge(turned, n + 1)
                copy(dst, src)
            act.wait_ge(scored, 1)
            nc.scalar.activation(sc[:], score[:], ACT.Sigmoid).then_inc(sig_done, 1)
            act.wait_ge(projected, 1)
            nc.scalar.activation(a[:].rearrange("p m e h -> p m (e h)"), hid[:, :, 0, :], ACT.Silu).then_inc(silu_done, 1)
            act.wait_ge(two_ready, 1)
            nc.scalar.activation(two[:], two[:], ACT.Exp).then_inc(two_done, 1)
            act.wait_ge(var_ready, 1)
            nc.scalar.activation(std[:], var[:], ACT.Sqrt).then_inc(std_ready, 1)
            act.wait_ge(turned, 6)
            copy(zT[:].rearrange("p m k t -> p m (k t)"), turn[:])
            act.wait_ge(turned, 7)
            copy(hotT[:].rearrange("e m t -> e (m t)"), turn[0:E, 0, 0:M * P])

        @block.vector
        def _(dve):
            V = nc.vector
            link = Chain(dve, step)
            TT = lambda o, p, q, op: link(V.tensor_tensor(o, p, q, op))
            dve.wait_ge(idx_loaded, 2 * M * DMA)
            for f, i, size in ((fb, ib, BATCH), (ft, it, SEQ)):
                link(V.tensor_copy(f[:], i[:]))
                link(V.tensor_scalar(neg[:], f[:], 0.0, float(size), ALU.is_lt, ALU.mult))
                TT(f[:], f[:], neg[:], ALU.add)
            link(V.scalar_tensor_tensor(out=fb[:], in0=fb[:], scalar=float(SEQ), in1=ft[:], op0=ALU.mult, op1=ALU.add))
            V.tensor_copy(row[:], fb[:]).then_inc(row_ready, 1)
            dve.wait_ge(consts, NCONST * DMA)
            dve.wait_ge(made, 3)
            dve.wait_ge(sig_done, 1)
            s8 = sc[:, :, 0:E]
            TT(pick[:], s8, xbias[:].unsqueeze(1).to_broadcast([P, M, E]), ALU.add)
            four = [P, M, E, E]
            vi, vj = over(pick[:].unsqueeze(3), four), pick[:].unsqueeze(2).to_broadcast(four)
            flat = lambda t: t[:].rearrange("p m i j -> p m (i j)")
            TT(pair[:], vj, vi, ALU.is_gt)
            TT(pair2[:], vj, vi, ALU.is_equal)
            TT(flat(pair2), flat(pair2), before[:].rearrange("p i j -> p (i j)").unsqueeze(1).to_broadcast([P, M, E * E]), ALU.mult)
            TT(flat(pair), flat(pair), flat(pair2), ALU.add)
            link(V.reduce_sum(hot[:], pair[:], AX.X))
            link(V.tensor_scalar(hot[:], hot[:], 0.5, None, ALU.is_lt))
            TT(tmp[:], s8, hot[:], ALU.mult)
            link(V.reduce_sum(red[:], tmp[:], AX.X))
            link(V.tensor_copy(two[:, :, 0], sc[:, :, E]))
            link(V.tensor_copy(two[:, :, 1], red[:]))
            link(V.reduce_max(red[:], two[:], AX.X))
            V.tensor_tensor(two[:], two[:], over(red[:].unsqueeze(2), [P, M, 2]), ALU.subtract).then_inc(two_ready, 1)
            dve.wait_ge(two_done, 1)
            link(V.reduce_sum(red[:], two[:], AX.X))
            link(V.reciprocal(red[:], red[:]))
            TT(two[:], two[:], over(red[:].unsqueeze(2), [P, M, 2]), ALU.mult)
            dve.wait_ge(silu_done, 1)
            wide, me = [P, M * E, H], lambda t: t[:].rearrange("p m e h -> p (m e) h")
            st8 = lambda t: over(t[:].rearrange("p m e -> p (m e)").unsqueeze(2), wide)
            TT(z[:].rearrange("p m e h -> p m (e h)"), hid[:, :, 1, :], a[:].rearrange("p m e h -> p m (e h)"), ALU.mult)
            link(V.reduce_sum(total[:], z[:], AX.X))
            link(V.tensor_scalar(total[:], total[:], -1.0 / H, None, ALU.mult))
            TT(me(z), me(z), st8(total), ALU.add)
            TT(sq[:], z[:], z[:], ALU.mult)
            link(V.reduce_sum(var[:], sq[:], AX.X))
            V.tensor_scalar(var[:], var[:], 1.0 / H, 1e-5, ALU.mult, ALU.add).then_inc(var_ready, 1)
            dve.wait_ge(std_ready, 1)
            link(V.reciprocal(total[:], std[:]))
            TT(me(z), me(z), st8(total), ALU.mult)
            TT(me(z), me(z), gamma[:].unsqueeze(1).to_broadcast(wide), ALU.mult)
            TT(me(z), me(z), beta[:].unsqueeze(1).to_broadcast(wide), ALU.add)
            V.tensor_tensor(me(z), me(z), st8(hot), ALU.mult).then_inc(z_ready, 1)
            dve.wait_ge(out_ready, 1)
            dve.wait_ge(old_loaded, DMA * M)
            rowwise = [P, M, D]
            TT(old[:], old[:], over(two[:, :, 0:1], rowwise), ALU.mult)
            TT(new[:], out[:], over(two[:, :, 1:2], rowwise), ALU.mult)
            V.tensor_tensor(new[:], new[:], old[:], ALU.add).then_inc(new_ready, 1)


def recurrent_block_kernel(nc, a, out):
    def scratch(name, shape, dt=F32):
        return nc.dram_tensor(name, shape, dt).ap()

    def inputs(prefix, names):
        return [a[prefix + n] for n in names.split()]

    x = [a["L0_attn_x"].rearrange("b t d -> (b t) d")] + [scratch(f"x{n}", [TOK, D]) for n in (1, 2, 3)]
    xn, xnT = scratch("xn", [TOK, D]), scratch("xnT", [D, TOK])
    s, fT, f = scratch("s", [TOK, D]), scratch("fT", [D, TOK]), scratch("f", [TOK, D])
    c, cT = scratch("c", [32, TOK]), scratch("cT", [96, TOK], BF16)
    BLOCKS = 2 * TOK // P + 8
    sorted_x, sorted_y = scratch("sorted_x", [BLOCKS * P, D]), scratch("sorted_y", [BLOCKS * P, D])
    picks, owner = (scratch("pick_place", [P, 2, NT], I32), scratch("pick_weight", [P, 2, NT])), scratch("owner", [1, BLOCKS], I32)
    with ExitStack() as ctx:
        ident = ctx.enter_context(nc.sbuf_tensor("identity", [P, P], F32))
        make_identity(nc, ident)

        def mixture(layer, kind, blocks, names):
            w, bias, *weights = inputs(f"L{layer}_ffn_", names)
            xs, y, own = sorted_x[0:blocks * P, :], sorted_y[0:blocks * P, :], owner[:, 0:blocks]
            dispatch_stage(nc, f"dispatch{layer}", kind, xn, xnT, w, bias, blocks, xs, *picks, own)
            sorted_experts_stage(nc, f"experts{layer}", ident, blocks, xs, own, weights, y)

        layernorm_stage(nc, "norm0", ident, x[0], xn, xnT)

        q0, kh0, kl0 = (scratch(n, [16, P, TOK], F16) for n in ("q0", "kh0", "kl0"))
        v0, o0 = scratch("v0", [8, TOK, P]), scratch("o0", [8, P, TOK])
        project_l0(nc, xnT, *inputs("L0_attn_", "w_q w_k w_v"), q0, kh0, kl0, v0)
        o0h = o0.rearrange("g (h r) t -> h g r t", h=2)
        attention_stage(nc, "attn0", ident, q0, [kh0, kl0], v0, [o0h[0], o0h[1]], scratch("inv0", [2, 8, P]), 8, 2, P, 64, 512, 1.0)
        output_projection(nc, "out0", o0.rearrange("g r t -> (g r) t"), None, None, a["L0_attn_w_proj"], a["L0_attn_b_proj"], xn, s)
        routing_stage(nc, "route0", ident, "grouped", xnT, a["L0_ffn_gate_w"], a["L0_ffn_gate_bias"], c, cT)
        experts_stage(nc, "experts0", ident, "silu", xnT, c, cT, inputs("L0_ffn_", "w_gate w_up w_down sh_gate sh_up sh_down"), fT)
        combine_stage(nc, "mix0", ident, x[0], s, (a["L0_attn_ln_gamma"], a["L0_attn_ln_beta"], 1e-6), fT, True, None, x[1], xn, xnT)

        q1, k1 = scratch("q1", [3, P, TOK], BF16), scratch("k1", [3, P, TOK], BF16)
        v1, o1, sums1 = scratch("v1", [4, TOK, 32]), scratch("o1", [P, TOK]), scratch("sums1", [P, TOK])
        project_l1(nc, xnT, a["L1_attn_W_qkv"], a["L1_attn_b_qkv"], q1, k1, v1)
        narrow_attention_stage(nc, ident, q1, k1, v1, o1, sums1, scratch("max1", [2, 32, P], BF16))
        output_projection(nc, "out1", o1, sums1, D ** -0.5, a["L1_attn_W_out"], a["L1_attn_b_out"], None, s)
        mixture(1, "top2", BLOCKS, "Wg bg W1 b1 W2 b2")
        combine_stage(nc, "mix1", ident, x[1], s, None, sorted_y, False, (a["L1_ffn_gamma"], a["L1_ffn_beta"], 1e-5), x[2], xn, xnT,
                      picks)

        ssm_stage(nc, ident, xnT, *inputs("L2_attn_", "A_real A_imag B_real B_imag C_real C_imag D"), s)
        mixture(2, "capacity", 5 * TOK // 4 // P, "w_router b_router w1 b1 w2 b2")
        combine_stage(nc, "mix2", ident, x[2], s, None, sorted_y, False, None, x[3], xn, xnT, picks)

        linear_attention_stage(nc, ident, xnT, *inputs("L3_attn_", "Wq bq Wk bk Wv bv Wg bg Wo bo"), s)
        shared_ffn_stage(nc, ident, xnT, *inputs("L3_ffn_", "sw1 sb1 sw2 sb2 sw3 sb3 s_ln_g s_ln_b"), f)
        routed_ffn_stage(nc, ident, xn, f, *inputs(
            "L3_ffn_", "index_b index_t sg_w sg_b eg_w eg_b exp_bias ew1 eb1 ew2 eb2 ew3 eb3 sel_ln_g sel_ln_b"))
        combine_stage(nc, "mix3", ident, x[3], s, None, f, False, None, out.rearrange("b t d -> (b t) d"), None, None)


def kernel(**inputs):
    import numpy as _np
    import concourse.bacc as _bacc
    from concourse import mybir as _mybir
    from concourse.bass_utils import run_bass_kernel_spmd as _run

    nc = _bacc.Bacc("TRN2", target_bir_lowering=False, num_devices=1)
    arrays, args = {}, {}
    for name, value in inputs.items():
        value = _np.ascontiguousarray(value)
        arrays[f"in_{name}"] = value
        args[name] = nc.dram_tensor(f"in_{name}", value.shape, _mybir.dt.from_np(value.dtype), kind="ExternalInput").ap()
    out = nc.dram_tensor("out", (BATCH, SEQ, D), F32, kind="ExternalOutput").ap()
    recurrent_block_kernel(nc, args, out)
    return _run(nc, [arrays], core_ids=[0]).results[0]["out"]
```
